# Optimizing a Trainium2 kernel written in Bass

```python
import numpy as np
import jax
import jax.numpy as jnp

def _softmax(x, axis=-1):
    return jax.nn.softmax(x, axis=axis)

def _gelu(x):
    return jax.nn.gelu(x, approximate=True)

def _silu(x):
    return jax.nn.silu(x)

def _sigmoid(x):
    return jax.nn.sigmoid(x)

def _layernorm(x, axis=-1, eps=1e-05):
    m = jnp.mean(x, axis=axis, keepdims=True)
    v = jnp.var(x, axis=axis, keepdims=True)
    return (x - m) / jnp.sqrt(v + eps)

def _scatter_add(tgt, idx, src, axis=0):
    return tgt.at[idx].add(src)

def _segment_sum(src, seg, n):
    return jax.ops.segment_sum(src, seg, n)
kernel_name = 'mk_macaron_d2_jaxref_r8_8a33c1'

def setup_inputs(seed: int=0):
    np.random.seed(seed)
    _w = jnp.asarray

    def _L0_attn_setup():
        import jax, jax.numpy as jnp
        import numpy as np
        D_MODEL = 128
        D_STATE = 16
        D_CONV = 4
        EXPAND = 2
        D_INNER = D_MODEL * EXPAND
        B = 1
        L = 256
        key = jax.random.key(seed)
        ks = jax.random.split(key, 8)
        s = lambda k, shape, scale: jax.random.normal(k, shape, dtype=jnp.float32) * scale
        return {'x': jax.random.normal(ks[0], (B, L, D_MODEL), dtype=jnp.float32), 'in_proj_w': s(ks[1], (D_INNER * 2, D_MODEL), D_MODEL ** (-0.5)), 'conv_w': s(ks[2], (D_INNER, 1, D_CONV), D_CONV ** (-0.5)), 'conv_b': jnp.zeros((D_INNER,), jnp.float32), 'x_proj_w': s(ks[3], (2 * D_STATE + 1, D_INNER), D_INNER ** (-0.5)), 'dt_proj_w': s(ks[4], (D_INNER, 1), 1.0), 'dt_proj_b': jnp.zeros((D_INNER,), jnp.float32), 'A_log': jnp.log(jnp.broadcast_to(jnp.arange(1, D_STATE + 1, dtype=jnp.float32), (D_INNER, D_STATE))), 'D': jnp.ones((D_INNER,), jnp.float32), 'out_proj_w': s(ks[5], (D_MODEL, D_INNER), D_INNER ** (-0.5))}
    _L0_attn_in = _L0_attn_setup()

    def _L0_ffn_setup():
        import jax, jax.numpy as jnp
        import numpy as np
        D_IN, D_HID = (128, 512)

        def _ternary(key, shape):
            return jax.random.randint(key, shape, -1, 2).astype(jnp.float32)

        def _tlin(x, w, s):
            return jnp.einsum('bsi,oi->bso', x, w) * s
        key = jax.random.key(seed)
        ks = jax.random.split(key, 12)
        inv = lambda fan: 1.0 / np.sqrt(fan).astype(np.float32)
        return {'x': jax.random.normal(ks[0], (4, 256, D_IN), dtype=jnp.float32), 'w1_w': _ternary(ks[1], (D_HID, D_IN)), 'w1_s': jax.random.uniform(ks[2], (D_HID,), dtype=jnp.float32) * inv(D_IN), 'w2_w': _ternary(ks[3], (D_HID, D_IN)), 'w2_s': jax.random.uniform(ks[4], (D_HID,), dtype=jnp.float32) * inv(D_IN), 'h1_w': _ternary(ks[5], (D_HID, D_HID)), 'h1_s': jax.random.uniform(ks[6], (D_HID,), dtype=jnp.float32) * inv(D_HID), 'h2_w': _ternary(ks[7], (D_HID, D_HID)), 'h2_s': jax.random.uniform(ks[8], (D_HID,), dtype=jnp.float32) * inv(D_HID), 'w3_w': _ternary(ks[9], (D_IN, D_HID)), 'w3_s': jax.random.uniform(ks[10], (D_IN,), dtype=jnp.float32) * inv(D_HID)}
    _L0_ffn_in = _L0_ffn_setup()

    def _L1_attn_setup():
        import jax, jax.numpy as jnp
        import numpy as np
        import math
        NUM_HEADS = 8
        EMB = 128
        HEAD_DIM = 128
        B, T = (1, 512)

        def sinusoidal_pe(T, d, dtype=jnp.float32):
            pos = jnp.arange(T, dtype=dtype)[:, None]
            inv_freq = jnp.exp(-math.log(10000.0) * jnp.arange(0, d, 2, dtype=dtype) / d)
            ang = pos * inv_freq[None, :]
            pe = jnp.zeros((T, d), dtype=dtype)
            pe = pe.at[:, 0::2].set(jnp.sin(ang))
            pe = pe.at[:, 1::2].set(jnp.cos(ang))
            return pe
        key = jax.random.key(seed)
        ks = jax.random.split(key, 6)
        s = lambda fan_in: 1.0 / math.sqrt(fan_in)
        x = jax.random.normal(ks[0], (B, T, EMB), dtype=jnp.float32)
        Wq = jax.random.normal(ks[1], (EMB, NUM_HEADS * HEAD_DIM), dtype=jnp.float32) * s(EMB)
        bq = jax.random.normal(ks[2], (NUM_HEADS * HEAD_DIM,), dtype=jnp.float32) * s(EMB)
        Wkv = jax.random.normal(ks[3], (EMB, 2 * HEAD_DIM), dtype=jnp.float32) * s(EMB)
        bkv = jax.random.normal(ks[4], (2 * HEAD_DIM,), dtype=jnp.float32) * s(EMB)
        Wo = jax.random.normal(ks[5], (NUM_HEADS * HEAD_DIM, EMB), dtype=jnp.float32) * s(NUM_HEADS * HEAD_DIM)
        return {'x': x, 'Wq': Wq, 'bq': bq, 'Wkv': Wkv, 'bkv': bkv, 'Wo': Wo}
    _L1_attn_in = _L1_attn_setup()

    def _L1_ffn_setup():
        import jax, jax.numpy as jnp
        import numpy as np
        H = 128
        I = 88
        E = 64
        TOP_K = 8
        NG = 8
        TOPK_GROUP = 4
        N_SHARED = 2
        ROUTED_SCALE = 2.5
        S_I = I * N_SHARED

        def _route(x, gate_w, gate_bias):
            T = x.shape[0]
            logits = x @ gate_w.T
            scores = jax.nn.sigmoid(logits)
            scores_for_choice = scores + gate_bias[None, :]
            grp = scores_for_choice.reshape(T, NG, E // NG)
            group_scores = jnp.sum(jax.lax.top_k(grp, 2)[0], axis=-1)
            _, gidx = jax.lax.top_k(group_scores, TOPK_GROUP)
            gmask = jnp.zeros((T, NG), dtype=scores.dtype).at[jnp.arange(T)[:, None], gidx].set(1.0)
            emask = jnp.repeat(gmask, E // NG, axis=1)
            masked = jnp.where(emask > 0, scores_for_choice, 0.0)
            _, topk_idx = jax.lax.top_k(masked, TOP_K)
            topk_w = jnp.take_along_axis(scores, topk_idx, axis=1)
            topk_w = topk_w / (jnp.sum(topk_w, axis=-1, keepdims=True) + 1e-20)
            topk_w = topk_w * ROUTED_SCALE
            rw = jnp.zeros((T, E), dtype=scores.dtype).at[jnp.arange(T)[:, None], topk_idx].add(topk_w)
            return rw

        def _mlp(x, gw, uw, dw):
            return jax.nn.silu(x @ gw.T) * (x @ uw.T) @ dw.T
        key = jax.random.key(seed)
        ks = jax.random.split(key, 10)
        sc = 0.02
        return {'hidden_states': jax.random.normal(ks[0], (1, 128, H), dtype=jnp.float32), 'gate_w': sc * jax.random.normal(ks[1], (E, H), dtype=jnp.float32), 'gate_bias': sc * jax.random.normal(ks[2], (E,), dtype=jnp.float32), 'Wg': sc * jax.random.normal(ks[3], (E, I, H), dtype=jnp.float32), 'Wu': sc * jax.random.normal(ks[4], (E, I, H), dtype=jnp.float32), 'Wd': sc * jax.random.normal(ks[5], (E, H, I), dtype=jnp.float32), 'Sg': sc * jax.random.normal(ks[6], (S_I, H), dtype=jnp.float32), 'Su': sc * jax.random.normal(ks[7], (S_I, H), dtype=jnp.float32), 'Sd': sc * jax.random.normal(ks[8], (H, S_I), dtype=jnp.float32)}
    _L1_ffn_in = _L1_ffn_setup()
    _d = {'L0_attn_x': _L0_attn_in['x'], 'L0_attn_in_proj_w': _L0_attn_in['in_proj_w'], 'L0_attn_conv_w': _L0_attn_in['conv_w'], 'L0_attn_conv_b': _L0_attn_in['conv_b'], 'L0_attn_x_proj_w': _L0_attn_in['x_proj_w'], 'L0_attn_dt_proj_w': _L0_attn_in['dt_proj_w'], 'L0_attn_dt_proj_b': _L0_attn_in['dt_proj_b'], 'L0_attn_A_log': _L0_attn_in['A_log'], 'L0_attn_D': _L0_attn_in['D'], 'L0_attn_out_proj_w': _L0_attn_in['out_proj_w'], 'L0_ffn_w1_w': _L0_ffn_in['w1_w'], 'L0_ffn_w1_s': _L0_ffn_in['w1_s'], 'L0_ffn_w2_w': _L0_ffn_in['w2_w'], 'L0_ffn_w2_s': _L0_ffn_in['w2_s'], 'L0_ffn_h1_w': _L0_ffn_in['h1_w'], 'L0_ffn_h1_s': _L0_ffn_in['h1_s'], 'L0_ffn_h2_w': _L0_ffn_in['h2_w'], 'L0_ffn_h2_s': _L0_ffn_in['h2_s'], 'L0_ffn_w3_w': _L0_ffn_in['w3_w'], 'L0_ffn_w3_s': _L0_ffn_in['w3_s'], 'L1_attn_Wq': _L1_attn_in['Wq'], 'L1_attn_bq': _L1_attn_in['bq'], 'L1_attn_Wkv': _L1_attn_in['Wkv'], 'L1_attn_bkv': _L1_attn_in['bkv'], 'L1_attn_Wo': _L1_attn_in['Wo'], 'L1_ffn_gate_w': _L1_ffn_in['gate_w'], 'L1_ffn_gate_bias': _L1_ffn_in['gate_bias'], 'L1_ffn_Wg': _L1_ffn_in['Wg'], 'L1_ffn_Wu': _L1_ffn_in['Wu'], 'L1_ffn_Wd': _L1_ffn_in['Wd'], 'L1_ffn_Sg': _L1_ffn_in['Sg'], 'L1_ffn_Su': _L1_ffn_in['Su'], 'L1_ffn_Sd': _L1_ffn_in['Sd']}
    _x0 = _d['L0_attn_x']
    _d['L0_attn_x'] = jax.random.normal(jax.random.fold_in(jax.random.key(seed), 1), (4, 512, 128), dtype=_x0.dtype)
    del _x0
    return _d

def reference(L0_attn_x, L0_attn_in_proj_w, L0_attn_conv_w, L0_attn_conv_b, L0_attn_x_proj_w, L0_attn_dt_proj_w, L0_attn_dt_proj_b, L0_attn_A_log, L0_attn_D, L0_attn_out_proj_w, L0_ffn_w1_w, L0_ffn_w1_s, L0_ffn_w2_w, L0_ffn_w2_s, L0_ffn_h1_w, L0_ffn_h1_s, L0_ffn_h2_w, L0_ffn_h2_s, L0_ffn_w3_w, L0_ffn_w3_s, L1_attn_Wq, L1_attn_bq, L1_attn_Wkv, L1_attn_bkv, L1_attn_Wo, L1_ffn_gate_w, L1_ffn_gate_bias, L1_ffn_Wg, L1_ffn_Wu, L1_ffn_Wd, L1_ffn_Sg, L1_ffn_Su, L1_ffn_Sd):

    def _L0_attn_ref(x, in_proj_w, conv_w, conv_b, x_proj_w, dt_proj_w, dt_proj_b, A_log, D, out_proj_w):
        import jax, jax.numpy as jnp
        import numpy as np
        D_MODEL = 128
        D_STATE = 16
        D_CONV = 4
        EXPAND = 2
        D_INNER = D_MODEL * EXPAND
        B = 1
        L = 256
        Bb = x.shape[0]
        xz = x @ in_proj_w.T
        x_ssm, z = jnp.split(xz, 2, axis=-1)
        xt = jnp.swapaxes(x_ssm, 1, 2)
        xc = jax.lax.conv_general_dilated(xt, conv_w, window_strides=(1,), padding=[(D_CONV - 1, 0)], feature_group_count=D_INNER, dimension_numbers=('NCH', 'OIH', 'NCH'))
        xc = xc + conv_b[None, :, None]
        xc = jax.nn.silu(jnp.swapaxes(xc, 1, 2))
        A = -jnp.exp(A_log)
        xp = xc @ x_proj_w.T
        dt_r = xp[..., :1]
        Bv = xp[..., 1:1 + D_STATE]
        Cv = xp[..., 1 + D_STATE:]
        dt = jax.nn.softplus(dt_r @ dt_proj_w.T + dt_proj_b)
        dA = jnp.exp(dt[..., None] * A)
        dBx = dt[..., None] * Bv[:, :, None, :] * xc[..., None]

        def step(h, inps):
            dA_t, dBx_t, C_t = inps
            h = dA_t * h + dBx_t
            y = jnp.einsum('bdn,bn->bd', h, C_t)
            return (h, y)
        h0 = jnp.zeros((Bb, D_INNER, D_STATE), x.dtype)
        _, ys = jax.lax.scan(step, h0, (jnp.swapaxes(dA, 0, 1), jnp.swapaxes(dBx, 0, 1), jnp.swapaxes(Cv, 0, 1)))
        y = jnp.swapaxes(ys, 0, 1) + xc * D
        return y * jax.nn.silu(z) @ out_proj_w.T

    def _L0_ffn_ref(x, w1_w, w1_s, w2_w, w2_s, h1_w, h1_s, h2_w, h2_s, w3_w, w3_s):
        import jax, jax.numpy as jnp
        import numpy as np
        D_IN, D_HID = (128, 512)

        def _ternary(key, shape):
            return jax.random.randint(key, shape, -1, 2).astype(jnp.float32)

        def _tlin(x, w, s):
            return jnp.einsum('bsi,oi->bso', x, w) * s
        h = jax.nn.silu(_tlin(x, w1_w, w1_s)) * _tlin(x, w2_w, w2_s)
        h = jax.nn.gelu(_tlin(h, h1_w, h1_s), approximate=False)
        h = jax.nn.gelu(_tlin(h, h2_w, h2_s), approximate=False)
        return _tlin(h, w3_w, w3_s)

    def _L1_attn_ref(x, Wq, bq, Wkv, bkv, Wo):
        import jax, jax.numpy as jnp
        import numpy as np
        import math
        NUM_HEADS = 8
        EMB = 128
        HEAD_DIM = 128
        B, T = (1, 512)

        def sinusoidal_pe(T, d, dtype=jnp.float32):
            pos = jnp.arange(T, dtype=dtype)[:, None]
            inv_freq = jnp.exp(-math.log(10000.0) * jnp.arange(0, d, 2, dtype=dtype) / d)
            ang = pos * inv_freq[None, :]
            pe = jnp.zeros((T, d), dtype=dtype)
            pe = pe.at[:, 0::2].set(jnp.sin(ang))
            pe = pe.at[:, 1::2].set(jnp.cos(ang))
            return pe
        Bsz, Tlen, E = x.shape
        q = (x @ Wq + bq).reshape(Bsz, Tlen, NUM_HEADS, HEAD_DIM)
        kv = x @ Wkv + bkv
        k, v = (kv[..., :HEAD_DIM], kv[..., HEAD_DIM:])
        q = jnp.transpose(q, (0, 2, 1, 3))
        pe = sinusoidal_pe(Tlen, HEAD_DIM, x.dtype)
        q = q + pe[None, None, :, :]
        k = k + pe[None, :, :]
        scale = 1.0 / math.sqrt(HEAD_DIM)
        scores = jnp.einsum('bhqd,bkd->bhqk', q, k) * scale
        causal = jnp.tril(jnp.ones((Tlen, Tlen), dtype=bool))
        scores = jnp.where(causal[None, None, :, :], scores, jnp.finfo(scores.dtype).min)
        probs = jax.nn.softmax(scores, axis=-1)
        attn = jnp.einsum('bhqk,bkd->bhqd', probs, v)
        out = jnp.transpose(attn, (0, 2, 1, 3)).reshape(Bsz, Tlen, NUM_HEADS * HEAD_DIM)
        return out @ Wo

    def _L1_ffn_ref(hidden_states, gate_w, gate_bias, Wg, Wu, Wd, Sg, Su, Sd):
        import jax, jax.numpy as jnp
        import numpy as np
        H = 128
        I = 88
        E = 64
        TOP_K = 8
        NG = 8
        TOPK_GROUP = 4
        N_SHARED = 2
        ROUTED_SCALE = 2.5
        S_I = I * N_SHARED

        def _route(x, gate_w, gate_bias):
            T = x.shape[0]
            logits = x @ gate_w.T
            scores = jax.nn.sigmoid(logits)
            scores_for_choice = scores + gate_bias[None, :]
            grp = scores_for_choice.reshape(T, NG, E // NG)
            group_scores = jnp.sum(jax.lax.top_k(grp, 2)[0], axis=-1)
            _, gidx = jax.lax.top_k(group_scores, TOPK_GROUP)
            gmask = jnp.zeros((T, NG), dtype=scores.dtype).at[jnp.arange(T)[:, None], gidx].set(1.0)
            emask = jnp.repeat(gmask, E // NG, axis=1)
            masked = jnp.where(emask > 0, scores_for_choice, 0.0)
            _, topk_idx = jax.lax.top_k(masked, TOP_K)
            topk_w = jnp.take_along_axis(scores, topk_idx, axis=1)
            topk_w = topk_w / (jnp.sum(topk_w, axis=-1, keepdims=True) + 1e-20)
            topk_w = topk_w * ROUTED_SCALE
            rw = jnp.zeros((T, E), dtype=scores.dtype).at[jnp.arange(T)[:, None], topk_idx].add(topk_w)
            return rw

        def _mlp(x, gw, uw, dw):
            return jax.nn.silu(x @ gw.T) * (x @ uw.T) @ dw.T
        B, S, _ = hidden_states.shape
        x = hidden_states.reshape(B * S, H)
        rw = _route(x, gate_w, gate_bias)
        expert_out = jax.vmap(lambda gw_, uw_, dw_: _mlp(x, gw_, uw_, dw_))(Wg, Wu, Wd)
        routed = jnp.einsum('eth,te->th', expert_out, rw)
        shared = _mlp(x, Sg, Su, Sd)
        out = (routed + shared).reshape(B, S, H)
        return out
    x = L0_attn_x
    x = x + 0.5 * _L0_ffn_ref(_layernorm(x, axis=-1), L0_ffn_w1_w, L0_ffn_w1_s, L0_ffn_w2_w, L0_ffn_w2_s, L0_ffn_h1_w, L0_ffn_h1_s, L0_ffn_h2_w, L0_ffn_h2_s, L0_ffn_w3_w, L0_ffn_w3_s)
    x = x + _L0_attn_ref(_layernorm(x, axis=-1), L0_attn_in_proj_w, L0_attn_conv_w, L0_attn_conv_b, L0_attn_x_proj_w, L0_attn_dt_proj_w, L0_attn_dt_proj_b, L0_attn_A_log, L0_attn_D, L0_attn_out_proj_w)
    x = x + 0.5 * _L0_ffn_ref(_layernorm(x, axis=-1), L0_ffn_w1_w, L0_ffn_w1_s, L0_ffn_w2_w, L0_ffn_w2_s, L0_ffn_h1_w, L0_ffn_h1_s, L0_ffn_h2_w, L0_ffn_h2_s, L0_ffn_w3_w, L0_ffn_w3_s)
    x = x + 0.5 * _L1_ffn_ref(_layernorm(x, axis=-1), L1_ffn_gate_w, L1_ffn_gate_bias, L1_ffn_Wg, L1_ffn_Wu, L1_ffn_Wd, L1_ffn_Sg, L1_ffn_Su, L1_ffn_Sd)
    x = x + _L1_attn_ref(_layernorm(x, axis=-1), L1_attn_Wq, L1_attn_bq, L1_attn_Wkv, L1_attn_bkv, L1_attn_Wo)
    x = x + 0.5 * _L1_ffn_ref(_layernorm(x, axis=-1), L1_ffn_gate_w, L1_ffn_gate_bias, L1_ffn_Wg, L1_ffn_Wu, L1_ffn_Wd, L1_ffn_Sg, L1_ffn_Su, L1_ffn_Sd)
    return x

_drawn_inputs = setup_inputs


def setup_inputs(seed=0):
    import zlib

    import numpy as np

    out = dict(_drawn_inputs(seed))
    spreads = {'L0_attn_conv_b': (0.0, 0.1), 'L0_attn_dt_proj_b': (0.0, 0.1), 'L0_attn_D': (1.0, 0.2)}
    factors = {}
    for name, (base, spread) in spreads.items():
        noise = np.random.default_rng([zlib.crc32(name.encode()), seed]).standard_normal(out[name].shape)
        drawn = base * np.exp(spread * noise) if base else spread * noise
        out[name] = jnp.asarray(drawn.astype(out[name].dtype))
    for name, factor in factors.items():
        out[name] = (out[name] * factor).astype(out[name].dtype)
    return out
```

```python
from contextlib import ExitStack

import numpy as np

import concourse.bass as bass
from concourse import mybir

P = 128
T = 512
NB = 4
NT = T * NB
HID = 512
HC = HID // P
DS = 16
MC = 2
HEADS = 8
E, I = 64, 88
NG = 8
CH = E * I // P
PAIRS = CH // 2
NTT = NT // P
EPS = 1e-5
NEG = -1e30
GONE = -3e38

F32 = mybir.dt.float32
F32R = mybir.dt.float32r
ACT = mybir.ActivationFunctionType
ALU = mybir.AluOpType
AX = mybir.AxisListType.X

C_W1, C_W2, C_H1, C_H2, C_W3 = 0, 4, 8, 12, 16
C_CONV, C_CB, C_DTW, C_DTB, C_D = 17, 25, 27, 29, 31
C_ALOG, C_BQ, C_BK, C_EPS = 33, 65, 73, 74
NCOL = 75
R_GB, R_BV, NROW = 0, 64, 192
K_ID, K_MASK, K_PE, K_TIE, K_ID64, K_ID32, NCONST = 0, 128, 256, 768, 832, 896, 928
W_G, W_U, W_H1, W_H2, W_3, NW = 0, 512, 1024, 3072, 5120, 5632
M_IN, M_X, M_OUT, NM = 0, 512, 578, 834
A_Q, A_K, A_V, A_O, NA = 0, 1024, 1152, 1280, 2304
S_R, S_G, S_U, NS = 0, 64, 240, 416


def program(nc, d):
    ctx = ExitStack()
    with ctx:
        def keeper(stack):
            return lambda name, shape, dt=F32: stack.enter_context(nc.sbuf_tensor(name, shape, dt))

        def sem(name):
            return ctx.enter_context(nc.semaphore(name))

        sb = keeper(ctx)
        x = sb("x", [P, NT])
        xn_hi = sb("xn_hi", [P, NT], F32R)
        xn_lo = sb("xn_lo", [P, NT], F32R)
        ln_c = sb("ln_c", [P, NT])
        ln_t = sb("ln_t", [P, NT])
        cols = sb("cols", [P, NCOL])
        rows = sb("rows", [P, NROW])
        const = sb("const", [P, NCONST])
        mean_w = sb("mean_w", [P, P])
        rstd = sb("rstd", [P, NTT])
        w3_half = sb("w3_half", [P, 1])
        neg_a = sb("neg_a", [P, MC * DS])

        with ExitStack() as layer:
            lb = keeper(layer)
            wh, wl = lb("wh", [P, NW], F32R), lb("wl", [P, NW], F32R)
            with ExitStack() as s:
                fb = keeper(s)
                w_raw = fb("w_raw", [P, NW])
                f_s = fb("f_s", [P, HC, T])
                f_h = fb("f_h", [P, HC, T])
                hid_hi = fb("hid_hi", [P, 3, HC, T], F32R)
                hid_lo = fb("hid_lo", [P, 3, HC, T], F32R)
            with ExitStack() as s:
                fb = keeper(s)
                m_raw = fb("m_raw", [P, 2 * T])
                dt_b = m_raw[:, :].rearrange("p (m t) -> p m t", m=MC)
                mh, ml = fb("mh", [P, NM], F32R), fb("ml", [P, NM], F32R)
                dtw_hi = fb("dtw_hi", [P, MC, P], F32R)
                dtw_lo = fb("dtw_lo", [P, MC, P], F32R)
                sel_bc = fb("sel_bc", [P, 2 * DS, P], F32R)
                bc = fb("bc", [P, NT], F32R)
                xc = fb("xc", [P, MC, NT])
                sz = fb("sz", [P, MC, NT])
                dt = fb("dt", [P, MC, NT])
                du = fb("du", [P, MC, NT])
                g_hi = fb("g_hi", [P, MC, T], F32R)
                g_lo = fb("g_lo", [P, MC, T], F32R)
                m_y = fb("m_y", [P, MC, T])
                m_da = fb("m_da", [P, 2, T])
                m_db = ln_c[:, 0:2 * T].rearrange("p (k t) -> p k t", k=2)
                m_c = ln_c[:, 2 * T:NT].rearrange("p (k t) -> p k t", k=2)
                m_h = ln_t[:, 0:2 * T].rearrange("p (k t) -> p k t", k=2)
                m_hc = ln_t[:, 2 * T:NT].rearrange("p (k t) -> p k t", k=2)
        with ExitStack() as layer:
            lb = keeper(layer)
            ah, al = lb("ah", [P, NA], F32R), lb("al", [P, NA], F32R)
            sh, sl = lb("sh", [P, NS], F32R), lb("sl", [P, NS], F32R)
            sd_h, sd_l = lb("sd_h", [I, 2, P], F32R), lb("sd_l", [I, 2, P], F32R)
            with ExitStack() as s:
                fb = keeper(s)
                s_raw = fb("s_raw", [P, NS])
                sd_raw = fb("sd_raw", [I, 2, P])
                a_raw = fb("a_raw", [P, NA])
                e_raw = fb("e_raw", [P, 2, 4, P])
                eh, el = fb("eh", [P, 2, 4, P], F32R), fb("el", [P, 2, 3, P], F32R)
                rwt = fb("rwt", [P, NT], F32R)
                r_s = fb("r_s", [P, NTT, E])
                r_c = fb("r_c", [P, NTT, E])
                r_t = fb("r_t", [P, NTT * E])
                r_u = fb("r_u", [P, NTT * E])
                r_small = fb("r_small", [P, 4, NTT * NG])
                rw_cat = fb("rw_cat", [P, NTT, 2, E])
                e_s = fb("e_s", [P, 4, T])
                e_p = fb("e_p", [P, 2, T])
                e_h = fb("e_h", [P, 4, T])
                e_hi = fb("e_hi", [P, 4, T], F32R)
                e_lo = fb("e_lo", [P, 4, T], F32R)
            with ExitStack() as s:
                fb = keeper(s)
                xb_hi, xb_lo = fb("xb_hi", [P, T], F32R), fb("xb_lo", [P, T], F32R)
                k_hi, k_lo = fb("k_hi", [P, T], F32R), fb("k_lo", [P, T], F32R)
                v_hi, v_lo = fb("v_hi", [P, 4, P], F32R), fb("v_lo", [P, 4, P], F32R)
                kv32 = fb("kv32", [P, 2, T])
                q32 = fb("q32", [P, 2, T])
                q_hi, q_lo = fb("q_hi", [P, 2, T], F32R), fb("q_lo", [P, 2, T], F32R)
                p32 = fb("p32", [P, 4, T])
                pt_hi, pt_lo = fb("pt_hi", [P, 3, T], F32R), fb("pt_lo", [P, 3, T], F32R)
                o_hi, o_lo = fb("o_hi", [P, 2, T], F32R), fb("o_lo", [P, 2, T], F32R)
                st = fb("st", [P, 2, 4, 4])
                maskr, idr = fb("maskr", [P, P], F32R), fb("idr", [P, P], F32R)

        ps = ctx.enter_context(nc.psum_tensor("ps", [P, 8, T], F32))
        ident = const[:, K_ID:K_ID + P]

        loaded = sem("loaded")
        ffn_in = [sem(f"ffn_in{k}") for k in range(3)]
        ones_set = sem("ones_set")
        w_split = sem("w_split")
        w_hi_c = sem("w_hi_c")
        w_split_c = sem("w_split_c")
        stored = sem("stored")
        phase_end = sem("phase_end")
        a_in, a_hi, a_lo = sem("a_in"), sem("a_hi"), sem("a_lo")

        class Signals:

            def __init__(self, sems, base):
                self.sems, self.base = sems, base

            def __getitem__(self, name):
                return self.sems[name]

            def __call__(self, name, n):
                return self.sems[name], self.base[name] + n

        def group(tag, counts, runs):
            sems = {n: sem(f"{tag}_{n}") for n in counts}
            primed.extend(sems.values())
            return [Signals(sems, {n: 1 + k * c for n, c in counts.items()}) for k in range(runs)]

        primed, primed_all = [], sem("primed_all")

        TILES = 2 * NB + CH * NB
        ROUTE_STEPS = 26
        LN = group("ln", dict.fromkeys("mean centred squared var dev inv diag spread normed xn_hi xn_lo".split(), NB), 6)
        F1, F2 = group("ffn", {"gate": 4 * NB, "up": 4 * NB, "silu": 4 * NB, "hidden": 4 * NB, "mid": 8 * NB, "gelu": 8 * NB,
                               "hid_hi": 12 * NB, "hid_lo": 12 * NB, "out": NB, "x_new": NB}, 2)
        E1, E2 = group("moe", {"raw_in0": 32 * PAIRS, "raw_in1": 32 * PAIRS, "small_in": 32, "small_hi": 2, "small_lo": 2,
                               "logits": 2, "scores": 2, "route": ROUTE_STEPS, "routed": 2, "rw_t": 4, "rwt": 4,
                               "spread": CH * NB, "w_hi": 2 * CH, "w_lo": 2 * CH, "x_new": NB}
                       | dict.fromkeys("gate up silu gated weighted h_hi h_lo down".split(), TILES), 2)
        M, = group("mix", dict.fromkeys((
            "raw_in w_hi w_lo dt_w sel_set inproj zproj biased conv xc sz xc_hi xc_lo bcdt "
            "bc_hi bc_lo v nabs e ln dt du b_spread c_spread da db h c_copy hc y_sum ylin "
            "gated g_hi g_lo out x_new aexp bc_zero dt_b").split(), 0), 1)
        A, = group("att", dict.fromkeys((
            "mask xb_hi xb_lo kv k32 k_hi k_lo v32 v_hi v_lo qp q32 q_hi q_lo s "
            "mx nmx p inv pn pt pt_hi pt_lo o o_hi o_lo y x_new").split(), 0), 1)

        block = ctx.enter_context(nc.Block())

        def end_phase(eng):
            eng.drain().then_inc(phase_end, 1)

        def start_phase(eng, k):
            eng.wait_ge(phase_end, 4 * k)

        def cut(b):
            return slice(b * T, (b + 1) * T)

        def mm3(pe, out, w_hi, w_lo, x_hi, x_lo, start, stop):
            pe.matmul(out, w_hi, x_hi, start=start, stop=False, skip_group_check=True)
            pe.matmul(out, w_hi, x_lo, start=False, stop=False, skip_group_check=True)
            return pe.matmul(out, w_lo, x_hi, start=False, stop=stop, skip_group_check=True)

        def split_hi(act, hi, full):
            return act.activation(hi, full, ACT.Identity)

        def split_lo(eng, lo, full, hi):
            return eng.tensor_tensor(lo, full, hi.bitcast(F32), ALU.subtract)

        def ln_pe(pe, L):
            def mean(b):
                pe.matmul(ps[:, b, :], mean_w[:, :], x[:, cut(b)], start=True, stop=True).then_inc(L["mean"], 1)

            def var(b):
                pe.wait_ge(*L("squared", b + 1))
                for t in range(4):
                    tt = slice(b * T + t * P, b * T + (t + 1) * P)
                    last = pe.matmul(ps[:, 4 + b, t:t + 1], ln_t[:, tt], mean_w[:, 0:1], start=True, stop=True, skip_group_check=True)
                last.then_inc(L["var"], 1)

            def spread(b):
                pe.wait_ge(*L("diag", b + 1))
                pe.matmul(ps[:, 4 + b, :], mean_w[:, :], ln_t[:, cut(b)], start=True, stop=True).then_inc(L["spread"], 1)

            mean(0)
            mean(1)
            var(0)
            mean(2)
            var(1)
            spread(0)
            mean(3)
            var(2)
            spread(1)
            var(3)
            spread(2)
            spread(3)

        def banks_free(pe, L):
            pe.wait_ge(*L("centred", NB))
            pe.wait_ge(*L("normed", NB))

        def ln_dve(dve, L):
            def centre(b):
                dve.wait_ge(*L("mean", b + 1))
                dve.tensor_tensor(ln_c[:, cut(b)], x[:, cut(b)], ps[:, b, :], ALU.subtract).then_inc(L["centred"], 1)

            def diagonal(b):
                r = rstd[:, 4 * b:4 * b + 4]
                dve.wait_ge(*L("dev", b + 1))
                dve.reciprocal(r, r).then_inc(L["inv"], 1)
                dve.wait_ge(*L("inv", b + 1))
                dve.scalar_tensor_tensor(ln_t[:, cut(b)].rearrange("p (t n) -> p t n", t=4), ident.unsqueeze(1).broadcast_to([P, 4, P]),
                                         float(P), r.unsqueeze(2).broadcast_to([P, 4, P]), ALU.mult, ALU.mult).then_inc(L["diag"], 1)

            def normalise(b):
                dve.wait_ge(*L("spread", b + 1))
                dve.tensor_tensor(ln_c[:, cut(b)], ln_c[:, cut(b)], ps[:, 4 + b, :], ALU.mult).then_inc(L["normed"], 1)

            centre(0)
            centre(1)
            diagonal(0)
            centre(2)
            diagonal(1)
            normalise(0)
            centre(3)
            diagonal(2)
            normalise(1)
            diagonal(3)
            normalise(2)
            normalise(3)

        def ln_act(act, L):
            def square(b):
                act.wait_ge(*L("centred", b + 1))
                act.activation(ln_t[:, cut(b)], ln_c[:, cut(b)], ACT.Square).then_inc(L["squared"], 1)

            def deviation(b):
                act.wait_ge(*L("var", b + 1))
                act.activation(rstd[:, 4 * b:4 * b + 4], ps[:, 4 + b, 0:4], ACT.Sqrt, bias=cols[:, C_EPS:C_EPS + 1]).then_inc(L["dev"], 1)

            def high(b):
                act.wait_ge(*L("normed", b + 1))
                split_hi(act, xn_hi[:, cut(b)], ln_c[:, cut(b)]).then_inc(L["xn_hi"], 1)

            square(0)
            square(1)
            deviation(0)
            square(2)
            deviation(1)
            high(0)
            square(3)
            deviation(2)
            high(1)
            deviation(3)
            high(2)
            high(3)

        def ln_pool(pool, L):
            for b in range(NB):
                pool.wait_ge(*L("xn_hi", b + 1))
                split_lo(pool, xn_lo[:, cut(b)], ln_c[:, cut(b)], xn_hi[:, cut(b)]).then_inc(L["xn_lo"], 1)

        def ffn_pe(pe, S, L):
            banks_free(pe, L)
            with pe.Fori(0, NB) as i:
                blk = bass.ds(i * T, T)
                pe.wait_ge(*L("xn_lo", i + 1))
                for o in range(HC):
                    c = slice(o * P, (o + 1) * P)
                    g = slice(W_G + o * P, W_G + (o + 1) * P)
                    u = slice(W_U + o * P, W_U + (o + 1) * P)
                    if o == 3:
                        pe.wait_ge(*S("x_new", i))
                    mm3(pe, ps[:, o, :], wh[:, g], wl[:, g], xn_hi[:, blk], xn_lo[:, blk], True, True).then_inc(S["gate"], 1)
                    mm3(pe, ps[:, 4 + o, :], wh[:, u], wl[:, u], xn_hi[:, blk], xn_lo[:, blk], True, True).then_inc(S["up"], 1)
                for layer_, (w0, bank) in enumerate(((W_H1, 0), (W_H2, 4))):
                    if S is F1 and layer_ == 1:
                        pe.wait_ge(w_split_c, 1)
                    for k in range(HC):
                        pe.wait_ge(*S("hid_lo", 12 * i + 4 * layer_ + k + 1))
                        for o in range(HC):
                            if layer_ == 0 and k == 0:
                                pe.wait_ge(*S("silu", 4 * i + o + 1))
                            w = slice(w0 + k * HID + o * P, w0 + k * HID + (o + 1) * P)
                            last = mm3(pe, ps[:, bank + o, :], wh[:, w], wl[:, w], hid_hi[:, layer_, k, :],
                                       hid_lo[:, layer_, k, :], k == 0, k == HC - 1)
                            if k == HC - 1:
                                last.then_inc(S["mid"], 1)
                for k in range(HC):
                    pe.wait_ge(*S("hid_lo", 12 * i + 8 + k + 1))
                    w = slice(W_3 + k * P, W_3 + (k + 1) * P)
                    last = mm3(pe, ps[:, 3, :], wh[:, w], wl[:, w], hid_hi[:, 2, k, :], hid_lo[:, 2, k, :], k == 0, k == HC - 1)
                last.then_inc(S["out"], 1)

        def ffn_act(act, S):
            with act.Fori(0, NB) as i:
                for o in range(HC):
                    act.wait_ge(*S("gate", 4 * i + o + 1))
                    act.activation(f_s[:, o, :], ps[:, o, :], ACT.Silu, scale=cols[:, C_W1 + o:C_W1 + o + 1]).then_inc(S["silu"], 1)
                for layer_, (c0, bank) in enumerate(((C_H1, 0), (C_H2, 4))):
                    for o in range(HC):
                        act.wait_ge(*S("mid", 8 * i + 4 * layer_ + o + 1))
                        act.wait_ge(*S("hid_lo", 12 * i + 4 * layer_ + o + 1))
                        act.activation(f_h[:, o, :], ps[:, bank + o, :], ACT.Gelu, scale=cols[:, c0 + o:c0 + o + 1]).then_inc(S["gelu"], 1)

        def ffn_dve(dve, S):
            def split(i, layer_, o):
                q = 4 * layer_ + o
                dve.tensor_copy(hid_hi[:, layer_, o, :], f_h[:, o, :]).then_inc(S["hid_hi"], 1)
                dve.wait_ge(*S("hid_hi", 12 * i + q + 1))
                split_lo(dve, hid_lo[:, layer_, o, :], f_h[:, o, :], hid_hi[:, layer_, o, :]).then_inc(S["hid_lo"], 1)

            with dve.Fori(0, NB) as i:
                blk = bass.ds(i * T, T)
                for o in range(HC):
                    dve.wait_ge(*S("up", 4 * i + o + 1))
                    dve.wait_ge(*S("silu", 4 * i + o + 1))
                    dve.scalar_tensor_tensor(f_h[:, o, :], ps[:, 4 + o, :], cols[:, C_W2 + o:C_W2 + o + 1], f_s[:, o, :],
                                             ALU.mult, ALU.mult).then_inc(S["hidden"], 1)
                    dve.wait_ge(*S("hidden", 4 * i + o + 1))
                    split(i, 0, o)
                for layer_ in (1, 2):
                    for o in range(HC):
                        dve.wait_ge(*S("gelu", 8 * i + 4 * (layer_ - 1) + o + 1))
                        split(i, layer_, o)
                dve.wait_ge(*S("out", i + 1))
                dve.scalar_tensor_tensor(x[:, blk], ps[:, 3, :], w3_half[:, :], x[:, blk], ALU.mult, ALU.add).then_inc(S["x_new"], 1)

        def mix_pe(pe, L):
            pe.wait_ge(*M("w_lo", 1))
            banks_free(pe, L)
            with pe.Fori(0, NB) as i:
                blk = bass.ds(i * T, T)
                pe.wait_ge(*L("xn_lo", i + 1))
                pe.wait_ge(*M("conv", 6 * i))
                pe.wait_ge(*M("sz", 2 * i))
                for o in range(2 * MC):
                    w = slice(M_IN + o * P, M_IN + (o + 1) * P)
                    mm3(pe, ps[:, o, :], mh[:, w], ml[:, w], xn_hi[:, blk], xn_lo[:, blk], True, True)\
                        .then_inc(M["inproj"] if o < MC else M["zproj"], 1)
                for m in range(MC):
                    pe.wait_ge(*M("xc_lo", 2 * i + m + 1))
                    if m == 0:
                        pe.wait_ge(*M("dt_w", 2))
                        pe.wait_ge(*M("bc_lo", i))
                        pe.wait_ge(*M("v", 2 * i))
                    w = slice(M_X + 33 * m + 1, M_X + 33 * m + 33)
                    mm3(pe, ps[0:2 * DS, 4, :], mh[:, w], ml[:, w], g_hi[:, m, :], g_lo[:, m, :], m == 0, m == MC - 1)
                    last = mm3(pe, ps[:, 5, :], dtw_hi[:, m, :], dtw_lo[:, m, :], g_hi[:, m, :], g_lo[:, m, :], m == 0, m == MC - 1)
                last.then_inc(M["bcdt"], 1)
            pe.wait_ge(*M("v", 2 * NB))
            pe.wait_ge(*M("sel_set", 1))
            pe.wait_ge(*M("conv", 6 * NB))
            pe.wait_ge(*M("sz", 2 * NB))
            pe.wait_ge(*M("bc_lo", NB))
            pe.wait_ge(*M("bc_zero", 1))
            with pe.Fori(0, NB) as i:
                blk = bass.ds(i * T, T)

                def spread(n):
                    pe.wait_ge(*M("db", 32 * i + (2 * n - 2 if n >= 2 else 0)))
                    pe.matmul(ps[:, n % 2, :], sel_bc[:, n, :], bc[:, blk], start=True, stop=True).then_inc(M["b_spread"], 1)
                    pe.wait_ge(*M("c_copy", 16 * i + (n - 1 if n >= 2 else 0)))
                    pe.matmul(ps[:, 2 + n % 2, :], sel_bc[:, DS + n, :], bc[:, blk], start=True, stop=True).then_inc(M["c_spread"], 1)

                spread(0)
                spread(1)
                pe.wait_ge(*M("ylin", 2 * i))
                for n in range(DS):
                    for m in range(MC):
                        q = 2 * n + m
                        pe.wait_ge(*M("hc", 32 * i + q + 1))
                        pe.matmul(ps[:, 4 + m, :], ident, m_hc[:, q % 2, :], start=(n == 0), stop=(n == DS - 1),
                                  skip_group_check=True).then_inc(M["y_sum"], 1)
                    if n + 2 < DS:
                        spread(n + 2)
                pe.wait_ge(*M("x_new", i))
                for m in range(MC):
                    pe.wait_ge(*M("g_lo", 2 * i + m + 1))
                    w = slice(M_OUT + m * P, M_OUT + (m + 1) * P)
                    last = mm3(pe, ps[:, 6, :], mh[:, w], ml[:, w], g_hi[:, m, :], g_lo[:, m, :], m == 0, m == MC - 1)
                last.then_inc(M["out"], 1)

        def mix_act(act):
            with act.Fori(0, NB) as i:
                blk = bass.ds(i * T, T)
                for m in range(MC):
                    act.wait_ge(*M("inproj", 2 * i + m + 1))
                    act.wait_ge(*M("xc", 2 * i))
                    act.activation(m_y[:, m, :], ps[:, m, :], ACT.Identity, scale=cols[:, C_CONV + 4 * m + 3:C_CONV + 4 * m + 4],
                                   bias=cols[:, C_CB + m:C_CB + m + 1]).then_inc(M["biased"], 1)
                for m in range(MC):
                    act.wait_ge(*M("zproj", 2 * i + m + 1))
                    act.wait_ge(phase_end, 4)
                    act.activation(sz[:, m, blk], ps[:, 2 + m, :], ACT.Silu).then_inc(M["sz"], 1)
                for m in range(MC):
                    act.wait_ge(*M("conv", 6 * i + 3 * m + 3))
                    act.wait_ge(phase_end, 4)
                    act.activation(xc[:, m, blk], m_y[:, m, :], ACT.Silu).then_inc(M["xc"], 1)
                act.wait_ge(*M("bcdt", i + 1))
                act.wait_ge(phase_end, 4)
                act.activation(bc[0:2 * DS, blk], ps[0:2 * DS, 4, :], ACT.Identity).then_inc(M["bc_hi"], 1)
                for m in range(MC):
                    act.wait_ge(phase_end, 4)
                    act.activation(dt[:, m, blk], ps[:, 5, :], ACT.Identity, scale=cols[:, C_DTW + m:C_DTW + m + 1],
                                   bias=cols[:, C_DTB + m:C_DTB + m + 1]).then_inc(M["v"], 1)
            act.activation(neg_a[:, :], cols[:, C_ALOG:C_ALOG + MC * DS], ACT.Exp).then_inc(M["aexp"], 1)
            for b in range(NB):
                act.wait_ge(*M("nabs", b + 1))
                act.activation(du[:, :, cut(b)], du[:, :, cut(b)], ACT.Exp).then_inc(M["e"], 1)
            for b in range(NB):
                act.wait_ge(*M("e", b + 1))
                act.activation(du[:, :, cut(b)], du[:, :, cut(b)], ACT.Ln, bias=1.0).then_inc(M["ln"], 1)
            act.wait_ge(*M("aexp", 2))
            with act.Fori(0, NB) as i:
                act.wait_ge(*M("dt_b", i + 1))
                for n in range(DS):
                    act.wait_ge(*M("c_spread", 16 * i + n + 1))
                    act.wait_ge(*M("hc", 32 * i + (2 * n - 2 if n >= 2 else 0)))
                    act.activation(m_c[:, n % 2, :], ps[:, 2 + n % 2, :], ACT.Identity).then_inc(M["c_copy"], 1)
                    for m in range(MC):
                        q = 2 * n + m
                        act.wait_ge(*M("h", 32 * i + (q - 1 if q >= 2 else 0)))
                        act.activation(m_da[:, q % 2, :], dt_b[:, m, :], ACT.Exp,
                                       scale=neg_a[:, m * DS + n:m * DS + n + 1]).then_inc(M["da"], 1)
                for m in range(MC):
                    act.wait_ge(*M("gated", 2 * i + m + 1))
                    split_hi(act, g_hi[:, m, :], m_y[:, m, :]).then_inc(M["g_hi"], 1)

        def mix_dve(dve):
            dve.wait_ge(*M("w_lo", 1))
            for half, (src, dst) in enumerate(((mh, dtw_hi), (ml, dtw_lo))):
                v = src[:, M_X:M_X + 66].rearrange("p (m c) -> p m c", m=MC)[:, :, 0:1].bitcast(F32)
                dve.tensor_copy(dst[:, :, :], v.broadcast_to([P, MC, P])).then_inc(M["dt_w"], 1)
            dve.tensor_copy(sel_bc[:, :, :], const[:, K_ID32:K_ID32 + 2 * DS].unsqueeze(2).broadcast_to([P, 2 * DS, P]))\
                .then_inc(M["sel_set"], 1)
            with dve.Fori(0, NB) as i:
                blk = bass.ds(i * T, T)
                for m in range(MC):
                    dve.wait_ge(*M("biased", 2 * i + m + 1))
                    for s_, j in enumerate((2, 1, 0)):
                        back = 3 - j
                        dve.wait_ge(*M("conv", 6 * i + 3 * m + s_))
                        dve.scalar_tensor_tensor(m_y[:, m, back:T], ps[:, m, 0:T - back], cols[:, C_CONV + 4 * m + j:C_CONV + 4 * m + j + 1],
                                                 m_y[:, m, back:T], ALU.mult, ALU.add).then_inc(M["conv"], 1)
                for m in range(MC):
                    dve.wait_ge(*M("xc", 2 * i + m + 1))
                    dve.wait_ge(*M("bcdt", i))
                    dve.tensor_copy(g_hi[:, m, :], xc[:, m, blk]).then_inc(M["xc_hi"], 1)
                    dve.wait_ge(*M("xc_hi", 2 * i + m + 1))
                    split_lo(dve, g_lo[:, m, :], xc[:, m, blk], g_hi[:, m, :]).then_inc(M["xc_lo"], 1)
                dve.wait_ge(*M("bc_hi", i + 1))
                split_lo(dve, bc[2 * DS:4 * DS, blk], ps[0:2 * DS, 4, :], bc[0:2 * DS, blk]).then_inc(M["bc_lo"], 1)
            dve.wait_ge(*M("v", 2 * NB))
            for b in range(NB):
                dve.scalar_tensor_tensor(du[:, :, cut(b)], dt[:, :, cut(b)], -1.0, dt[:, :, cut(b)], ALU.mult, ALU.min).then_inc(M["nabs"], 1)
            dve.wait_ge(*M("aexp", 1))
            dve.tensor_scalar(neg_a[:, :], neg_a[:, :], -1.0, None, ALU.mult).then_inc(M["aexp"], 1)
            for b in range(NB):
                dve.wait_ge(*M("ln", b + 1))
                dve.scalar_tensor_tensor(dt[:, :, cut(b)], dt[:, :, cut(b)], 0.0, du[:, :, cut(b)], ALU.max, ALU.add).then_inc(M["dt"], 1)
                dve.wait_ge(*M("dt", b + 1))
                dve.tensor_tensor(du[:, :, cut(b)], dt[:, :, cut(b)], xc[:, :, cut(b)], ALU.mult).then_inc(M["du"], 1)
            dve.wait_ge(*M("du", NB))
            with dve.Fori(0, NB) as i:
                blk = bass.ds(i * T, T)

                def input_term(q):
                    n, m = q // 2, q % 2
                    dve.wait_ge(*M("h", 32 * i + max(q - 1, 0)))
                    dve.wait_ge(*M("b_spread", 16 * i + n + 1))
                    dve.tensor_tensor(m_db[:, q % 2, :], du[:, m, blk], ps[:, n % 2, :], ALU.mult).then_inc(M["db"], 1)

                dve.tensor_copy(dt_b, dt[:, :, blk]).then_inc(M["dt_b"], 1)
                input_term(0)
                for q in range(2 * DS):
                    if q + 1 < 2 * DS:
                        input_term(q + 1)
                    dve.wait_ge(*M("da", 32 * i + q + 1))
                    dve.wait_ge(*M("db", 32 * i + q + 1))
                    dve.wait_ge(*M("hc", 32 * i + (q - 1 if q >= 2 else 0)))
                    dve.tensor_tensor_scan(m_h[:, q % 2, :], m_da[:, q % 2, :], m_db[:, q % 2, :], 0.0,
                                           ALU.mult, ALU.add).then_inc(M["h"], 1)
                for m in range(MC):
                    dve.wait_ge(*M("y_sum", 32 * i + 31 + m))
                    dve.scalar_tensor_tensor(m_y[:, m, :], xc[:, m, blk], cols[:, C_D + m:C_D + m + 1], ps[:, 4 + m, :],
                                             ALU.mult, ALU.add).then_inc(M["ylin"], 1)
                for m in range(MC):
                    dve.wait_ge(*M("ylin", 2 * i + m + 1))
                    dve.tensor_tensor(m_y[:, m, :], m_y[:, m, :], sz[:, m, blk], ALU.mult).then_inc(M["gated"], 1)
                for m in range(MC):
                    dve.wait_ge(*M("g_hi", 2 * i + m + 1))
                    split_lo(dve, g_lo[:, m, :], m_y[:, m, :], g_hi[:, m, :]).then_inc(M["g_lo"], 1)
                dve.wait_ge(*M("out", i + 1))
                dve.tensor_tensor(x[:, blk], x[:, blk], ps[:, 6, :], ALU.add).then_inc(M["x_new"], 1)

        def mix_pool(pool):
            with pool.Fori(0, NB) as i:
                for q in range(2 * DS):
                    n = q // 2
                    pool.wait_ge(*M("h", 32 * i + q + 1))
                    pool.wait_ge(*M("c_copy", 16 * i + n + 1))
                    pool.wait_ge(*M("y_sum", 32 * i + (q - 1 if q >= 2 else 0)))
                    pool.tensor_tensor(m_hc[:, q % 2, :], m_h[:, q % 2, :], m_c[:, n % 2, :], ALU.mult).then_inc(M["hc"], 1)

        SHARED = 2 * NB
        PER = 2 * NB

        def moe_pe(pe, S, L):
            pe.wait_ge(*S("small_lo", 1))
            banks_free(pe, L)
            for t in range(NTT):
                pe.wait_ge(*L("xn_lo", t // 4 + 1))
                tt = slice(t * P, (t + 1) * P)
                r = slice(S_R, S_R + E)
                out = ps[:, 6 + t // 8, (t % 8) * E:(t % 8 + 1) * E]
                pe.matmul(out, xn_hi[:, tt], sh[:, r], start=True, stop=False, skip_group_check=True)
                pe.matmul(out, xn_hi[:, tt], sl[:, r], start=False, stop=False, skip_group_check=True)
                last = pe.matmul(out, xn_lo[:, tt], sh[:, r], start=False, stop=True, skip_group_check=True)
                if t % 8 == 7:
                    last.then_inc(S["logits"], 1)
            pe.wait_ge(*S("small_lo", 2))

            def gate_up(t, gh, gl, uh, ul, b, rows_):
                pe.wait_ge(*S("silu", t))
                mm3(pe, ps[0:rows_, 4, :], gh, gl, xn_hi[:, cut(b)], xn_lo[:, cut(b)], True, True).then_inc(S["gate"], 1)
                pe.wait_ge(*S("gated", t))
                mm3(pe, ps[0:rows_, 5, :], uh, ul, xn_hi[:, cut(b)], xn_lo[:, cut(b)], True, True).then_inc(S["up"], 1)

            def down(t, dh, dl, b, start, stop, rows_):
                pe.wait_ge(*S("h_lo", t + 1))
                mm3(pe, ps[:, b, :], dh, dl, e_hi[0:rows_, b, :], e_lo[0:rows_, b, :], start, stop).then_inc(S["down"], 1)

            def shared_gate_up(t):
                c, b = t // NB, t % NB
                g = slice(S_G + c * I, S_G + (c + 1) * I)
                u = slice(S_U + c * I, S_U + (c + 1) * I)
                gate_up(t, sh[:, g], sl[:, g], sh[:, u], sl[:, u], b, I)

            def shared_down(t):
                c, b = t // NB, t % NB
                down(t, sd_h[:, c, :], sd_l[:, c, :], b, c == 0, False, I)

            def expert_gate_up(i, j):
                c, b = j // NB, j % NB
                t = PER * i + SHARED + j
                if b == 0:
                    pe.wait_ge(*S("w_lo", 4 * i + 2 * c + 1))
                gate_up(t, eh[:, c, 1, :], el[:, c, 1, :], eh[:, c, 2, :], el[:, c, 2, :], b, P)
                pe.wait_ge(*S("weighted", t))
                pe.matmul(ps[:, 6, :], eh[:, c, 3, :], rwt[:, cut(b)], start=True, stop=True).then_inc(S["spread"], 1)

            def expert_down(i, j, stop):
                c, b = j // NB, j % NB
                if b == 0:
                    pe.wait_ge(*S("w_lo", 4 * i + 2 * c + 2))
                down(PER * i + SHARED + j, eh[:, c, 0, :], el[:, c, 0, :], b, False, stop, P)

            for t in range(SHARED):
                shared_gate_up(t)
                if t >= 2:
                    shared_down(t - 2)
            shared_down(SHARED - 2)
            shared_down(SHARED - 1)
            pe.wait_ge(*S("routed", 2))
            for g in range(4):
                pe.wait_ge(*S("rwt", g))
                for t in range(4):
                    last = pe.transpose(ps[:, 6, t * P:(t + 1) * P],
                                        rw_cat[:, 4 * g + t, :, :].rearrange("p a e -> p (a e)"), ident)
                last.then_inc(S["rw_t"], 1)
            pe.wait_ge(*S("rwt", 4))
            expert_gate_up(0, 0)
            expert_gate_up(0, 1)
            with pe.Fori(0, PAIRS - 1) as i:
                for j in range(PER):
                    expert_gate_up(i + (j + 2) // PER, (j + 2) % PER)
                    expert_down(i, j, False)
            for j in range(PER):
                if j + 2 < PER:
                    expert_gate_up(PAIRS - 1, j + 2)
                expert_down(PAIRS - 1, j, j >= NB)

        def moe_act(act, S):
            act.wait_ge(*S("small_in", 32))
            act.activation(sh[:, :], s_raw[:, :], ACT.Identity).then_inc(S["small_hi"], 1)
            act.activation(sd_h[:, :, :], sd_raw[:, :, :], ACT.Identity).then_inc(S["small_hi"], 1)

        def moe_act_tiles(act, S):
            for half in range(2):
                act.wait_ge(*S("logits", half + 1))
                act.activation(r_s[:, 8 * half:8 * half + 8, :].rearrange("p t e -> p (t e)"), ps[:, 6 + half, :], ACT.Sigmoid)\
                    .then_inc(S["scores"], 1)

            def gate_up_high(i, c, read):
                act.wait_ge(*S(f"raw_in{c}", 32 * i + 32))
                act.wait_ge(*S("spread", read))
                act.activation(eh[:, c, 1:4, :], e_raw[:, c, 1:4, :], ACT.Identity).then_inc(S["w_hi"], 1)

            def down_high(i, c, read):
                act.wait_ge(*S("down", read))
                act.activation(eh[:, c, 0, :], e_raw[:, c, 0, :], ACT.Identity).then_inc(S["w_hi"], 1)

            def silu(t, buf, rows_):
                act.wait_ge(*S("gate", t + 1))
                if not (isinstance(t, int) and t < 4):
                    act.wait_ge(*S("gated", t - 3))
                act.activation(e_s[0:rows_, buf, :], ps[0:rows_, 4, :], ACT.Silu).then_inc(S["silu"], 1)

            def high(t, buf, rows_):
                act.wait_ge(*S("weighted", t + 1))
                if not (isinstance(t, int) and t < 4):
                    act.wait_ge(*S("down", t - 3))
                split_hi(act, e_hi[0:rows_, buf, :], e_h[0:rows_, buf, :]).then_inc(S["h_hi"], 1)

            gate_up_high(0, 0, 0)
            down_high(0, 0, 0)
            for t in range(SHARED):
                silu(t, t % 4, I)
                if t:
                    high(t - 1, (t - 1) % 4, I)
            high(SHARED - 1, 3, I)
            for g in range(4):
                act.wait_ge(*S("rw_t", g + 1))
                act.activation(rwt[:, cut(g)], ps[:, 6, :], ACT.Identity).then_inc(S["rwt"], 1)

            def pair(i, last):
                for j in range(PER):
                    t = PER * i + SHARED + j
                    silu(t, j % 4, P)
                    if j:
                        high(t - 1, (j - 1) % 4, P)
                    if j == 0:
                        gate_up_high(i, 1, PER * i)
                    if j == 2:
                        down_high(i, 1, PER * i + SHARED)
                    if j == 4 and not last:
                        gate_up_high(i + 1, 0, PER * i + 4)
                    if j == 6 and not last:
                        down_high(i + 1, 0, PER * i + SHARED + 4)
                high(PER * i + SHARED + PER - 1, 3, P)

            with act.Fori(0, PAIRS - 1) as i:
                pair(i, False)
            pair(PAIRS - 1, True)

        def moe_pool(pool, S):
            pool.wait_ge(*S("small_hi", 1))
            split_lo(pool, sl[:, :], s_raw[:, :], sh[:, :]).then_inc(S["small_lo"], 1)
            pool.wait_ge(*S("small_hi", 2))
            split_lo(pool, sd_l[:, :, :], sd_raw[:, :, :], sd_h[:, :, :]).then_inc(S["small_lo"], 1)

        def moe_pool_tiles(pool, S):
            def gate_up_low(i, c):
                pool.wait_ge(*S("w_hi", 4 * i + 2 * c + 1))
                split_lo(pool, el[:, c, 1:3, :], e_raw[:, c, 1:3, :], eh[:, c, 1:3, :]).then_inc(S["w_lo"], 1)

            def down_low(i, c):
                pool.wait_ge(*S("w_hi", 4 * i + 2 * c + 2))
                split_lo(pool, el[:, c, 0, :], e_raw[:, c, 0, :], eh[:, c, 0, :]).then_inc(S["w_lo"], 1)

            def low(t, buf, rows_):
                pool.wait_ge(*S("h_hi", t + 1))
                split_lo(pool, e_lo[0:rows_, buf, :], e_h[0:rows_, buf, :], e_hi[0:rows_, buf, :]).then_inc(S["h_lo"], 1)

            gate_up_low(0, 0)
            down_low(0, 0)
            for t in range(SHARED):
                low(t, t % 4, I)

            def pair(i, last):
                for j in range(PER):
                    if j == 0:
                        gate_up_low(i, 1)
                    if j == 2:
                        down_low(i, 1)
                    if j == 4 and not last:
                        gate_up_low(i + 1, 0)
                    if j == 6 and not last:
                        down_low(i + 1, 0)
                    low(PER * i + SHARED + j, j % 4, P)

            with pool.Fori(0, PAIRS - 1) as i:
                pair(i, False)
            pair(PAIRS - 1, True)

        def moe_dve(dve, S):
            steps = [0]

            def step(ins):
                steps[0] += 1
                ins.then_inc(S["route"], 1)
                dve.wait_ge(*S("route", steps[0]))

            NGT = NTT * NG
            small = [r_small[:, k, :] for k in range(4)]

            def pairs_of(tile, lo, n):
                v = tile[:, lo:lo + NGT * n].rearrange("p (g k) -> p g k", k=n)
                return v[:, :, 0:n // 2], v[:, :, n // 2:n]

            def out_of(tile, lo, n):
                return tile[:, lo:lo + NGT * n].rearrange("p (g k) -> p g k", k=n)

            dve.wait_ge(*S("scores", 2))
            bias = rows[:, R_GB:R_GB + E].unsqueeze(1).broadcast_to([P, NTT, E])
            step(dve.tensor_tensor(r_c[:, :, :], r_s[:, :, :], bias, ALU.add))
            c8 = r_c[:, :, :].rearrange("p t (g k) -> p (t g) k", k=8)
            a, b = c8[:, :, 0:4], c8[:, :, 4:8]
            step(dve.tensor_tensor(out_of(r_t, 0, 4), a, b, ALU.max))
            step(dve.tensor_tensor(out_of(r_u, 0, 4), a, b, ALU.min))
            a, b = pairs_of(r_t, 0, 4)
            ma, mb = pairs_of(r_u, 0, 4)
            step(dve.tensor_tensor(out_of(r_u, 512, 2), a, b, ALU.min))
            step(dve.tensor_tensor(out_of(r_t, 512, 2), a, b, ALU.max))
            step(dve.tensor_tensor(out_of(r_t, 768, 2), ma, mb, ALU.max))
            step(dve.tensor_tensor(out_of(r_u, 768, 2), out_of(r_u, 512, 2), out_of(r_t, 768, 2), ALU.max))
            a, b = pairs_of(r_t, 512, 2)
            ma, mb = pairs_of(r_u, 768, 2)
            one = [s_.unsqueeze(2) for s_ in small]
            step(dve.tensor_tensor(one[0], a, b, ALU.max))
            step(dve.tensor_tensor(one[1], a, b, ALU.min))
            step(dve.tensor_tensor(one[2], ma, mb, ALU.max))
            step(dve.tensor_tensor(small[1], small[1], small[2], ALU.max))
            step(dve.tensor_tensor(small[0], small[0], small[1], ALU.add))
            g3 = small[0].rearrange("p (t g) -> p t g", g=NG)
            other = g3.unsqueeze(2).broadcast_to([P, NTT, NG, NG])
            own = g3.unsqueeze(3).broadcast_to([P, NTT, NG, NG])
            t4 = r_t[:, :].rearrange("p (t g k) -> p t g k", g=NG, k=NG)
            u4 = r_u[:, :].rearrange("p (t g k) -> p t g k", g=NG, k=NG)
            tie = const[:, K_TIE:K_TIE + E].unsqueeze(1).broadcast_to([P, NTT, E])
            t3 = r_t[:, :].rearrange("p (t e) -> p t e", e=E)
            u3 = r_u[:, :].rearrange("p (t e) -> p t e", e=E)
            step(dve.tensor_tensor(t4, other, own, ALU.is_gt))
            step(dve.tensor_tensor(u4, other, own, ALU.is_equal))
            step(dve.tensor_tensor(u3, u3, tie, ALU.mult))
            step(dve.tensor_tensor(r_t[:, :], r_t[:, :], r_u[:, :], ALU.add))
            step(dve.tensor_reduce(small[1], out_of(r_t, 0, 8), AX, ALU.add))
            step(dve.tensor_scalar(small[1], small[1], 4.0, None, ALU.is_lt))
            step(dve.tensor_tensor(c8, c8, small[1].unsqueeze(2).broadcast_to([P, NGT, 8]), ALU.mult))
            for t in range(NTT):
                ins = dve.max(small[2][:, t * 8:t * 8 + 8], r_c[:, t, :])
                if t == NTT - 1:
                    step(ins)
            for t in range(NTT):
                ins = dve.match_replace(t3[:, t, :], small[2][:, t * 8:t * 8 + 8], r_c[:, t, :], GONE)
                if t == NTT - 1:
                    step(ins)
            step(dve.scalar_tensor_tensor(u3, t3, GONE, r_s[:, :, :], ALU.is_equal, ALU.mult))
            total = small[3][:, 0:NTT]
            step(dve.tensor_reduce(total, u3, AX, ALU.add))
            step(dve.tensor_scalar(total, total, 1e-20, None, ALU.add))
            step(dve.reciprocal(total, total))
            step(dve.scalar_tensor_tensor(t3, u3, 2.5, total.unsqueeze(2).broadcast_to([P, NTT, E]), ALU.mult, ALU.mult))
            dve.tensor_copy(rw_cat[:, :, 0, :].bitcast(F32R), t3).then_inc(S["routed"], 1)
            dve.wait_ge(*S("routed", 1))
            dve.tensor_tensor(rw_cat[:, :, 1, :].bitcast(F32R), t3, rw_cat[:, :, 0, :], ALU.subtract).then_inc(S["routed"], 1)

            assert steps[0] == ROUTE_STEPS

            def gate(t, buf, rows_):
                dve.wait_ge(*S("up", t + 1))
                dve.wait_ge(*S("silu", t + 1))
                if not (isinstance(t, int) and t < 2):
                    dve.wait_ge(*S("weighted", t - 1))
                dve.tensor_tensor(e_p[0:rows_, buf % 2, :], e_s[0:rows_, buf, :], ps[0:rows_, 5, :], ALU.mult).then_inc(S["gated"], 1)
                dve.wait_ge(*S("gated", t + 1))
                if not (isinstance(t, int) and t < 4):
                    dve.wait_ge(*S("h_lo", t - 3))

            for t in range(SHARED):
                gate(t, t % 4, I)
                dve.tensor_copy(e_h[0:I, t % 4, :], e_p[0:I, t % 2, :]).then_inc(S["weighted"], 1)
            with dve.Fori(0, PAIRS) as i:
                for j in range(PER):
                    t = PER * i + SHARED + j
                    gate(t, j % 4, P)
                    dve.wait_ge(*S("spread", PER * i + j + 1))
                    dve.tensor_tensor(e_h[:, j % 4, :], e_p[:, j % 2, :], ps[:, 6, :], ALU.mult).then_inc(S["weighted"], 1)
            for b in range(NB):
                dve.wait_ge(*S("down", SHARED + PER * (PAIRS - 1) + NB + b + 1))
                dve.scalar_tensor_tensor(x[:, cut(b)], ps[:, b, :], 0.5, x[:, cut(b)], ALU.mult, ALU.add).then_inc(S["x_new"], 1)

        def moe_load_small(sp, S):
            sp.dma_start(s_raw[:, :], d["l1_small"]).then_inc(S["small_in"], 16)
            sp.dma_start(sd_raw[:, :, :], d["sd"]).then_inc(S["small_in"], 16)

        def moe_load(sp, S):
            def chunk(i, c):
                sp.dma_start(e_raw[:, c, 0:3, :], d["experts"][bass.ds(2 * i + c, 1)].rearrange("a p k n -> p (a k) n"))\
                    .then_inc(S[f"raw_in{c}"], 16)
                sp.dma_start(e_raw[:, c, 3, :], d["pick"][bass.ds(2 * i + c, 1)].rearrange("a p n -> p (a n)"))\
                    .then_inc(S[f"raw_in{c}"], 16)

            chunk(0, 0)
            chunk(0, 1)
            with sp.Fori(0, PAIRS - 1) as i:
                for c in range(2):
                    sp.wait_ge(*S("w_lo", 4 * i + 2 * c + 2))
                    chunk(i + 1, c)

        SCALE = float(P) ** -0.5
        S_AT = {0: (1, 384), 1: (2, 0), 2: (1, 0), 3: (0, 0)}
        PT_AT = {0: (3, 0), 1: (4, 0), 2: (2, 256), 3: (4, 384)}

        def scores_at(r):
            bank, lo = S_AT[r]
            return ps[:, bank, lo:lo + P * (r + 1)]

        S_BANKS = ((3,), (2, 0), (1,))
        PT_UNITS = ((3, 0, T), (4, 0, T), (2, 256, 256))
        PT_PART = {0: (0, 0), 1: (1, 0), 2: (2, 0), 3: (1, 384)}

        def pt_psum(unit):
            bank, lo, n = PT_UNITS[unit]
            return ps[:, bank, lo:lo + n]

        def pt_at(kb):
            bank, lo = PT_AT[kb]
            return ps[:, bank, lo:lo + T - P * kb]

        def att_pe(pe, L):
            def q_proj(i, h):
                pe.wait_ge(*A("q32", 8 * i + h))
                w = slice(A_Q + h * P, A_Q + (h + 1) * P)
                mm3(pe, ps[:, 5, :], ah[:, w], al[:, w], xb_hi[:, :], xb_lo[:, :], True, True).then_inc(A["qp"], 1)

            def score(i, h):
                pe.wait_ge(*A("q_lo", 8 * i + h + 1))
                pe.wait_ge(*A("p", 4 * (8 * i + h)))
                for bank, tiles in enumerate(S_BANKS):
                    if bank == 2:
                        pe.wait_ge(*A("pt_lo", 3 * (8 * i + h)))
                    for r in tiles:
                        n = P * (r + 1)
                        q = slice(r * P, n)
                        out = scores_at(r)
                        pe.matmul(out, q_hi[:, h % 2, q], k_hi[:, 0:n], start=True, stop=False, skip_group_check=True)
                        pe.matmul(out, q_hi[:, h % 2, q], k_lo[:, 0:n], start=False, stop=False, skip_group_check=True)
                        pe.matmul(out, q_lo[:, h % 2, q], k_hi[:, 0:n], start=False, stop=False, skip_group_check=True)
                        last = pe.matmul(out[:, r * P:n], idr[:, :], maskr[:, :], start=False, stop=True, skip_group_check=True)
                    last.then_inc(A["s"], 1)

            def turn(i, h):
                pe.wait_ge(*A("pn", 4 * (8 * i + h) + 4))
                pe.wait_ge(*A("pt_lo", 3 * (8 * i + h)))
                for tiles in ((0,), (1, 3), (2,)):
                    for kb in tiles:
                        for r in range(kb, 4):
                            last = pe.transpose(pt_at(kb)[:, (r - kb) * P:(r - kb + 1) * P], p32[:, r, kb * P:(kb + 1) * P], ident)
                    last.then_inc(A["pt"], 1)

            def values(i, h):
                pe.wait_ge(*A("o_lo", 8 * i + h))
                for kb in range(4):
                    unit, lo = PT_PART[kb]
                    if kb < 3:
                        pe.wait_ge(*A("pt_lo", 3 * (8 * i + h) + kb + 1))
                    n = T - kb * P
                    last = mm3(pe, ps[:, 6, kb * P:T], v_hi[:, kb, :], v_lo[:, kb, :], pt_hi[:, unit, lo:lo + n],
                               pt_lo[:, unit, lo:lo + n], kb == 0, kb == 3)
                last.then_inc(A["o"], 1)

            def out_proj(i, h):
                pe.wait_ge(*A("o_lo", 8 * i + h + 1))
                if h == 0:
                    pe.wait_ge(*A("x_new", i))
                w = slice(A_O + h * P, A_O + (h + 1) * P)
                mm3(pe, ps[:, 7, :], ah[:, w], al[:, w], o_hi[:, h % 2, :], o_lo[:, h % 2, :], h == 0, h == HEADS - 1)\
                    .then_inc(A["y"], 1)

            pe.wait_ge(*A("mask", 2))
            pe.wait_ge(a_lo, 1)
            banks_free(pe, L)
            with pe.Fori(0, NB) as i:
                pe.wait_ge(*A("xb_lo", i + 1))
                pe.wait_ge(*A("q32", 8 * i))
                pe.wait_ge(*A("o_lo", 8 * i))
                w = slice(A_K, A_K + P)
                mm3(pe, ps[:, 5, :], ah[:, w], al[:, w], xb_hi[:, :], xb_lo[:, :], True, True).then_inc(A["kv"], 1)
                w = slice(A_V, A_V + P)
                for t in range(4):
                    tt = slice(t * P, (t + 1) * P)
                    out = ps[:, 6, tt]
                    pe.matmul(out, xb_hi[:, tt], ah[:, w], start=True, stop=False, skip_group_check=True)
                    pe.matmul(out, xb_hi[:, tt], al[:, w], start=False, stop=False, skip_group_check=True)
                    last = pe.matmul(out, xb_lo[:, tt], ah[:, w], start=False, stop=True, skip_group_check=True)
                last.then_inc(A["kv"], 1)
                pe.wait_ge(*A("k32", i + 1))
                q_proj(i, 0)
                pe.wait_ge(*A("k_lo", i + 1))
                pe.wait_ge(*A("v_lo", i + 1))
                score(i, 0)
                for h in range(HEADS):
                    if h + 1 < HEADS:
                        q_proj(i, h + 1)
                    turn(i, h)
                    if h + 1 < HEADS:
                        score(i, h + 1)
                    if h:
                        out_proj(i, h - 1)
                    values(i, h)
                out_proj(i, HEADS - 1)

        def att_act(act):
            with act.Fori(0, NB) as i:
                def q_high(h):
                    act.wait_ge(*A("q32", 8 * i + h + 1))
                    act.wait_ge(*A("s", 3 * (8 * i + (h - 1 if h >= 2 else 0))))
                    split_hi(act, q_hi[:, h % 2, :], q32[:, h % 2, :]).then_inc(A["q_hi"], 1)

                def probs(h):
                    act.wait_ge(*A("nmx", 8 * i + h + 1))
                    act.wait_ge(*A("pt", 3 * (8 * i + h)))
                    for r in (3, 2, 0, 1):
                        act.activation(p32[:, r, 0:P * (r + 1)], scores_at(r), ACT.Exp, scale=SCALE, bias=st[:, h % 2, 1, r:r + 1],
                                       accum_out=st[:, h % 2, 2, r:r + 1]).then_inc(A["p"], 1)

                def o_high(h):
                    act.wait_ge(*A("o", 8 * i + h + 1))
                    act.wait_ge(*A("y", 8 * i + (h - 1 if h >= 2 else 0)))
                    act.activation(o_hi[:, h % 2, :], ps[:, 6, :], ACT.Identity).then_inc(A["o_hi"], 1)

                act.wait_ge(*A("k32", i + 1))
                split_hi(act, k_hi[:, :], kv32[:, 0, :]).then_inc(A["k_hi"], 1)
                act.wait_ge(*A("v32", i + 1))
                act.activation(v_hi[:, :, :].rearrange("p t n -> p (t n)"), kv32[:, 1, :], ACT.Identity).then_inc(A["v_hi"], 1)
                q_high(0)
                probs(0)
                for h in range(HEADS):
                    if h:
                        o_high(h - 1)
                    if h + 1 < HEADS:
                        q_high(h + 1)
                    for unit, (_, _, n) in enumerate(PT_UNITS):
                        act.wait_ge(*A("pt", 3 * (8 * i + h) + unit + 1))
                        act.wait_ge(*A("o", 8 * i + h))
                        act.activation(pt_hi[:, unit, 0:n], pt_psum(unit), ACT.Identity).then_inc(A["pt_hi"], 1)
                    if h + 1 < HEADS:
                        probs(h + 1)
                o_high(HEADS - 1)

        def att_dve(dve, L):
            dve.tensor_copy(idr[:, :], ident).then_inc(A["mask"], 1)
            dve.tensor_copy(maskr[:, :], const[:, K_MASK:K_MASK + P]).then_inc(A["mask"], 1)
            pe_t = const[:, K_PE:K_PE + T]
            with dve.Fori(0, NB) as i:
                blk = bass.ds(i * T, T)

                def q_full(h):
                    dve.wait_ge(*A("qp", 8 * i + h + 1))
                    dve.wait_ge(*A("q_lo", 8 * i + (h - 1 if h >= 2 else 0)))
                    dve.scalar_tensor_tensor(q32[:, h % 2, :], ps[:, 5, :], cols[:, C_BQ + h:C_BQ + h + 1], pe_t,
                                             ALU.add, ALU.add).then_inc(A["q32"], 1)

                def maxima(h):
                    for r in (3, 2, 0, 1):
                        dve.wait_ge(*A("s", 3 * (8 * i + h) + {3: 1, 2: 2, 0: 2, 1: 3}[r]))
                        dve.tensor_reduce(st[:, h % 2, 0, r:r + 1], scores_at(r), AX, ALU.max).then_inc(A["mx"], 1)
                    dve.wait_ge(*A("mx", 4 * (8 * i + h) + 4))
                    dve.tensor_scalar(st[:, h % 2, 1, :], st[:, h % 2, 0, :], -SCALE, None, ALU.mult).then_inc(A["nmx"], 1)

                def o_low(h):
                    dve.wait_ge(*A("o_hi", 8 * i + h + 1))
                    split_lo(dve, o_lo[:, h % 2, :], ps[:, 6, :], o_hi[:, h % 2, :]).then_inc(A["o_lo"], 1)

                dve.wait_ge(*L("xn_lo", NB))
                dve.wait_ge(*A("qp", 8 * i))
                dve.tensor_copy(xb_hi[:, :], xn_hi[:, blk].bitcast(F32)).then_inc(A["xb_hi"], 1)
                dve.wait_ge(*A("xb_hi", i + 1))
                dve.tensor_copy(xb_lo[:, :], xn_lo[:, blk].bitcast(F32)).then_inc(A["xb_lo"], 1)
                dve.wait_ge(*A("kv", 2 * i + 1))
                dve.scalar_tensor_tensor(kv32[:, 0, :], ps[:, 5, :], cols[:, C_BK:C_BK + 1], pe_t, ALU.add, ALU.add).then_inc(A["k32"], 1)
                dve.wait_ge(*A("kv", 2 * i + 2))
                dve.tensor_tensor(kv32[:, 1, :].rearrange("p (t n) -> p t n", t=4), ps[:, 6, :].rearrange("p (t n) -> p t n", t=4),
                                  rows[:, R_BV:R_BV + P].unsqueeze(1).broadcast_to([P, 4, P]), ALU.add).then_inc(A["v32"], 1)
                q_full(0)
                maxima(0)
                for h in range(HEADS):
                    if h:
                        o_low(h - 1)
                    if h + 1 < HEADS:
                        q_full(h + 1)
                    dve.wait_ge(*A("p", 4 * (8 * i + h) + 4))
                    dve.reciprocal(st[:, h % 2, 3, :], st[:, h % 2, 2, :]).then_inc(A["inv"], 1)
                    dve.wait_ge(*A("inv", 8 * i + h + 1))
                    for r in range(4):
                        n = P * (r + 1)
                        dve.tensor_scalar(p32[:, r, 0:n], p32[:, r, 0:n], st[:, h % 2, 3, r:r + 1], None, ALU.mult).then_inc(A["pn"], 1)
                    for unit, (_, _, n) in enumerate(PT_UNITS):
                        dve.wait_ge(*A("pt_hi", 3 * (8 * i + h) + unit + 1))
                        split_lo(dve, pt_lo[:, unit, 0:n], pt_psum(unit), pt_hi[:, unit, 0:n]).then_inc(A["pt_lo"], 1)
                    if h + 1 < HEADS:
                        maxima(h + 1)
                o_low(HEADS - 1)
                dve.wait_ge(*A("y", 8 * i + 8))
                dve.tensor_tensor(x[:, blk], x[:, blk], ps[:, 7, :], ALU.add).then_inc(A["x_new"], 1)

        def att_pool(pool):
            with pool.Fori(0, NB) as i:
                pool.wait_ge(*A("k_hi", i + 1))
                split_lo(pool, k_lo[:, :], kv32[:, 0, :], k_hi[:, :]).then_inc(A["k_lo"], 1)
                pool.wait_ge(*A("v_hi", i + 1))
                split_lo(pool, v_lo[:, :, :].rearrange("p t n -> p (t n)"), kv32[:, 1, :],
                         v_hi[:, :, :].rearrange("p t n -> p (t n)")).then_inc(A["v_lo"], 1)
                for h in range(HEADS):
                    pool.wait_ge(*A("q_hi", 8 * i + h + 1))
                    split_lo(pool, q_lo[:, h % 2, :], q32[:, h % 2, :], q_hi[:, h % 2, :]).then_inc(A["q_lo"], 1)

        FFN_CUTS = (W_G, W_H1, W_H2, NW)

        @block.sync
        def _(sp):
            sp.dma_start(x[:, 0:T], d["x"][:, 0:T]).then_inc(loaded, 16)
            sp.dma_start(x[:, T:NT], d["x"][:, T:NT]).then_inc(loaded, 16)
            sp.dma_start(cols[:, :], d["cols"]).then_inc(loaded, 16)
            for k in range(3):
                w = slice(FFN_CUTS[k], FFN_CUTS[k + 1])
                sp.dma_start(w_raw[:, w], d["ffn"][:, w]).then_inc(ffn_in[k], 16)
            sp.dma_start(const[:, :], d["const"]).then_inc(loaded, 16)
            sp.dma_start(rows[:, :], d["rows"]).then_inc(loaded, 16)
            sp.wait_ge(primed_all, 1)
            start_phase(sp, 1)
            sp.dma_start(m_raw[:, 0:NM], d["mixer"]).then_inc(M["raw_in"], 16)
            start_phase(sp, 3)
            moe_load_small(sp, E1)
            sp.dma_start(a_raw[:, :], d["attn"]).then_inc(a_in, 16)
            moe_load(sp, E1)
            start_phase(sp, 5)
            moe_load_small(sp, E2)
            moe_load(sp, E2)
            start_phase(sp, 6)
            sp.dma_start(d["out"], x[:, :]).then_inc(stored, 16)
            sp.wait_ge(stored, 16)

        @block.tensor
        def _(pe):
            pe.wait_ge(primed_all, 1)
            pe.wait_ge(ones_set, 1)
            pe.wait_ge(loaded, 80)
            ln_pe(pe, LN[0])
            pe.wait_ge(w_split, 4)
            ffn_pe(pe, F1, LN[0])
            end_phase(pe)
            start_phase(pe, 1)
            ln_pe(pe, LN[1])
            mix_pe(pe, LN[1])
            end_phase(pe)
            start_phase(pe, 2)
            ln_pe(pe, LN[2])
            ffn_pe(pe, F2, LN[2])
            end_phase(pe)
            start_phase(pe, 3)
            ln_pe(pe, LN[3])
            moe_pe(pe, E1, LN[3])
            end_phase(pe)
            start_phase(pe, 4)
            ln_pe(pe, LN[4])
            att_pe(pe, LN[4])
            end_phase(pe)
            start_phase(pe, 5)
            ln_pe(pe, LN[5])
            moe_pe(pe, E2, LN[5])
            end_phase(pe)

        @block.scalar
        def _(act):
            act.wait_ge(primed_all, 1)
            act.wait_ge(loaded, 80)
            act.wait_ge(ones_set, 3)
            ln_act(act, LN[0])
            act.wait_ge(ffn_in[2], 16)
            split_hi(act, wh[:, W_H2:NW], w_raw[:, W_H2:NW]).then_inc(w_hi_c, 1)
            ffn_act(act, F1)
            end_phase(act)
            start_phase(act, 1)
            act.wait_ge(*M("raw_in", 16))
            split_hi(act, mh[:, :], m_raw[:, 0:NM]).then_inc(M["w_hi"], 1)
            ln_act(act, LN[1])
            mix_act(act)
            end_phase(act)
            start_phase(act, 2)
            ln_act(act, LN[2])
            ffn_act(act, F2)
            end_phase(act)
            start_phase(act, 3)
            moe_act(act, E1)
            ln_act(act, LN[3])
            act.wait_ge(a_in, 16)
            split_hi(act, ah[:, :], a_raw[:, :]).then_inc(a_hi, 1)
            moe_act_tiles(act, E1)
            end_phase(act)
            start_phase(act, 4)
            ln_act(act, LN[4])
            att_act(act)
            end_phase(act)
            start_phase(act, 5)
            moe_act(act, E2)
            ln_act(act, LN[5])
            moe_act_tiles(act, E2)
            end_phase(act)

        @block.vector
        def _(dve):
            dve.wait_ge(primed_all, 1)
            dve.memset(mean_w[:, :], 1.0 / P).then_inc(ones_set, 1)
            dve.wait_ge(loaded, 80)
            dve.tensor_scalar(w3_half[:, :], cols[:, C_W3:C_W3 + 1], 0.5, None, ALU.mult).then_inc(ones_set, 1)
            dve.memset(cols[:, C_EPS:C_EPS + 1], EPS).then_inc(ones_set, 1)
            dve.wait_ge(ones_set, 3)
            for k in range(2):
                w = slice(FFN_CUTS[k], FFN_CUTS[k + 1])
                dve.wait_ge(ffn_in[k], 16)
                dve.tensor_copy(wh[:, w], w_raw[:, w]).then_inc(w_split, 1)
                dve.wait_ge(w_split, 2 * k + 1)
                split_lo(dve, wl[:, w], w_raw[:, w], wh[:, w]).then_inc(w_split, 1)
            ln_dve(dve, LN[0])
            ffn_dve(dve, F1)
            end_phase(dve)
            start_phase(dve, 1)
            ln_dve(dve, LN[1])
            mix_dve(dve)
            end_phase(dve)
            start_phase(dve, 2)
            ln_dve(dve, LN[2])
            ffn_dve(dve, F2)
            end_phase(dve)
            start_phase(dve, 3)
            ln_dve(dve, LN[3])
            moe_dve(dve, E1)
            end_phase(dve)
            start_phase(dve, 4)
            ln_dve(dve, LN[4])
            att_dve(dve, LN[4])
            end_phase(dve)
            start_phase(dve, 5)
            ln_dve(dve, LN[5])
            moe_dve(dve, E2)
            end_phase(dve)

        @block.gpsimd
        def _(pool):
            for signal in primed:
                pool.sem_inc(signal, 1)
            pool.sem_inc(primed_all, 1)
            ln_pool(pool, LN[0])
            pool.wait_ge(w_hi_c, 1)
            split_lo(pool, wl[:, W_H2:NW], w_raw[:, W_H2:NW], wh[:, W_H2:NW]).then_inc(w_split_c, 1)
            end_phase(pool)
            start_phase(pool, 1)
            pool.memset(bc[4 * DS:P, :].bitcast(F32), 0.0).then_inc(M["bc_zero"], 1)
            pool.wait_ge(*M("bc_zero", 1))
            pool.wait_ge(*M("w_hi", 1))
            split_lo(pool, ml[:, :], m_raw[:, 0:NM], mh[:, :]).then_inc(M["w_lo"], 1)
            ln_pool(pool, LN[1])
            mix_pool(pool)
            end_phase(pool)
            start_phase(pool, 2)
            ln_pool(pool, LN[2])
            end_phase(pool)
            start_phase(pool, 3)
            moe_pool(pool, E1)
            ln_pool(pool, LN[3])
            pool.wait_ge(a_hi, 1)
            split_lo(pool, al[:, :], a_raw[:, :], ah[:, :]).then_inc(a_lo, 1)
            moe_pool_tiles(pool, E1)
            end_phase(pool)
            start_phase(pool, 4)
            ln_pool(pool, LN[4])
            att_pool(pool)
            end_phase(pool)
            start_phase(pool, 5)
            moe_pool(pool, E2)
            ln_pool(pool, LN[5])
            moe_pool_tiles(pool, E2)
            end_phase(pool)


def constants():
    k = np.zeros((P, NCONST), np.float32)
    p = np.arange(P)
    k[:, K_ID:K_ID + P] = np.eye(P)
    k[:, K_MASK:K_MASK + P] = np.where(p[None, :] > p[:, None], NEG, 0.0)
    inv_freq = np.exp(np.float32(-np.log(10000.0)) * np.arange(0, P, 2, dtype=np.float32) / np.float32(P))
    ang = np.arange(T, dtype=np.float32)[:, None] * inv_freq.astype(np.float32)[None, :]
    k[0::2, K_PE:K_PE + T] = np.sin(ang).T
    k[1::2, K_PE:K_PE + T] = np.cos(ang).T
    g = np.arange(NG)
    k[:, K_TIE:K_TIE + E] = (g[None, :] < g[:, None]).reshape(-1)
    k[:2 * 2 * DS, K_ID32:K_ID32 + 2 * DS] = p[:2 * 2 * DS, None] % 32 == np.arange(2 * DS)[None, :]
    expert = np.arange(E * I) // I
    pick = (p[:, None] % E == expert[None, :]).astype(np.float32)
    return k, np.ascontiguousarray(pick.reshape(P, CH, P).transpose(1, 0, 2))


def kernel(**a):
    import concourse.bacc as bacc
    from concourse.bass_utils import run_bass_kernel_spmd

    a = {k: np.asarray(v) for k, v in a.items()}
    f, m, t, r = "L0_ffn_", "L0_attn_", "L1_attn_", "L1_ffn_"

    def chunks(w):
        return w.reshape(-1, P, w.shape[-1]).transpose(1, 0, 2).reshape(P, -1)

    def column(v):
        return v.reshape(-1, P).T

    arrays = {
        "x": a[m + "x"].reshape(NT, P).T,
        "ffn": np.concatenate([a[f + "w1_w"].T, a[f + "w2_w"].T, chunks(a[f + "h1_w"].T), chunks(a[f + "h2_w"].T),
                               chunks(a[f + "w3_w"].T)], axis=1),
        "mixer": np.concatenate([a[m + "in_proj_w"].T, chunks(a[m + "x_proj_w"].T), chunks(a[m + "out_proj_w"].T)], axis=1),
        "attn": np.concatenate([a[t + "Wq"], a[t + "Wkv"], chunks(a[t + "Wo"])], axis=1),
        "l1_small": np.concatenate([a[r + "gate_w"].T, a[r + "Sg"].T, a[r + "Su"].T], axis=1),
        "sd": a[r + "Sd"].T.reshape(2, I, P).transpose(1, 0, 2),
        "experts": np.stack([a[r + "Wd"].transpose(0, 2, 1).reshape(CH, P, P),
                             a[r + "Wg"].reshape(CH, P, P).transpose(0, 2, 1),
                             a[r + "Wu"].reshape(CH, P, P).transpose(0, 2, 1)], axis=2),
        "cols": np.concatenate(
            [column(a[f + n]) for n in ("w1_s", "w2_s", "h1_s", "h2_s", "w3_s")]
            + [a[m + "conv_w"].reshape(MC, P, 4).transpose(1, 0, 2).reshape(P, -1), column(a[m + "conv_b"]),
               column(a[m + "dt_proj_w"].reshape(-1)), column(a[m + "dt_proj_b"]), column(a[m + "D"]),
               a[m + "A_log"].reshape(MC, P, DS).transpose(1, 0, 2).reshape(P, -1),
               column(a[t + "bq"]), column(a[t + "bkv"][:P]), np.zeros((P, 1), np.float32)], axis=1),
        "rows": np.concatenate([np.broadcast_to(a[r + "gate_bias"], (P, E)), np.broadcast_to(a[t + "bkv"][P:], (P, P))], axis=1),
    }
    arrays["const"], arrays["pick"] = constants()
    arrays = {f"in_{k}": np.ascontiguousarray(v) for k, v in arrays.items()}

    nc = bacc.Bacc("TRN2", target_bir_lowering=False, num_devices=1)
    d = {k[3:]: nc.dram_tensor(k, v.shape, F32, kind="ExternalInput").ap() for k, v in arrays.items()}
    d["out"] = nc.dram_tensor("out", (P, NT), F32, kind="ExternalOutput").ap()
    program(nc, d)
    got = run_bass_kernel_spmd(nc, [arrays], core_ids=[0]).results[0]["out"]
    return np.ascontiguousarray(got.T).reshape(NB, T, P)
```

```python
from contextlib import ExitStack

import numpy as np

import concourse.bass as bass
from concourse import mybir

P = 128
T = 512
NB = 4
NT = T * NB
HID = 512
HC = HID // P
DS = 16
MC = 2
HEADS = 8
E, I = 64, 88
NG = 8
CH = E * I // P
PAIRS = CH // 2
DU_DVE = 2
NTT = NT // P
EPS = 1e-5
MASKED = 1e30
GONE = -3e38

F32 = mybir.dt.float32
F32R = mybir.dt.float32r
ACT = mybir.ActivationFunctionType
ALU = mybir.AluOpType
AX = mybir.AxisListType.X

C_W1, C_W2, C_H1, C_H2, C_W3 = 0, 4, 8, 12, 16
C_CONV, C_CB, C_DTW, C_DTB, C_D = 17, 25, 27, 29, 31
C_ALOG, C_BQ, C_BK, C_EPS = 33, 65, 73, 74
NCOL = 75
R_GB, R_BV, NROW = 0, 64, 192
K_ID, K_MASK, K_PE, K_TIE, K_ID64, K_ID32, NCONST = 0, 128, 256, 768, 832, 896, 928
W_G, W_U, W_H1, W_H2, W_3, NW = 0, 512, 1024, 3072, 5120, 5632
M_IN, M_X, M_OUT, NM = 0, 512, 578, 834
A_Q, A_K, A_V, A_O, NA = 0, 1024, 1152, 1280, 2304
S_R, S_G, S_U, NS = 0, 64, 240, 416


def program(nc, d):
    ctx = ExitStack()
    with ctx:
        def keeper(stack):
            return lambda name, shape, dt=F32: stack.enter_context(nc.sbuf_tensor(name, shape, dt))

        def sem(name):
            return ctx.enter_context(nc.semaphore(name))

        sb = keeper(ctx)
        x = sb("x", [P, NT])
        with ExitStack() as s:
            m_h = keeper(s)("m_h", [P, 4, T])
            m_hc = keeper(s)("m_hc", [P, 4, T])
        xn_hi = sb("xn_hi", [P, NT], F32R)
        xn_lo = sb("xn_lo", [P, NT], F32R)
        ln_c = sb("ln_c", [P, NT])
        ln_t = sb("ln_t", [P, NT])
        cols = sb("cols", [P, NCOL])
        rows = sb("rows", [P, NROW])
        const = sb("const", [P, NCONST])
        mean_w = sb("mean_w", [P, P])
        rstd = sb("rstd", [P, NTT])
        w3_half = sb("w3_half", [P, 1])
        neg_a = sb("neg_a", [P, MC * DS])

        with ExitStack() as layer:
            lb = keeper(layer)
            wh, wl = lb("wh", [P, NW], F32R), lb("wl", [P, NW], F32R)
            with ExitStack() as s:
                fb = keeper(s)
                w_raw = fb("w_raw", [P, NW])
                f_s = fb("f_s", [P, HC, T])
                f_h = fb("f_h", [P, HC, T])
                hid_hi = fb("hid_hi", [P, 3, HC, T], F32R)
                hid_lo = fb("hid_lo", [P, 3, HC, T], F32R)
            with ExitStack() as s:
                fb = keeper(s)
                m_raw = fb("m_raw", [P, 2 * T])
                dt_b = m_raw[:, :].rearrange("p (m t) -> p m t", m=MC)
                mh, ml = fb("mh", [P, NM], F32R), fb("ml", [P, NM], F32R)
                dtw_hi = fb("dtw_hi", [P, MC, P], F32R)
                dtw_lo = fb("dtw_lo", [P, MC, P], F32R)
                sel_bc = fb("sel_bc", [P, 2 * DS, P], F32R)
                bc = fb("bc", [P, NT], F32R)
                xc = fb("xc", [P, MC, NT])
                sz = fb("sz", [P, MC, NT])
                dt = fb("dt", [P, MC, NT])
                du = fb("du", [P, MC, NT])
                g_hi = fb("g_hi", [P, MC, T], F32R)
                g_lo = fb("g_lo", [P, MC, T], F32R)
                m_y = fb("m_y", [P, MC, T])
                warm = fb("warm", [P, 1])
                m_db = ln_c[:, 0:2 * T].rearrange("p (k t) -> p k t", k=2)
                m_c = ln_c[:, 2 * T:NT].rearrange("p (k t) -> p k t", k=2)
                m_da = ln_t[:, :].rearrange("p (k t) -> p k t", k=4)
        with ExitStack() as layer:
            lb = keeper(layer)
            ah, al = lb("ah", [P, NA], F32R), lb("al", [P, NA], F32R)
            sh, sl = lb("sh", [P, NS], F32R), lb("sl", [P, NS], F32R)
            sd_h, sd_l = lb("sd_h", [I, 2, P], F32R), lb("sd_l", [I, 2, P], F32R)
            with ExitStack() as s:
                fb = keeper(s)
                s_raw = fb("s_raw", [P, NS])
                sd_raw = fb("sd_raw", [I, 2, P])
                a_raw = fb("a_raw", [P, NA])
                e_raw = fb("e_raw", [P, 2, 4, P])
                eh, el = fb("eh", [P, 2, 4, P], F32R), fb("el", [P, 2, 3, P], F32R)
                rwt = fb("rwt", [P, NT], F32R)
                r_s = fb("r_s", [P, NTT, E])
                r_c = fb("r_c", [P, NTT, E])
                r_t = fb("r_t", [P, NTT * E])
                r_u = fb("r_u", [P, NTT * E])
                r_small = fb("r_small", [P, 4, NTT * NG])
                rw_cat = fb("rw_cat", [P, NTT, 2, E])
                e_s = fb("e_s", [P, 4, T])
                e_p = fb("e_p", [P, 2, T])
                e_h = fb("e_h", [P, 4, T])
                e_hi = fb("e_hi", [P, 4, T], F32R)
                e_lo = fb("e_lo", [P, 4, T], F32R)
            with ExitStack() as s:
                fb = keeper(s)
                xb_hi, xb_lo = fb("xb_hi", [P, T], F32R), fb("xb_lo", [P, T], F32R)
                k_hi, k_lo = fb("k_hi", [P, T], F32R), fb("k_lo", [P, T], F32R)
                v_hi, v_lo = fb("v_hi", [P, 4, P], F32R), fb("v_lo", [P, 4, P], F32R)
                kv32 = fb("kv32", [P, 2, T])
                q32 = fb("q32", [P, 2, T])
                q_hi, q_lo = fb("q_hi", [P, 2, T], F32R), fb("q_lo", [P, 2, T], F32R)
                p32 = fb("p32", [P, 4, T])
                pt_hi, pt_lo = fb("pt_hi", [P, 3, T], F32R), fb("pt_lo", [P, 3, T], F32R)
                o_hi, o_lo = fb("o_hi", [P, 2, T], F32R), fb("o_lo", [P, 2, T], F32R)
                o32 = fb("o32", [P, T])
                k_add = fb("k_add", [P, T])
                st = fb("st", [P, 2, 3, 4])
                maskr, idr = fb("maskr", [P, P], F32R), fb("idr", [P, P], F32R)

        ps = ctx.enter_context(nc.psum_tensor("ps", [P, 8, T], F32))
        ident = const[:, K_ID:K_ID + P]

        loaded = sem("loaded")
        ffn_in = [sem(f"ffn_in{k}") for k in range(3)]
        ones_set = sem("ones_set")
        w_split = sem("w_split")
        w_hi_c = sem("w_hi_c")
        w_split_c = sem("w_split_c")
        stored = sem("stored")
        phase_end = sem("phase_end")
        a_in, a_hi, a_lo = sem("a_in"), sem("a_hi"), sem("a_lo")

        class Signals:

            def __init__(self, sems, base):
                self.sems, self.base = sems, base

            def __getitem__(self, name):
                return self.sems[name]

            def __call__(self, name, n):
                return self.sems[name], self.base[name] + n

        def group(tag, counts, runs):
            sems = {n: sem(f"{tag}_{n}") for n in counts}
            primed.extend(sems.values())
            return [Signals(sems, {n: 1 + k * c for n, c in counts.items()}) for k in range(runs)]

        primed, primed_all = [], sem("primed_all")

        TILES = 2 * NB + CH * NB
        ROUTE_STEPS = 26
        LN = group("ln", dict.fromkeys("mean centred squared var dev inv diag spread normed xn_hi xn_lo".split(), NB), 6)
        F1, F2 = group("ffn", {"gate": 4 * NB, "up": 4 * NB, "silu": 4 * NB, "hidden": 4 * NB, "mid": 8 * NB, "gelu": 8 * NB,
                               "hid_hi": 12 * NB, "hid_lo": 12 * NB, "out": NB, "x_new": NB}, 2)
        E1, E2 = group("moe", {"raw_in0": 32 * PAIRS, "raw_in1": 32 * PAIRS, "small_in": 32, "small_hi": 2, "small_lo": 2,
                               "logits": 2, "scores": 2, "route": ROUTE_STEPS, "routed": 2, "rw_t": 4, "rwt": 4,
                               "spread": CH * NB, "w_hi": 2 * CH, "w_lo": 2 * CH, "x_new": NB}
                       | dict.fromkeys("gate up silu gated weighted h_hi h_lo down".split(), TILES), 2)
        M, = group("mix", dict.fromkeys((
            "raw_in w_hi w_lo dt_w sel_set inproj zproj biased conv xc sz xc_hi xc_lo bcdt "
            "bc_hi bc_lo v nabs e ln dt du du_pool b_spread c_spread da db h c_copy hc y_sum ylin "
            "gated g_hi g_lo out x_new aexp bc_zero dt_b").split(), 0), 1)
        A, = group("att", dict.fromkeys((
            "mask k_add xb_hi xb_lo kp vp k32 k_hi k_lo v32 v_hi v_lo qp q32 q_hi q_lo s "
            "min p inv pn pt pt_hi pt_lo o o32 o_hi o_lo y x_new").split(), 0), 1)

        block = ctx.enter_context(nc.Block())

        def end_phase(eng):
            eng.drain().then_inc(phase_end, 1)

        def start_phase(eng, k):
            eng.wait_ge(phase_end, 4 * k)

        def cut(b):
            return slice(b * T, (b + 1) * T)

        def mm3(pe, out, w_hi, w_lo, x_hi, x_lo, start, stop):
            pe.matmul(out, w_hi, x_hi, start=start, stop=False, skip_group_check=True)
            pe.matmul(out, w_hi, x_lo, start=False, stop=False, skip_group_check=True)
            return pe.matmul(out, w_lo, x_hi, start=False, stop=stop, skip_group_check=True)

        def split_hi(act, hi, full):
            return act.activation(hi, full, ACT.Identity)

        def split_lo(eng, lo, full, hi):
            return eng.tensor_tensor(lo, full, hi.bitcast(F32), ALU.subtract)

        def ln_pe(pe, L):
            def mean(b):
                pe.matmul(ps[:, b, :], mean_w[:, :], x[:, cut(b)], start=True, stop=True).then_inc(L["mean"], 1)

            def var(b):
                pe.wait_ge(*L("squared", b + 1))
                for t in range(4):
                    tt = slice(b * T + t * P, b * T + (t + 1) * P)
                    last = pe.matmul(ps[:, 4 + b, t:t + 1], ln_t[:, tt], mean_w[:, 0:1], start=True, stop=True, skip_group_check=True)
                last.then_inc(L["var"], 1)

            def spread(b):
                pe.wait_ge(*L("diag", b + 1))
                pe.matmul(ps[:, 4 + b, :], mean_w[:, :], ln_t[:, cut(b)], start=True, stop=True).then_inc(L["spread"], 1)

            mean(0)
            mean(1)
            var(0)
            mean(2)
            var(1)
            spread(0)
            mean(3)
            var(2)
            spread(1)
            var(3)
            spread(2)
            spread(3)

        def banks_free(pe, L):
            pe.wait_ge(*L("centred", NB))
            pe.wait_ge(*L("normed", NB))

        def ln_dve(dve, L):
            def centre(b):
                dve.wait_ge(*L("mean", b + 1))
                dve.tensor_tensor(ln_c[:, cut(b)], x[:, cut(b)], ps[:, b, :], ALU.subtract).then_inc(L["centred"], 1)

            def diagonal(b):
                r = rstd[:, 4 * b:4 * b + 4]
                dve.wait_ge(*L("dev", b + 1))
                dve.reciprocal(r, r).then_inc(L["inv"], 1)
                dve.wait_ge(*L("inv", b + 1))
                dve.scalar_tensor_tensor(ln_t[:, cut(b)].rearrange("p (t n) -> p t n", t=4), ident.unsqueeze(1).broadcast_to([P, 4, P]),
                                         float(P), r.unsqueeze(2).broadcast_to([P, 4, P]), ALU.mult, ALU.mult).then_inc(L["diag"], 1)

            def normalise(b):
                dve.wait_ge(*L("spread", b + 1))
                dve.tensor_tensor(ln_c[:, cut(b)], ln_c[:, cut(b)], ps[:, 4 + b, :], ALU.mult).then_inc(L["normed"], 1)

            centre(0)
            centre(1)
            diagonal(0)
            centre(2)
            diagonal(1)
            normalise(0)
            centre(3)
            diagonal(2)
            normalise(1)
            diagonal(3)
            normalise(2)
            normalise(3)

        def ln_act(act, L):
            def square(b):
                act.wait_ge(*L("centred", b + 1))
                act.activation(ln_t[:, cut(b)], ln_c[:, cut(b)], ACT.Square).then_inc(L["squared"], 1)

            def deviation(b):
                act.wait_ge(*L("var", b + 1))
                act.activation(rstd[:, 4 * b:4 * b + 4], ps[:, 4 + b, 0:4], ACT.Sqrt, bias=cols[:, C_EPS:C_EPS + 1]).then_inc(L["dev"], 1)

            def high(b):
                act.wait_ge(*L("normed", b + 1))
                split_hi(act, xn_hi[:, cut(b)], ln_c[:, cut(b)]).then_inc(L["xn_hi"], 1)

            square(0)
            square(1)
            deviation(0)
            square(2)
            deviation(1)
            high(0)
            square(3)
            deviation(2)
            high(1)
            deviation(3)
            high(2)
            high(3)

        def ln_pool(pool, L):
            for b in range(NB):
                pool.wait_ge(*L("xn_hi", b + 1))
                split_lo(pool, xn_lo[:, cut(b)], ln_c[:, cut(b)], xn_hi[:, cut(b)]).then_inc(L["xn_lo"], 1)

        def ffn_pe(pe, S, L):
            banks_free(pe, L)
            with pe.Fori(0, NB) as i:
                blk = bass.ds(i * T, T)
                pe.wait_ge(*L("xn_lo", i + 1))
                for o in range(HC):
                    c = slice(o * P, (o + 1) * P)
                    g = slice(W_G + o * P, W_G + (o + 1) * P)
                    u = slice(W_U + o * P, W_U + (o + 1) * P)
                    if o == 3:
                        pe.wait_ge(*S("x_new", i))
                    mm3(pe, ps[:, o, :], wh[:, g], wl[:, g], xn_hi[:, blk], xn_lo[:, blk], True, True).then_inc(S["gate"], 1)
                    mm3(pe, ps[:, 4 + o, :], wh[:, u], wl[:, u], xn_hi[:, blk], xn_lo[:, blk], True, True).then_inc(S["up"], 1)
                for layer_, (w0, bank) in enumerate(((W_H1, 0), (W_H2, 4))):
                    if S is F1 and layer_ == 1:
                        pe.wait_ge(w_split_c, 1)
                    for k in range(HC):
                        pe.wait_ge(*S("hid_lo", 12 * i + 4 * layer_ + k + 1))
                        for o in range(HC):
                            if layer_ == 0 and k == 0:
                                pe.wait_ge(*S("silu", 4 * i + o + 1))
                            w = slice(w0 + k * HID + o * P, w0 + k * HID + (o + 1) * P)
                            last = mm3(pe, ps[:, bank + o, :], wh[:, w], wl[:, w], hid_hi[:, layer_, k, :],
                                       hid_lo[:, layer_, k, :], k == 0, k == HC - 1)
                            if k == HC - 1:
                                last.then_inc(S["mid"], 1)
                for k in range(HC):
                    pe.wait_ge(*S("hid_lo", 12 * i + 8 + k + 1))
                    w = slice(W_3 + k * P, W_3 + (k + 1) * P)
                    last = mm3(pe, ps[:, 3, :], wh[:, w], wl[:, w], hid_hi[:, 2, k, :], hid_lo[:, 2, k, :], k == 0, k == HC - 1)
                last.then_inc(S["out"], 1)

        def ffn_act(act, S):
            with act.Fori(0, NB) as i:
                for o in range(HC):
                    act.wait_ge(*S("gate", 4 * i + o + 1))
                    act.activation(f_s[:, o, :], ps[:, o, :], ACT.Silu, scale=cols[:, C_W1 + o:C_W1 + o + 1]).then_inc(S["silu"], 1)
                for layer_, (c0, bank) in enumerate(((C_H1, 0), (C_H2, 4))):
                    for o in range(HC):
                        act.wait_ge(*S("mid", 8 * i + 4 * layer_ + o + 1))
                        act.wait_ge(*S("hid_lo", 12 * i + 4 * layer_ + o + 1))
                        act.activation(f_h[:, o, :], ps[:, bank + o, :], ACT.Gelu, scale=cols[:, c0 + o:c0 + o + 1]).then_inc(S["gelu"], 1)

        def ffn_dve(dve, S):
            def split(i, layer_, o):
                q = 4 * layer_ + o
                dve.tensor_copy(hid_hi[:, layer_, o, :], f_h[:, o, :]).then_inc(S["hid_hi"], 1)
                dve.wait_ge(*S("hid_hi", 12 * i + q + 1))
                split_lo(dve, hid_lo[:, layer_, o, :], f_h[:, o, :], hid_hi[:, layer_, o, :]).then_inc(S["hid_lo"], 1)

            with dve.Fori(0, NB) as i:
                blk = bass.ds(i * T, T)
                for o in range(HC):
                    dve.wait_ge(*S("up", 4 * i + o + 1))
                    dve.wait_ge(*S("silu", 4 * i + o + 1))
                    dve.scalar_tensor_tensor(f_h[:, o, :], ps[:, 4 + o, :], cols[:, C_W2 + o:C_W2 + o + 1], f_s[:, o, :],
                                             ALU.mult, ALU.mult).then_inc(S["hidden"], 1)
                    dve.wait_ge(*S("hidden", 4 * i + o + 1))
                    split(i, 0, o)
                for layer_ in (1, 2):
                    for o in range(HC):
                        dve.wait_ge(*S("gelu", 8 * i + 4 * (layer_ - 1) + o + 1))
                        split(i, layer_, o)
                dve.wait_ge(*S("out", i + 1))
                dve.scalar_tensor_tensor(x[:, blk], ps[:, 3, :], w3_half[:, :], x[:, blk], ALU.mult, ALU.add).then_inc(S["x_new"], 1)

        ITEMS, HEAD = DS * MC, 8
        DEEP = 4

        def after(eng, name, n):
            if not isinstance(n, int) or n > 0:
                eng.wait_ge(*M(name, n))

        def scan_blocks(eng, item, finish):
            for q in range(HEAD):
                item(0, cut(0), q, False)
            with eng.Fori(0, NB - 1) as i:
                blk, following = bass.ds(i * T, T), bass.ds((i + 1) * T, T)
                for q in range(HEAD, ITEMS):
                    item(i, blk, q, False)
                for q in range(HEAD):
                    item(i + 1, following, q, False)
                    finish(i, blk, q)
            for q in range(HEAD, ITEMS):
                item(NB - 1, cut(NB - 1), q, True)
            for q in range(HEAD):
                finish(NB - 1, cut(NB - 1), q)

        def mix_pe(pe, L):
            def in_proj(i, blk):
                after(pe, "conv", 6 * i)
                after(pe, "sz", 2 * i)
                for o in range(2 * MC):
                    w = slice(M_IN + o * P, M_IN + (o + 1) * P)
                    mm3(pe, ps[:, o, :], mh[:, w], ml[:, w], xn_hi[:, blk], xn_lo[:, blk], True, True)\
                        .then_inc(M["inproj"] if o < MC else M["zproj"], 1)

            def x_proj(i):
                for m in range(MC):
                    pe.wait_ge(*M("xc_lo", 2 * i + m + 1))
                    if m == 0:
                        after(pe, "bc_lo", i)
                        after(pe, "v", 2 * i)
                    w = slice(M_X + 33 * m + 1, M_X + 33 * m + 33)
                    mm3(pe, ps[0:2 * DS, 4, :], mh[:, w], ml[:, w], g_hi[:, m, :], g_lo[:, m, :], m == 0, m == MC - 1)
                    last = mm3(pe, ps[:, 5, :], dtw_hi[:, m, :], dtw_lo[:, m, :], g_hi[:, m, :], g_lo[:, m, :], m == 0, m == MC - 1)
                last.then_inc(M["bcdt"], 1)

            pe.wait_ge(*M("w_lo", 1))
            banks_free(pe, L)
            pe.wait_ge(*L("xn_lo", NB))
            in_proj(0, cut(0))
            pe.wait_ge(*M("dt_w", 2))
            with pe.Fori(0, NB - 1) as i:
                in_proj(i + 1, bass.ds((i + 1) * T, T))
                x_proj(i)
            x_proj(NB - 1)

            def spread(i, blk, n):
                after(pe, "db", 32 * i + 2 * n - 2)
                pe.matmul(ps[:, n % 2, :], sel_bc[:, n, :], bc[:, blk], start=True, stop=True).then_inc(M["b_spread"], 1)
                after(pe, "c_copy", 16 * i + n - 1)
                pe.matmul(ps[:, 2 + n % 2, :], sel_bc[:, DS + n, :], bc[:, blk], start=True, stop=True).then_inc(M["c_spread"], 1)

            def item(i, blk, q, last):
                n, m = q // MC, q % MC
                if m == 1 and n + 2 < DS:
                    spread(i, blk, n + 2)
                elif m == 1 and not last:
                    spread(i + 1, bass.ds((i + 1) * T, T), n + 2 - DS)
                if n == 0:
                    after(pe, "ylin", 2 * i + m - 1)
                pe.wait_ge(*M("hc", 32 * i + q + 1))
                pe.matmul(ps[:, 4 + m, :], ident, m_hc[:, q % DEEP, :], start=(n == 0), stop=(n == DS - 1),
                          skip_group_check=True).then_inc(M["y_sum"], 1)

            def finish(i, blk, q):
                if q == 4:
                    after(pe, "x_new", i)
                    for m in range(MC):
                        pe.wait_ge(*M("g_lo", 2 * i + m + 1))
                        w = slice(M_OUT + m * P, M_OUT + (m + 1) * P)
                        last = mm3(pe, ps[:, 6, :], mh[:, w], ml[:, w], g_hi[:, m, :], g_lo[:, m, :], m == 0, m == MC - 1)
                    last.then_inc(M["out"], 1)

            pe.wait_ge(*M("sel_set", 1))
            pe.wait_ge(*M("bc_zero", 1))
            pe.wait_ge(*M("conv", 6 * NB))
            pe.wait_ge(*M("sz", 2 * NB))
            pe.wait_ge(*M("bc_lo", NB))
            pe.wait_ge(*M("v", 2 * NB))
            spread(0, cut(0), 0)
            spread(0, cut(0), 1)
            scan_blocks(pe, item, finish)

        def mix_act(act):
            def before_conv(i):
                for m in range(MC):
                    act.wait_ge(*M("inproj", 2 * i + m + 1))
                    after(act, "xc", 2 * (i - 1) + m + 1)
                    act.activation(m_y[:, m, :], ps[:, m, :], ACT.Identity, scale=cols[:, C_CONV + 4 * m + 3:C_CONV + 4 * m + 4],
                                   bias=cols[:, C_CB + m:C_CB + m + 1]).then_inc(M["biased"], 1)

            def silus(i, blk, out, name, source, done, count):
                for m in range(MC):
                    act.wait_ge(*M(done, count * (i * MC + m + 1)))
                    act.wait_ge(phase_end, 4)
                    act.activation(out[:, m, blk], source[:, m, :], ACT.Silu).then_inc(M[name], 1)

            def after_proj(i, blk):
                act.wait_ge(*M("bcdt", i + 1))
                act.wait_ge(phase_end, 4)
                act.activation(bc[0:2 * DS, blk], ps[0:2 * DS, 4, :], ACT.Identity).then_inc(M["bc_hi"], 1)
                for m in range(MC):
                    act.wait_ge(phase_end, 4)
                    act.activation(dt[:, m, blk], ps[:, 5, :], ACT.Identity, scale=cols[:, C_DTW + m:C_DTW + m + 1],
                                   bias=cols[:, C_DTB + m:C_DTB + m + 1]).then_inc(M["v"], 1)

            act.activation(warm[:, :], cols[:, 0:1], ACT.Silu)
            before_conv(0)
            silus(0, cut(0), sz, "sz", ps[:, MC:2 * MC, :], "zproj", 1)
            silus(0, cut(0), xc, "xc", m_y, "conv", 3)
            with act.Fori(0, NB - 1) as i:
                blk, following = bass.ds(i * T, T), bass.ds((i + 1) * T, T)
                before_conv(i + 1)
                silus(i + 1, following, sz, "sz", ps[:, MC:2 * MC, :], "zproj", 1)
                after_proj(i, blk)
                silus(i + 1, following, xc, "xc", m_y, "conv", 3)
            after_proj(NB - 1, cut(NB - 1))
            act.activation(neg_a[:, :], cols[:, C_ALOG:C_ALOG + MC * DS], ACT.Exp).then_inc(M["aexp"], 1)
            for b in range(NB):
                act.wait_ge(*M("nabs", b + 1))
                act.activation(du[:, :, cut(b)], du[:, :, cut(b)], ACT.Exp).then_inc(M["e"], 1)
            for b in range(NB):
                act.wait_ge(*M("e", b + 1))
                act.activation(du[:, :, cut(b)], du[:, :, cut(b)], ACT.Ln, bias=1.0).then_inc(M["ln"], 1)
            act.wait_ge(*M("aexp", 2))

            def item(i, blk, q, last):
                n, m = q // MC, q % MC
                if q == 0:
                    act.wait_ge(*M("dt_b", i + 1))
                after(act, "h", 32 * i + q + 1 - DEEP)
                act.activation(m_da[:, q % DEEP, :], dt_b[:, m, :], ACT.Exp,
                               scale=neg_a[:, m * DS + n:m * DS + n + 1]).then_inc(M["da"], 1)
                if m == 1:
                    act.wait_ge(*M("c_spread", 16 * i + n + 1))
                    after(act, "hc", 32 * i + 2 * n - 2)
                    act.activation(m_c[:, n % 2, :], ps[:, 2 + n % 2, :], ACT.Identity).then_inc(M["c_copy"], 1)

            def finish(i, blk, q):
                if q == 3:
                    after(act, "out", i)
                    for m in range(MC):
                        act.wait_ge(*M("gated", 2 * i + m + 1))
                        split_hi(act, g_hi[:, m, :], m_y[:, m, :]).then_inc(M["g_hi"], 1)

            scan_blocks(act, item, finish)

        def mix_dve(dve):
            dve.wait_ge(*M("w_lo", 1))
            for half, (src, dst) in enumerate(((mh, dtw_hi), (ml, dtw_lo))):
                v = src[:, M_X:M_X + 66].rearrange("p (m c) -> p m c", m=MC)[:, :, 0:1].bitcast(F32)
                dve.tensor_copy(dst[:, :, :], v.broadcast_to([P, MC, P])).then_inc(M["dt_w"], 1)

            def conv(i):
                for m in range(MC):
                    dve.wait_ge(*M("biased", 2 * i + m + 1))
                    for s_, j in enumerate((2, 1, 0)):
                        back = 3 - j
                        after(dve, "conv", 6 * i + 3 * m + s_)
                        dve.scalar_tensor_tensor(m_y[:, m, back:T], ps[:, m, 0:T - back], cols[:, C_CONV + 4 * m + j:C_CONV + 4 * m + j + 1],
                                                 m_y[:, m, back:T], ALU.mult, ALU.add).then_inc(M["conv"], 1)

            def split(i, blk):
                for m in range(MC):
                    dve.wait_ge(*M("xc", 2 * i + m + 1))
                    after(dve, "bcdt", i)
                    dve.tensor_copy(g_hi[:, m, :], xc[:, m, blk]).then_inc(M["xc_hi"], 1)
                    dve.wait_ge(*M("xc_hi", 2 * i + m + 1))
                    split_lo(dve, g_lo[:, m, :], xc[:, m, blk], g_hi[:, m, :]).then_inc(M["xc_lo"], 1)

            def after_proj(i, blk):
                dve.wait_ge(*M("bc_hi", i + 1))
                split_lo(dve, bc[2 * DS:4 * DS, blk], ps[0:2 * DS, 4, :], bc[0:2 * DS, blk]).then_inc(M["bc_lo"], 1)
                dve.wait_ge(*M("v", 2 * i + 2))
                dve.scalar_tensor_tensor(du[:, :, blk], dt[:, :, blk], -1.0, dt[:, :, blk], ALU.mult, ALU.min).then_inc(M["nabs"], 1)

            conv(0)
            with dve.Fori(0, NB - 1) as i:
                blk = bass.ds(i * T, T)
                split(i, blk)
                conv(i + 1)
                after_proj(i, blk)
            split(NB - 1, cut(NB - 1))
            after_proj(NB - 1, cut(NB - 1))
            dve.wait_ge(*M("aexp", 1))
            dve.tensor_scalar(neg_a[:, :], neg_a[:, :], -1.0, None, ALU.mult).then_inc(M["aexp"], 1)

            def dt_copy(i, blk):
                dve.tensor_copy(dt_b, dt[:, :, blk]).then_inc(M["dt_b"], 1)

            for b in range(NB):
                dve.wait_ge(*M("ln", b + 1))
                dve.scalar_tensor_tensor(dt[:, :, cut(b)], dt[:, :, cut(b)], 0.0, du[:, :, cut(b)], ALU.max, ALU.add).then_inc(M["dt"], 1)
                dve.wait_ge(*M("dt", b + 1))
                if b == 0:
                    dt_copy(0, cut(0))
                if b < DU_DVE:
                    dve.tensor_tensor(du[:, :, cut(b)], dt[:, :, cut(b)], xc[:, :, cut(b)], ALU.mult).then_inc(M["du"], 1)

            def input_term(i, blk, q):
                n, m = q // MC, q % MC
                after(dve, "h", 32 * i + q - 1)
                dve.wait_ge(*M("b_spread", 16 * i + n + 1))
                dve.tensor_tensor(m_db[:, q % 2, :], du[:, m, blk], ps[:, n % 2, :], ALU.mult).then_inc(M["db"], 1)

            def item(i, blk, q, last):
                following = bass.ds((i + 1) * T, T)
                if q == ITEMS - 2 and not last:
                    dve.wait_ge(*M("da", 32 * i + ITEMS))
                    dt_copy(i + 1, following)
                if q + 1 < ITEMS:
                    input_term(i, blk, q + 1)
                elif not last:
                    dve.wait_ge(*M("du_pool", NB - DU_DVE))
                    input_term(i + 1, following, 0)
                dve.wait_ge(*M("da", 32 * i + q + 1))
                dve.wait_ge(*M("db", 32 * i + q + 1))
                after(dve, "hc", 32 * i + q + 1 - DEEP)
                dve.tensor_tensor_scan(m_h[:, q % DEEP, :], m_da[:, q % DEEP, :], m_db[:, q % 2, :], 0.0,
                                       ALU.mult, ALU.add).then_inc(M["h"], 1)

            def finish(i, blk, q):
                if q == 1:
                    for m in range(MC):
                        dve.wait_ge(*M("y_sum", 32 * i + 31 + m))
                        dve.scalar_tensor_tensor(m_y[:, m, :], xc[:, m, blk], cols[:, C_D + m:C_D + m + 1], ps[:, 4 + m, :],
                                                 ALU.mult, ALU.add).then_inc(M["ylin"], 1)
                if q == 2:
                    for m in range(MC):
                        dve.wait_ge(*M("ylin", 2 * i + m + 1))
                        dve.tensor_tensor(m_y[:, m, :], m_y[:, m, :], sz[:, m, blk], ALU.mult).then_inc(M["gated"], 1)
                if q == 4:
                    for m in range(MC):
                        dve.wait_ge(*M("g_hi", 2 * i + m + 1))
                        split_lo(dve, g_lo[:, m, :], m_y[:, m, :], g_hi[:, m, :]).then_inc(M["g_lo"], 1)
                if q == 7:
                    dve.wait_ge(*M("out", i + 1))
                    dve.tensor_tensor(x[:, blk], x[:, blk], ps[:, 6, :], ALU.add).then_inc(M["x_new"], 1)

            dve.wait_ge(*M("du", DU_DVE))
            input_term(0, cut(0), 0)
            scan_blocks(dve, item, finish)

        def mix_pool(pool):
            pool.tensor_copy(sel_bc[:, :, :], const[:, K_ID32:K_ID32 + 2 * DS].unsqueeze(2).broadcast_to([P, 2 * DS, P]))\
                .then_inc(M["sel_set"], 1)
            for b in range(DU_DVE, NB):
                pool.wait_ge(*M("dt", b + 1))
                pool.tensor_tensor(du[:, :, cut(b)], dt[:, :, cut(b)], xc[:, :, cut(b)], ALU.mult).then_inc(M["du_pool"], 1)

            def item(i, blk, q, last):
                n = q // MC
                pool.wait_ge(*M("h", 32 * i + q + 1))
                if q % MC == 0:
                    pool.wait_ge(*M("c_copy", 16 * i + n + 1))
                after(pool, "y_sum", 32 * i + q + 1 - DEEP)
                pool.tensor_tensor(m_hc[:, q % DEEP, :], m_h[:, q % DEEP, :], m_c[:, n % 2, :], ALU.mult).then_inc(M["hc"], 1)

            scan_blocks(pool, item, lambda i, blk, q: None)

        SHARED = 2 * NB
        PER = 2 * NB

        def moe_pe(pe, S, L):
            pe.wait_ge(*S("small_lo", 1))
            banks_free(pe, L)
            for t in range(NTT):
                pe.wait_ge(*L("xn_lo", t // 4 + 1))
                tt = slice(t * P, (t + 1) * P)
                r = slice(S_R, S_R + E)
                out = ps[:, 6 + t // 8, (t % 8) * E:(t % 8 + 1) * E]
                pe.matmul(out, xn_hi[:, tt], sh[:, r], start=True, stop=False, skip_group_check=True)
                pe.matmul(out, xn_hi[:, tt], sl[:, r], start=False, stop=False, skip_group_check=True)
                last = pe.matmul(out, xn_lo[:, tt], sh[:, r], start=False, stop=True, skip_group_check=True)
                if t % 8 == 7:
                    last.then_inc(S["logits"], 1)
            pe.wait_ge(*S("small_lo", 2))

            def gate_up(t, gh, gl, uh, ul, b, rows_):
                pe.wait_ge(*S("silu", t))
                mm3(pe, ps[0:rows_, 4, :], gh, gl, xn_hi[:, cut(b)], xn_lo[:, cut(b)], True, True).then_inc(S["gate"], 1)
                pe.wait_ge(*S("gated", t))
                mm3(pe, ps[0:rows_, 5, :], uh, ul, xn_hi[:, cut(b)], xn_lo[:, cut(b)], True, True).then_inc(S["up"], 1)

            def down(t, dh, dl, b, start, stop, rows_):
                pe.wait_ge(*S("h_lo", t + 1))
                mm3(pe, ps[:, b, :], dh, dl, e_hi[0:rows_, b, :], e_lo[0:rows_, b, :], start, stop).then_inc(S["down"], 1)

            def shared_gate_up(t):
                c, b = t // NB, t % NB
                g = slice(S_G + c * I, S_G + (c + 1) * I)
                u = slice(S_U + c * I, S_U + (c + 1) * I)
                gate_up(t, sh[:, g], sl[:, g], sh[:, u], sl[:, u], b, I)

            def shared_down(t):
                c, b = t // NB, t % NB
                down(t, sd_h[:, c, :], sd_l[:, c, :], b, c == 0, False, I)

            def expert_gate_up(i, j):
                c, b = j // NB, j % NB
                t = PER * i + SHARED + j
                if b == 0:
                    pe.wait_ge(*S("w_lo", 4 * i + 2 * c + 1))
                gate_up(t, eh[:, c, 1, :], el[:, c, 1, :], eh[:, c, 2, :], el[:, c, 2, :], b, P)
                pe.wait_ge(*S("weighted", t))
                pe.matmul(ps[:, 6, :], eh[:, c, 3, :], rwt[:, cut(b)], start=True, stop=True).then_inc(S["spread"], 1)

            def expert_down(i, j, stop):
                c, b = j // NB, j % NB
                if b == 0:
                    pe.wait_ge(*S("w_lo", 4 * i + 2 * c + 2))
                down(PER * i + SHARED + j, eh[:, c, 0, :], el[:, c, 0, :], b, False, stop, P)

            for t in range(SHARED):
                shared_gate_up(t)
                if t >= 2:
                    shared_down(t - 2)
            shared_down(SHARED - 2)
            shared_down(SHARED - 1)
            pe.wait_ge(*S("routed", 2))
            for g in range(4):
                pe.wait_ge(*S("rwt", g))
                for t in range(4):
                    last = pe.transpose(ps[:, 6, t * P:(t + 1) * P],
                                        rw_cat[:, 4 * g + t, :, :].rearrange("p a e -> p (a e)"), ident)
                last.then_inc(S["rw_t"], 1)
            pe.wait_ge(*S("rwt", 4))
            expert_gate_up(0, 0)
            expert_gate_up(0, 1)
            with pe.Fori(0, PAIRS - 1) as i:
                for j in range(PER):
                    expert_gate_up(i + (j + 2) // PER, (j + 2) % PER)
                    expert_down(i, j, False)
            for j in range(PER):
                if j + 2 < PER:
                    expert_gate_up(PAIRS - 1, j + 2)
                expert_down(PAIRS - 1, j, j >= NB)

        def moe_act(act, S):
            act.wait_ge(*S("small_in", 32))
            act.activation(sh[:, :], s_raw[:, :], ACT.Identity).then_inc(S["small_hi"], 1)
            act.activation(sd_h[:, :, :], sd_raw[:, :, :], ACT.Identity).then_inc(S["small_hi"], 1)

        def moe_act_tiles(act, S):
            for half in range(2):
                act.wait_ge(*S("logits", half + 1))
                act.activation(r_s[:, 8 * half:8 * half + 8, :].rearrange("p t e -> p (t e)"), ps[:, 6 + half, :], ACT.Sigmoid)\
                    .then_inc(S["scores"], 1)

            def gate_up_high(i, c, read):
                act.wait_ge(*S(f"raw_in{c}", 32 * i + 32))
                act.wait_ge(*S("spread", read))
                act.activation(eh[:, c, 1:4, :], e_raw[:, c, 1:4, :], ACT.Identity).then_inc(S["w_hi"], 1)

            def down_high(i, c, read):
                act.wait_ge(*S("down", read))
                act.activation(eh[:, c, 0, :], e_raw[:, c, 0, :], ACT.Identity).then_inc(S["w_hi"], 1)

            def silu(t, buf, rows_):
                act.wait_ge(*S("gate", t + 1))
                if not (isinstance(t, int) and t < 4):
                    act.wait_ge(*S("gated", t - 3))
                act.activation(e_s[0:rows_, buf, :], ps[0:rows_, 4, :], ACT.Silu).then_inc(S["silu"], 1)

            def high(t, buf, rows_):
                act.wait_ge(*S("weighted", t + 1))
                if not (isinstance(t, int) and t < 4):
                    act.wait_ge(*S("down", t - 3))
                split_hi(act, e_hi[0:rows_, buf, :], e_h[0:rows_, buf, :]).then_inc(S["h_hi"], 1)

            gate_up_high(0, 0, 0)
            down_high(0, 0, 0)
            for t in range(SHARED):
                silu(t, t % 4, I)
                if t:
                    high(t - 1, (t - 1) % 4, I)
            high(SHARED - 1, 3, I)
            for g in range(4):
                act.wait_ge(*S("rw_t", g + 1))
                act.activation(rwt[:, cut(g)], ps[:, 6, :], ACT.Identity).then_inc(S["rwt"], 1)

            def pair(i, last):
                for j in range(PER):
                    t = PER * i + SHARED + j
                    silu(t, j % 4, P)
                    if j:
                        high(t - 1, (j - 1) % 4, P)
                    if j == 0:
                        gate_up_high(i, 1, PER * i)
                    if j == 2:
                        down_high(i, 1, PER * i + SHARED)
                    if j == 4 and not last:
                        gate_up_high(i + 1, 0, PER * i + 4)
                    if j == 6 and not last:
                        down_high(i + 1, 0, PER * i + SHARED + 4)
                high(PER * i + SHARED + PER - 1, 3, P)

            with act.Fori(0, PAIRS - 1) as i:
                pair(i, False)
            pair(PAIRS - 1, True)

        def moe_pool(pool, S):
            pool.wait_ge(*S("small_hi", 1))
            split_lo(pool, sl[:, :], s_raw[:, :], sh[:, :]).then_inc(S["small_lo"], 1)
            pool.wait_ge(*S("small_hi", 2))
            split_lo(pool, sd_l[:, :, :], sd_raw[:, :, :], sd_h[:, :, :]).then_inc(S["small_lo"], 1)

        def moe_pool_tiles(pool, S):
            def gate_up_low(i, c):
                pool.wait_ge(*S("w_hi", 4 * i + 2 * c + 1))
                split_lo(pool, el[:, c, 1:3, :], e_raw[:, c, 1:3, :], eh[:, c, 1:3, :]).then_inc(S["w_lo"], 1)

            def down_low(i, c):
                pool.wait_ge(*S("w_hi", 4 * i + 2 * c + 2))
                split_lo(pool, el[:, c, 0, :], e_raw[:, c, 0, :], eh[:, c, 0, :]).then_inc(S["w_lo"], 1)

            def low(t, buf, rows_):
                pool.wait_ge(*S("h_hi", t + 1))
                split_lo(pool, e_lo[0:rows_, buf, :], e_h[0:rows_, buf, :], e_hi[0:rows_, buf, :]).then_inc(S["h_lo"], 1)

            gate_up_low(0, 0)
            down_low(0, 0)
            for t in range(SHARED):
                low(t, t % 4, I)

            def pair(i, last):
                for j in range(PER):
                    if j == 0:
                        gate_up_low(i, 1)
                    if j == 2:
                        down_low(i, 1)
                    if j == 4 and not last:
                        gate_up_low(i + 1, 0)
                    if j == 6 and not last:
                        down_low(i + 1, 0)
                    low(PER * i + SHARED + j, j % 4, P)

            with pool.Fori(0, PAIRS - 1) as i:
                pair(i, False)
            pair(PAIRS - 1, True)

        def moe_dve(dve, S):
            steps = [0]

            def step(ins):
                steps[0] += 1
                ins.then_inc(S["route"], 1)
                dve.wait_ge(*S("route", steps[0]))

            NGT = NTT * NG
            small = [r_small[:, k, :] for k in range(4)]

            def pairs_of(tile, lo, n):
                v = tile[:, lo:lo + NGT * n].rearrange("p (g k) -> p g k", k=n)
                return v[:, :, 0:n // 2], v[:, :, n // 2:n]

            def out_of(tile, lo, n):
                return tile[:, lo:lo + NGT * n].rearrange("p (g k) -> p g k", k=n)

            dve.wait_ge(*S("scores", 2))
            bias = rows[:, R_GB:R_GB + E].unsqueeze(1).broadcast_to([P, NTT, E])
            step(dve.tensor_tensor(r_c[:, :, :], r_s[:, :, :], bias, ALU.add))
            c8 = r_c[:, :, :].rearrange("p t (g k) -> p (t g) k", k=8)
            a, b = c8[:, :, 0:4], c8[:, :, 4:8]
            step(dve.tensor_tensor(out_of(r_t, 0, 4), a, b, ALU.max))
            step(dve.tensor_tensor(out_of(r_u, 0, 4), a, b, ALU.min))
            a, b = pairs_of(r_t, 0, 4)
            ma, mb = pairs_of(r_u, 0, 4)
            step(dve.tensor_tensor(out_of(r_u, 512, 2), a, b, ALU.min))
            step(dve.tensor_tensor(out_of(r_t, 512, 2), a, b, ALU.max))
            step(dve.tensor_tensor(out_of(r_t, 768, 2), ma, mb, ALU.max))
            step(dve.tensor_tensor(out_of(r_u, 768, 2), out_of(r_u, 512, 2), out_of(r_t, 768, 2), ALU.max))
            a, b = pairs_of(r_t, 512, 2)
            ma, mb = pairs_of(r_u, 768, 2)
            one = [s_.unsqueeze(2) for s_ in small]
            step(dve.tensor_tensor(one[0], a, b, ALU.max))
            step(dve.tensor_tensor(one[1], a, b, ALU.min))
            step(dve.tensor_tensor(one[2], ma, mb, ALU.max))
            step(dve.tensor_tensor(small[1], small[1], small[2], ALU.max))
            step(dve.tensor_tensor(small[0], small[0], small[1], ALU.add))
            g3 = small[0].rearrange("p (t g) -> p t g", g=NG)
            other = g3.unsqueeze(2).broadcast_to([P, NTT, NG, NG])
            own = g3.unsqueeze(3).broadcast_to([P, NTT, NG, NG])
            t4 = r_t[:, :].rearrange("p (t g k) -> p t g k", g=NG, k=NG)
            u4 = r_u[:, :].rearrange("p (t g k) -> p t g k", g=NG, k=NG)
            tie = const[:, K_TIE:K_TIE + E].unsqueeze(1).broadcast_to([P, NTT, E])
            t3 = r_t[:, :].rearrange("p (t e) -> p t e", e=E)
            u3 = r_u[:, :].rearrange("p (t e) -> p t e", e=E)
            step(dve.tensor_tensor(t4, other, own, ALU.is_gt))
            step(dve.tensor_tensor(u4, other, own, ALU.is_equal))
            step(dve.tensor_tensor(u3, u3, tie, ALU.mult))
            step(dve.tensor_tensor(r_t[:, :], r_t[:, :], r_u[:, :], ALU.add))
            step(dve.tensor_reduce(small[1], out_of(r_t, 0, 8), AX, ALU.add))
            step(dve.tensor_scalar(small[1], small[1], 4.0, None, ALU.is_lt))
            step(dve.tensor_tensor(c8, c8, small[1].unsqueeze(2).broadcast_to([P, NGT, 8]), ALU.mult))
            for t in range(NTT):
                ins = dve.max(small[2][:, t * 8:t * 8 + 8], r_c[:, t, :])
                if t == NTT - 1:
                    step(ins)
            for t in range(NTT):
                ins = dve.match_replace(t3[:, t, :], small[2][:, t * 8:t * 8 + 8], r_c[:, t, :], GONE)
                if t == NTT - 1:
                    step(ins)
            step(dve.scalar_tensor_tensor(u3, t3, GONE, r_s[:, :, :], ALU.is_equal, ALU.mult))
            total = small[3][:, 0:NTT]
            step(dve.tensor_reduce(total, u3, AX, ALU.add))
            step(dve.tensor_scalar(total, total, 1e-20, None, ALU.add))
            step(dve.reciprocal(total, total))
            step(dve.scalar_tensor_tensor(t3, u3, 2.5, total.unsqueeze(2).broadcast_to([P, NTT, E]), ALU.mult, ALU.mult))
            dve.tensor_copy(rw_cat[:, :, 0, :].bitcast(F32R), t3).then_inc(S["routed"], 1)
            dve.wait_ge(*S("routed", 1))
            dve.tensor_tensor(rw_cat[:, :, 1, :].bitcast(F32R), t3, rw_cat[:, :, 0, :], ALU.subtract).then_inc(S["routed"], 1)

            assert steps[0] == ROUTE_STEPS

            def gate(t, buf, rows_):
                dve.wait_ge(*S("up", t + 1))
                dve.wait_ge(*S("silu", t + 1))
                if not (isinstance(t, int) and t < 2):
                    dve.wait_ge(*S("weighted", t - 1))
                dve.tensor_tensor(e_p[0:rows_, buf % 2, :], e_s[0:rows_, buf, :], ps[0:rows_, 5, :], ALU.mult).then_inc(S["gated"], 1)
                dve.wait_ge(*S("gated", t + 1))
                if not (isinstance(t, int) and t < 4):
                    dve.wait_ge(*S("h_lo", t - 3))

            for t in range(SHARED):
                gate(t, t % 4, I)
                dve.tensor_copy(e_h[0:I, t % 4, :], e_p[0:I, t % 2, :]).then_inc(S["weighted"], 1)
            with dve.Fori(0, PAIRS) as i:
                for j in range(PER):
                    t = PER * i + SHARED + j
                    gate(t, j % 4, P)
                    dve.wait_ge(*S("spread", PER * i + j + 1))
                    dve.tensor_tensor(e_h[:, j % 4, :], e_p[:, j % 2, :], ps[:, 6, :], ALU.mult).then_inc(S["weighted"], 1)
            for b in range(NB):
                dve.wait_ge(*S("down", SHARED + PER * (PAIRS - 1) + NB + b + 1))
                dve.scalar_tensor_tensor(x[:, cut(b)], ps[:, b, :], 0.5, x[:, cut(b)], ALU.mult, ALU.add).then_inc(S["x_new"], 1)

        def moe_load_small(sp, S):
            sp.dma_start(s_raw[:, :], d["l1_small"]).then_inc(S["small_in"], 16)
            sp.dma_start(sd_raw[:, :, :], d["sd"]).then_inc(S["small_in"], 16)

        def moe_load(sp, S):
            def chunk(i, c):
                sp.dma_start(e_raw[:, c, 0:3, :], d["experts"][bass.ds(2 * i + c, 1)].rearrange("a p k n -> p (a k) n"))\
                    .then_inc(S[f"raw_in{c}"], 16)
                sp.dma_start(e_raw[:, c, 3, :], d["pick"][bass.ds(2 * i + c, 1)].rearrange("a p n -> p (a n)"))\
                    .then_inc(S[f"raw_in{c}"], 16)

            chunk(0, 0)
            chunk(0, 1)
            with sp.Fori(0, PAIRS - 1) as i:
                for c in range(2):
                    sp.wait_ge(*S("w_lo", 4 * i + 2 * c + 2))
                    chunk(i + 1, c)

        SCALE = float(P) ** -0.5
        S_AT = {0: (1, 384), 1: (2, 0), 2: (1, 0), 3: (0, 0)}
        PT_AT = {0: (3, 0), 1: (4, 0), 2: (2, 256), 3: (4, 384)}
        ORDER = (3, 2, 0, 1)

        def scores_at(r):
            bank, lo = S_AT[r]
            return ps[:, bank, lo:lo + P * (r + 1)]

        PT_UNITS = (((2,), 2, 256, 2), ((1, 3), 1, T, 4), ((0,), 0, T, 4))
        PT_PART = {0: (0, 0), 1: (1, 0), 2: (2, 0), 3: (1, 384)}

        def pt_at(kb):
            bank, lo = PT_AT[kb]
            return ps[:, bank, lo:lo + T - P * kb]

        def pt_psum(unit):
            (kb, *_), _, n, _ = PT_UNITS[unit]
            bank, lo = PT_AT[kb]
            return ps[:, bank, lo:lo + n]

        def att_pe(pe, L):
            def k_proj(i, blk, first=False):
                if not first:
                    pe.wait_ge(*A("q32", 8 * i - 2))
                w = slice(A_K, A_K + P)
                mm3(pe, ps[:, 5, :], ah[:, w], al[:, w], xn_hi[:, blk], xn_lo[:, blk], True, True).then_inc(A["kp"], 1)

            def v_proj(i, x_hi, x_lo, first=False):
                if not first:
                    pe.wait_ge(*A("xb_lo", i))
                    pe.wait_ge(*A("p", 32 * i - 3))
                w = slice(A_V, A_V + P)
                for t in range(4):
                    tt = slice(t * P, (t + 1) * P)
                    out = ps[:, 0, tt]
                    pe.matmul(out, x_hi[:, tt], ah[:, w], start=True, stop=False, skip_group_check=True)
                    pe.matmul(out, x_hi[:, tt], al[:, w], start=False, stop=False, skip_group_check=True)
                    last = pe.matmul(out, x_lo[:, tt], ah[:, w], start=False, stop=True, skip_group_check=True)
                last.then_inc(A["vp"], 1)

            def q_proj(i, blk, h):
                if h == 0:
                    pe.wait_ge(*A("k32", i + 1))
                else:
                    pe.wait_ge(*A("q32", 8 * i + h))
                w = slice(A_Q + h * P, A_Q + (h + 1) * P)
                mm3(pe, ps[:, 5, :], ah[:, w], al[:, w], xn_hi[:, blk], xn_lo[:, blk], True, True).then_inc(A["qp"], 1)

            def score(i, h, first=False):
                g = 8 * i + h
                if h == 0:
                    pe.wait_ge(*A("k_lo", i + 1))
                    pe.wait_ge(*A("v32", i + 1))
                pe.wait_ge(*A("q_lo", g + 1))
                for k, r in enumerate(ORDER):
                    if not first and r != 0:
                        pe.wait_ge(*A("p", 4 * g - 4 + {3: 1, 2: 3, 1: 4}[r]))
                        if r == 1:
                            pe.wait_ge(*A("pt_lo", 3 * g - 2))
                    n = P * (r + 1)
                    q = slice(r * P, n)
                    out = scores_at(r)
                    pe.matmul(out, q_hi[:, h % 2, q], k_hi[:, 0:n], start=True, stop=False, skip_group_check=True)
                    pe.matmul(out, q_hi[:, h % 2, q], k_lo[:, 0:n], start=False, stop=False, skip_group_check=True)
                    pe.matmul(out, q_lo[:, h % 2, q], k_hi[:, 0:n], start=False, stop=False, skip_group_check=True)
                    last = pe.matmul(out[:, r * P:n], idr[:, :], maskr[:, :], start=False, stop=True, skip_group_check=True)
                    if r != 2:
                        last.then_inc(A["s"], 1)

            def turn(i, h):
                g = 8 * i + h
                pe.wait_ge(*A("p", 4 * g + 4))
                pe.wait_ge(*A("pt_lo", 3 * g))
                for tiles, _, _, need in PT_UNITS:
                    pe.wait_ge(*A("pn", 4 * g + need))
                    for kb in tiles:
                        for r in range(kb, 4):
                            last = pe.transpose(pt_at(kb)[:, (r - kb) * P:(r - kb + 1) * P], p32[:, r, kb * P:(kb + 1) * P], ident)
                    last.then_inc(A["pt"], 1)

            def values(i, h):
                g = 8 * i + h
                if h == 0:
                    pe.wait_ge(*A("v_lo", i + 1))
                pe.wait_ge(*A("o32", g))
                pe.wait_ge(*A("pt_lo", 3 * g + 3))
                for kb in range(4):
                    part, lo = PT_PART[kb]
                    n = T - kb * P
                    last = mm3(pe, ps[:, 6, kb * P:T], v_hi[:, kb, :], v_lo[:, kb, :], pt_hi[:, part, lo:lo + n],
                               pt_lo[:, part, lo:lo + n], kb == 0, kb == 3)
                last.then_inc(A["o"], 1)

            def out_proj(i, h):
                pe.wait_ge(*A("o_lo", 8 * i + h + 1))
                if h == 0:
                    pe.wait_ge(*A("x_new", i))
                w = slice(A_O + h * P, A_O + (h + 1) * P)
                mm3(pe, ps[:, 7, :], ah[:, w], al[:, w], o_hi[:, h % 2, :], o_lo[:, h % 2, :], h == 0, h == HEADS - 1)\
                    .then_inc(A["y"], 1)

            def heads(i, last):
                blk, following = bass.ds(i * T, T), bass.ds((i + 1) * T, T)
                for h in range(HEADS):
                    if h:
                        score(i, h)
                        values(i, h - 1)
                    if h < HEADS - 2:
                        q_proj(i, blk, h + 2)
                    elif h == HEADS - 2 and not last:
                        k_proj(i + 1, following)
                    elif not last:
                        q_proj(i + 1, following, 0)
                    if h >= 2:
                        out_proj(i, h - 2)
                    turn(i, h)
                if not last:
                    v_proj(i + 1, xb_hi, xb_lo)
                out_proj(i, HEADS - 2)
                values(i, HEADS - 1)
                if not last:
                    q_proj(i + 1, following, 1)
                    score(i + 1, 0)
                out_proj(i, HEADS - 1)

            pe.wait_ge(*A("mask", 2))
            pe.wait_ge(a_lo, 1)
            banks_free(pe, L)
            pe.wait_ge(*L("xn_lo", NB))
            k_proj(0, cut(0), True)
            v_proj(0, xn_hi[:, 0:T], xn_lo[:, 0:T], True)
            q_proj(0, cut(0), 0)
            q_proj(0, cut(0), 1)
            score(0, 0, True)
            with pe.Fori(0, NB - 1) as i:
                heads(i, False)
            heads(NB - 1, True)

        def att_act(act):
            def k_high(i):
                act.wait_ge(*A("k32", i + 1))
                act.wait_ge(*A("s", 24 * i))
                split_hi(act, k_hi[:, :], kv32[:, 0, :]).then_inc(A["k_hi"], 1)

            def v_high(i):
                act.wait_ge(*A("v32", i + 1))
                act.wait_ge(*A("o", 8 * i))
                act.activation(v_hi[:, :, :].rearrange("p t n -> p (t n)"), kv32[:, 1, :], ACT.Identity).then_inc(A["v_hi"], 1)

            def q_high(i, h, first=False):
                g = 8 * i + h
                act.wait_ge(*A("q32", g + 1))
                if not first:
                    act.wait_ge(*A("s", 3 * g - 3))
                split_hi(act, q_hi[:, h % 2, :], q32[:, h % 2, :]).then_inc(A["q_hi"], 1)

            def probs(i, h):
                g = 8 * i + h
                act.wait_ge(*A("pt", 3 * g))
                for k, r in enumerate(ORDER):
                    act.wait_ge(*A("min", 4 * g + (1, 3, 3, 4)[k]))
                    act.activation(p32[:, r, 0:P * (r + 1)], scores_at(r), ACT.Exp, scale=-1.0, bias=st[:, h % 2, 0, r:r + 1],
                                   accum_out=st[:, h % 2, 1, r:r + 1]).then_inc(A["p"], 1)

            def output(i, h):
                g = 8 * i + h
                act.wait_ge(*A("o", g + 1))
                act.wait_ge(*A("o_lo", g))
                act.activation(o32[:, :], ps[:, 6, :], ACT.Identity).then_inc(A["o32"], 1)
                act.wait_ge(*A("o32", g + 1))
                act.wait_ge(*A("y", max(g - 1, 0) if isinstance(g, int) else (g - 1 if h else g)))
                split_hi(act, o_hi[:, h % 2, :], o32[:, :]).then_inc(A["o_hi"], 1)

            def heads(i, last):
                for h in range(HEADS):
                    if h:
                        probs(i, h)
                        output(i, h - 1)
                    if h < HEADS - 2:
                        q_high(i, h + 2)
                    elif h == HEADS - 1 and not last:
                        k_high(i + 1)
                        q_high(i + 1, 0)
                    for unit, (_, part, n, _) in enumerate(PT_UNITS):
                        act.wait_ge(*A("pt", 3 * (8 * i + h) + unit + 1))
                        act.wait_ge(*A("o", 8 * i + h))
                        act.activation(pt_hi[:, part, 0:n], pt_psum(unit), ACT.Identity).then_inc(A["pt_hi"], 1)
                output(i, HEADS - 1)
                if not last:
                    v_high(i + 1)
                    q_high(i + 1, 1)
                    probs(i + 1, 0)

            k_high(0)
            q_high(0, 0, True)
            v_high(0)
            q_high(0, 1, True)
            probs(0, 0)
            with act.Fori(0, NB - 1) as i:
                heads(i, False)
            heads(NB - 1, True)

        def att_dve(dve, L):
            dve.tensor_copy(idr[:, :], ident).then_inc(A["mask"], 1)
            dve.tensor_copy(maskr[:, :], const[:, K_MASK:K_MASK + P]).then_inc(A["mask"], 1)
            pe_t = const[:, K_PE:K_PE + T]
            dve.tensor_scalar(k_add[:, :], pe_t, cols[:, C_BK:C_BK + 1], -SCALE, ALU.add, ALU.mult).then_inc(A["k_add"], 1)
            dve.wait_ge(*A("k_add", 1))

            def k_full(i):
                dve.wait_ge(*A("kp", i + 1))
                dve.wait_ge(*A("k_lo", i))
                dve.scalar_tensor_tensor(kv32[:, 0, :], ps[:, 5, :], -SCALE, k_add[:, :], ALU.mult, ALU.add).then_inc(A["k32"], 1)

            def v_full(i):
                dve.wait_ge(*A("vp", i + 1))
                dve.wait_ge(*A("v_lo", i))
                dve.tensor_tensor(kv32[:, 1, :].rearrange("p (t n) -> p t n", t=4), ps[:, 0, :].rearrange("p (t n) -> p t n", t=4),
                                  rows[:, R_BV:R_BV + P].unsqueeze(1).broadcast_to([P, 4, P]), ALU.add).then_inc(A["v32"], 1)

            def q_full(i, h, first=False):
                g = 8 * i + h
                dve.wait_ge(*A("qp", g + 1))
                if not first:
                    dve.wait_ge(*A("q_lo", g - 1))
                dve.scalar_tensor_tensor(q32[:, h % 2, :], ps[:, 5, :], cols[:, C_BQ + h:C_BQ + h + 1], pe_t,
                                         ALU.add, ALU.add).then_inc(A["q32"], 1)

            def minima(i, h):
                for r in ORDER:
                    dve.wait_ge(*A("s", 3 * (8 * i + h) + {3: 1, 2: 2, 0: 2, 1: 3}[r]))
                    dve.tensor_reduce(st[:, h % 2, 0, r:r + 1], scores_at(r), AX, ALU.min).then_inc(A["min"], 1)

            def normalise(i, h):
                g = 8 * i + h
                for half, tiles in enumerate(((3, 2), (0, 1))):
                    lo = min(tiles)
                    dve.wait_ge(*A("p", 4 * g + 2 * half + 2))
                    dve.reciprocal(st[:, h % 2, 2, lo:lo + 2], st[:, h % 2, 1, lo:lo + 2]).then_inc(A["inv"], 1)
                    dve.wait_ge(*A("inv", 2 * g + half + 1))
                    for r in tiles:
                        n = P * (r + 1)
                        dve.tensor_scalar(p32[:, r, 0:n], p32[:, r, 0:n], st[:, h % 2, 2, r:r + 1], None, ALU.mult).then_inc(A["pn"], 1)

            def heads(i, last):
                blk = bass.ds(i * T, T) if not last else cut(i)
                for h in range(HEADS):
                    if h:
                        minima(i, h)
                    normalise(i, h)
                    if h < HEADS - 2:
                        q_full(i, h + 2)
                    elif h == HEADS - 2 and not last:
                        k_full(i + 1)
                    elif not last:
                        q_full(i + 1, 0)
                    for unit, (_, part, n, _) in enumerate(PT_UNITS):
                        dve.wait_ge(*A("pt_hi", 3 * (8 * i + h) + unit + 1))
                        split_lo(dve, pt_lo[:, part, 0:n], pt_psum(unit), pt_hi[:, part, 0:n]).then_inc(A["pt_lo"], 1)
                if not last:
                    v_full(i + 1)
                    q_full(i + 1, 1)
                    minima(i + 1, 0)
                dve.wait_ge(*A("y", 8 * i + 8))
                dve.tensor_tensor(x[:, blk], x[:, blk], ps[:, 7, :], ALU.add).then_inc(A["x_new"], 1)

            k_full(0)
            q_full(0, 0, True)
            v_full(0)
            q_full(0, 1, True)
            minima(0, 0)
            with dve.Fori(0, NB - 1) as i:
                heads(i, False)
            heads(NB - 1, True)

        def att_pool(pool):
            def k_low(i):
                pool.wait_ge(*A("k_hi", i + 1))
                split_lo(pool, k_lo[:, :], kv32[:, 0, :], k_hi[:, :]).then_inc(A["k_lo"], 1)

            def v_low(i):
                pool.wait_ge(*A("v_hi", i + 1))
                split_lo(pool, v_lo[:, :, :].rearrange("p t n -> p (t n)"), kv32[:, 1, :],
                         v_hi[:, :, :].rearrange("p t n -> p (t n)")).then_inc(A["v_lo"], 1)

            def q_low(i, h):
                pool.wait_ge(*A("q_hi", 8 * i + h + 1))
                split_lo(pool, q_lo[:, h % 2, :], q32[:, h % 2, :], q_hi[:, h % 2, :]).then_inc(A["q_lo"], 1)

            def o_low(i, h):
                pool.wait_ge(*A("o_hi", 8 * i + h + 1))
                split_lo(pool, o_lo[:, h % 2, :], o32[:, :], o_hi[:, h % 2, :]).then_inc(A["o_lo"], 1)

            def heads(i, last):
                for h in range(HEADS):
                    if h:
                        o_low(i, h - 1)
                    if h < HEADS - 2:
                        q_low(i, h + 2)
                    elif h == HEADS - 1 and not last:
                        k_low(i + 1)
                        q_low(i + 1, 0)
                    if h == 1 and not last:
                        pool.wait_ge(*A("vp", i + 1))
                        pool.tensor_copy(xb_hi[:, :], xn_hi[:, bass.ds((i + 1) * T, T)].bitcast(F32)).then_inc(A["xb_hi"], 1)
                    if h == 3 and not last:
                        pool.tensor_copy(xb_lo[:, :], xn_lo[:, bass.ds((i + 1) * T, T)].bitcast(F32)).then_inc(A["xb_lo"], 1)
                o_low(i, HEADS - 1)
                if not last:
                    v_low(i + 1)
                    q_low(i + 1, 1)

            k_low(0)
            q_low(0, 0)
            v_low(0)
            q_low(0, 1)
            with pool.Fori(0, NB - 1) as i:
                heads(i, False)
            heads(NB - 1, True)

        FFN_CUTS = (W_G, W_H1, W_H2, NW)

        @block.sync
        def _(sp):
            sp.dma_start(x[:, 0:T], d["x"][:, 0:T]).then_inc(loaded, 16)
            sp.dma_start(x[:, T:NT], d["x"][:, T:NT]).then_inc(loaded, 16)
            sp.dma_start(cols[:, :], d["cols"]).then_inc(loaded, 16)
            for k in range(3):
                w = slice(FFN_CUTS[k], FFN_CUTS[k + 1])
                sp.dma_start(w_raw[:, w], d["ffn"][:, w]).then_inc(ffn_in[k], 16)
            sp.dma_start(const[:, :], d["const"]).then_inc(loaded, 16)
            sp.dma_start(rows[:, :], d["rows"]).then_inc(loaded, 16)
            sp.wait_ge(primed_all, 1)
            start_phase(sp, 1)
            sp.dma_start(m_raw[:, 0:NM], d["mixer"]).then_inc(M["raw_in"], 16)
            start_phase(sp, 3)
            moe_load_small(sp, E1)
            sp.dma_start(a_raw[:, :], d["attn"]).then_inc(a_in, 16)
            moe_load(sp, E1)
            start_phase(sp, 5)
            moe_load_small(sp, E2)
            moe_load(sp, E2)
            start_phase(sp, 6)
            sp.dma_start(d["out"], x[:, :]).then_inc(stored, 16)
            sp.wait_ge(stored, 16)

        @block.tensor
        def _(pe):
            pe.wait_ge(primed_all, 1)
            pe.wait_ge(ones_set, 1)
            pe.wait_ge(loaded, 80)
            ln_pe(pe, LN[0])
            pe.wait_ge(w_split, 4)
            ffn_pe(pe, F1, LN[0])
            end_phase(pe)
            start_phase(pe, 1)
            ln_pe(pe, LN[1])
            mix_pe(pe, LN[1])
            end_phase(pe)
            start_phase(pe, 2)
            ln_pe(pe, LN[2])
            ffn_pe(pe, F2, LN[2])
            end_phase(pe)
            start_phase(pe, 3)
            ln_pe(pe, LN[3])
            moe_pe(pe, E1, LN[3])
            end_phase(pe)
            start_phase(pe, 4)
            ln_pe(pe, LN[4])
            att_pe(pe, LN[4])
            end_phase(pe)
            start_phase(pe, 5)
            ln_pe(pe, LN[5])
            moe_pe(pe, E2, LN[5])
            end_phase(pe)

        @block.scalar
        def _(act):
            act.wait_ge(primed_all, 1)
            act.wait_ge(loaded, 80)
            act.wait_ge(ones_set, 3)
            ln_act(act, LN[0])
            act.wait_ge(ffn_in[2], 16)
            split_hi(act, wh[:, W_H2:NW], w_raw[:, W_H2:NW]).then_inc(w_hi_c, 1)
            ffn_act(act, F1)
            end_phase(act)
            start_phase(act, 1)
            act.wait_ge(*M("raw_in", 16))
            split_hi(act, mh[:, :], m_raw[:, 0:NM]).then_inc(M["w_hi"], 1)
            ln_act(act, LN[1])
            mix_act(act)
            end_phase(act)
            start_phase(act, 2)
            ln_act(act, LN[2])
            ffn_act(act, F2)
            end_phase(act)
            start_phase(act, 3)
            moe_act(act, E1)
            ln_act(act, LN[3])
            act.wait_ge(a_in, 16)
            split_hi(act, ah[:, :], a_raw[:, :]).then_inc(a_hi, 1)
            moe_act_tiles(act, E1)
            end_phase(act)
            start_phase(act, 4)
            ln_act(act, LN[4])
            att_act(act)
            end_phase(act)
            start_phase(act, 5)
            moe_act(act, E2)
            ln_act(act, LN[5])
            moe_act_tiles(act, E2)
            end_phase(act)

        @block.vector
        def _(dve):
            dve.wait_ge(primed_all, 1)
            dve.memset(mean_w[:, :], 1.0 / P).then_inc(ones_set, 1)
            dve.wait_ge(loaded, 80)
            dve.tensor_scalar(w3_half[:, :], cols[:, C_W3:C_W3 + 1], 0.5, None, ALU.mult).then_inc(ones_set, 1)
            dve.memset(cols[:, C_EPS:C_EPS + 1], EPS).then_inc(ones_set, 1)
            dve.wait_ge(ones_set, 3)
            for k in range(2):
                w = slice(FFN_CUTS[k], FFN_CUTS[k + 1])
                dve.wait_ge(ffn_in[k], 16)
                dve.tensor_copy(wh[:, w], w_raw[:, w]).then_inc(w_split, 1)
                dve.wait_ge(w_split, 2 * k + 1)
                split_lo(dve, wl[:, w], w_raw[:, w], wh[:, w]).then_inc(w_split, 1)
            ln_dve(dve, LN[0])
            ffn_dve(dve, F1)
            end_phase(dve)
            start_phase(dve, 1)
            ln_dve(dve, LN[1])
            mix_dve(dve)
            end_phase(dve)
            start_phase(dve, 2)
            ln_dve(dve, LN[2])
            ffn_dve(dve, F2)
            end_phase(dve)
            start_phase(dve, 3)
            ln_dve(dve, LN[3])
            moe_dve(dve, E1)
            end_phase(dve)
            start_phase(dve, 4)
            ln_dve(dve, LN[4])
            att_dve(dve, LN[4])
            end_phase(dve)
            start_phase(dve, 5)
            ln_dve(dve, LN[5])
            moe_dve(dve, E2)
            end_phase(dve)

        @block.gpsimd
        def _(pool):
            for signal in primed:
                pool.sem_inc(signal, 1)
            pool.sem_inc(primed_all, 1)
            ln_pool(pool, LN[0])
            pool.wait_ge(w_hi_c, 1)
            split_lo(pool, wl[:, W_H2:NW], w_raw[:, W_H2:NW], wh[:, W_H2:NW]).then_inc(w_split_c, 1)
            end_phase(pool)
            start_phase(pool, 1)
            pool.memset(bc[4 * DS:P, :].bitcast(F32), 0.0).then_inc(M["bc_zero"], 1)
            pool.wait_ge(*M("bc_zero", 1))
            pool.wait_ge(*M("w_hi", 1))
            split_lo(pool, ml[:, :], m_raw[:, 0:NM], mh[:, :]).then_inc(M["w_lo"], 1)
            ln_pool(pool, LN[1])
            mix_pool(pool)
            end_phase(pool)
            start_phase(pool, 2)
            ln_pool(pool, LN[2])
            end_phase(pool)
            start_phase(pool, 3)
            moe_pool(pool, E1)
            ln_pool(pool, LN[3])
            pool.wait_ge(a_hi, 1)
            split_lo(pool, al[:, :], a_raw[:, :], ah[:, :]).then_inc(a_lo, 1)
            moe_pool_tiles(pool, E1)
            end_phase(pool)
            start_phase(pool, 4)
            ln_pool(pool, LN[4])
            att_pool(pool)
            end_phase(pool)
            start_phase(pool, 5)
            moe_pool(pool, E2)
            ln_pool(pool, LN[5])
            moe_pool_tiles(pool, E2)
            end_phase(pool)


def constants():
    k = np.zeros((P, NCONST), np.float32)
    p = np.arange(P)
    k[:, K_ID:K_ID + P] = np.eye(P)
    k[:, K_MASK:K_MASK + P] = np.where(p[None, :] > p[:, None], MASKED, 0.0)
    inv_freq = np.exp(np.float32(-np.log(10000.0)) * np.arange(0, P, 2, dtype=np.float32) / np.float32(P))
    ang = np.arange(T, dtype=np.float32)[:, None] * inv_freq.astype(np.float32)[None, :]
    k[0::2, K_PE:K_PE + T] = np.sin(ang).T
    k[1::2, K_PE:K_PE + T] = np.cos(ang).T
    g = np.arange(NG)
    k[:, K_TIE:K_TIE + E] = (g[None, :] < g[:, None]).reshape(-1)
    k[:2 * 2 * DS, K_ID32:K_ID32 + 2 * DS] = p[:2 * 2 * DS, None] % 32 == np.arange(2 * DS)[None, :]
    expert = np.arange(E * I) // I
    pick = (p[:, None] % E == expert[None, :]).astype(np.float32)
    return k, np.ascontiguousarray(pick.reshape(P, CH, P).transpose(1, 0, 2))


def kernel(**a):
    import concourse.bacc as bacc
    from concourse.bass_utils import run_bass_kernel_spmd

    a = {k: np.asarray(v) for k, v in a.items()}
    f, m, t, r = "L0_ffn_", "L0_attn_", "L1_attn_", "L1_ffn_"

    def chunks(w):
        return w.reshape(-1, P, w.shape[-1]).transpose(1, 0, 2).reshape(P, -1)

    def column(v):
        return v.reshape(-1, P).T

    arrays = {
        "x": a[m + "x"].reshape(NT, P).T,
        "ffn": np.concatenate([a[f + "w1_w"].T, a[f + "w2_w"].T, chunks(a[f + "h1_w"].T), chunks(a[f + "h2_w"].T),
                               chunks(a[f + "w3_w"].T)], axis=1),
        "mixer": np.concatenate([a[m + "in_proj_w"].T, chunks(a[m + "x_proj_w"].T), chunks(a[m + "out_proj_w"].T)], axis=1),
        "attn": np.concatenate([a[t + "Wq"], a[t + "Wkv"], chunks(a[t + "Wo"])], axis=1),
        "l1_small": np.concatenate([a[r + "gate_w"].T, a[r + "Sg"].T, a[r + "Su"].T], axis=1),
        "sd": a[r + "Sd"].T.reshape(2, I, P).transpose(1, 0, 2),
        "experts": np.stack([a[r + "Wd"].transpose(0, 2, 1).reshape(CH, P, P),
                             a[r + "Wg"].reshape(CH, P, P).transpose(0, 2, 1),
                             a[r + "Wu"].reshape(CH, P, P).transpose(0, 2, 1)], axis=2),
        "cols": np.concatenate(
            [column(a[f + n]) for n in ("w1_s", "w2_s", "h1_s", "h2_s", "w3_s")]
            + [a[m + "conv_w"].reshape(MC, P, 4).transpose(1, 0, 2).reshape(P, -1), column(a[m + "conv_b"]),
               column(a[m + "dt_proj_w"].reshape(-1)), column(a[m + "dt_proj_b"]), column(a[m + "D"]),
               a[m + "A_log"].reshape(MC, P, DS).transpose(1, 0, 2).reshape(P, -1),
               column(a[t + "bq"]), column(a[t + "bkv"][:P]), np.zeros((P, 1), np.float32)], axis=1),
        "rows": np.concatenate([np.broadcast_to(a[r + "gate_bias"], (P, E)), np.broadcast_to(a[t + "bkv"][P:], (P, P))], axis=1),
    }
    arrays["const"], arrays["pick"] = constants()
    arrays = {f"in_{k}": np.ascontiguousarray(v) for k, v in arrays.items()}

    nc = bacc.Bacc("TRN2", target_bir_lowering=False, num_devices=1)
    d = {k[3:]: nc.dram_tensor(k, v.shape, F32, kind="ExternalInput").ap() for k, v in arrays.items()}
    d["out"] = nc.dram_tensor("out", (P, NT), F32, kind="ExternalOutput").ap()
    program(nc, d)
    got = run_bass_kernel_spmd(nc, [arrays], core_ids=[0]).results[0]["out"]
    return np.ascontiguousarray(got.T).reshape(NB, T, P)
```

```python
from contextlib import ExitStack

import numpy as np

import concourse.bass as bass
from concourse import mybir

P = 128
T = 512
NB = 4
NT = T * NB
HID = 512
HC = HID // P
DS = 16
MC = 2
HEADS = 8
E, I = 64, 88
NG = 8
CH = E * I // P
PAIRS = CH // 2
NTT = NT // P
EPS = 1e-5
MASKED = 1e30
GONE = -3e38

F32 = mybir.dt.float32
F32R = mybir.dt.float32r
ACT = mybir.ActivationFunctionType
ALU = mybir.AluOpType
AX = mybir.AxisListType.X

C_W1, C_W2, C_H1, C_H2, C_W3 = 0, 4, 8, 12, 16
C_CONV, C_CB, C_DTW, C_DTB, C_D = 17, 25, 27, 29, 31
C_ALOG, C_BQ, C_BK, C_EPS = 33, 65, 73, 74
NCOL = 75
R_GB, R_BV, NROW = 0, 64, 192
K_ID, K_MASK, K_PE, K_TIE, K_ID64, K_ID32, NCONST = 0, 128, 256, 768, 832, 896, 928
W_G, W_U, W_H1, W_H2, W_3, NW = 0, 512, 1024, 3072, 5120, 5632
M_IN, M_X, M_OUT, NM = 0, 512, 578, 834
A_Q, A_K, A_V, A_O, NA = 0, 1024, 1152, 1280, 2304
S_R, S_G, S_U, NS = 0, 64, 240, 416


def program(nc, d):
    ctx = ExitStack()
    with ctx:
        def keeper(stack):
            return lambda name, shape, dt=F32: stack.enter_context(nc.sbuf_tensor(name, shape, dt))

        def sem(name):
            return ctx.enter_context(nc.semaphore(name))

        sb = keeper(ctx)
        x = sb("x", [P, NT])
        with ExitStack() as s:
            m_h = keeper(s)("m_h", [P, 4, T])
            m_hc = keeper(s)("m_hc", [P, 4, T])
        xn_hi = sb("xn_hi", [P, NT], F32R)
        xn_lo = sb("xn_lo", [P, NT], F32R)
        ln_c = sb("ln_c", [P, NT])
        ln_t = sb("ln_t", [P, NT])
        cols = sb("cols", [P, NCOL])
        rows = sb("rows", [P, NROW])
        const = sb("const", [P, NCONST])
        mean_w = sb("mean_w", [P, P])
        rstd = sb("rstd", [P, NTT])
        unused = sb("unused", [P, 1])
        w3_half = sb("w3_half", [P, 1])
        neg_a = sb("neg_a", [P, MC * DS])

        with ExitStack() as layer:
            lb = keeper(layer)
            wh, wl = lb("wh", [P, NW], F32R), lb("wl", [P, NW], F32R)
            with ExitStack() as s:
                fb = keeper(s)
                w_raw = fb("w_raw", [P, NW])
                f_s = fb("f_s", [P, HC, T])
                f_h = fb("f_h", [P, HC, T])
                hid_hi = fb("hid_hi", [P, 3, HC, T], F32R)
                hid_lo = fb("hid_lo", [P, 3, HC, T], F32R)
            with ExitStack() as s:
                fb = keeper(s)
                m_raw = fb("m_raw", [P, 2 * T])
                dt_b = m_raw[:, :].rearrange("p (m t) -> p m t", m=MC)
                mh, ml = fb("mh", [P, NM], F32R), fb("ml", [P, NM], F32R)
                dtw_hi = fb("dtw_hi", [P, MC, P], F32R)
                dtw_lo = fb("dtw_lo", [P, MC, P], F32R)
                sel_bc = fb("sel_bc", [P, 2 * DS, P], F32R)
                bc = fb("bc", [P, NT], F32R)
                xc = fb("xc", [P, MC, NT])
                sz = fb("sz", [P, MC, NT])
                dt = fb("dt", [P, MC, NT])
                du = fb("du", [P, MC, NT])
                g_hi = fb("g_hi", [P, MC, T], F32R)
                g_lo = fb("g_lo", [P, MC, T], F32R)
                m_y = fb("m_y", [P, MC, T])
                m_c = fb("m_c", [P, 2, T])
                m_db = ln_c[:, :].rearrange("p (k t) -> p k t", k=4)
                m_da = ln_t[:, :].rearrange("p (k t) -> p k t", k=4)
        with ExitStack() as layer:
            lb = keeper(layer)
            ah, al = lb("ah", [P, NA], F32R), lb("al", [P, NA], F32R)
            sh, sl = lb("sh", [P, NS], F32R), lb("sl", [P, NS], F32R)
            sd_h, sd_l = lb("sd_h", [I, 2, P], F32R), lb("sd_l", [I, 2, P], F32R)
            with ExitStack() as s:
                fb = keeper(s)
                a_raw = fb("a_raw", [P, NA])
                e_raw = fb("e_raw", [P, 2, 4, P])
                eh, el = fb("eh", [P, 2, 4, P], F32R), fb("el", [P, 2, 3, P], F32R)
                rwt = fb("rwt", [P, NT], F32R)
                s_raw = fb("s_raw", [P, NS])
                sd_raw = fb("sd_raw", [I, 2, P])
                r_s = fb("r_s", [P, NTT, E])
                r_c = fb("r_c", [P, NTT, E])
                r_t = fb("r_t", [P, NTT * E])
                r_u = fb("r_u", [P, NTT * E])
                r_small = fb("r_small", [P, 4, NTT * NG])
                rw_cat = fb("rw_cat", [P, NTT, 2, E])
                e_s = fb("e_s", [P, 4, T])
                e_p = fb("e_p", [P, 2, T])
                e_h = fb("e_h", [P, 4, T])
                e_hi = fb("e_hi", [P, 4, T], F32R)
                e_lo = fb("e_lo", [P, 4, T], F32R)
            with ExitStack() as s:
                fb = keeper(s)
                xb_hi, xb_lo = fb("xb_hi", [P, T], F32R), fb("xb_lo", [P, T], F32R)
                k_hi, k_lo = fb("k_hi", [P, T], F32R), fb("k_lo", [P, T], F32R)
                v_hi, v_lo = fb("v_hi", [P, 4, P], F32R), fb("v_lo", [P, 4, P], F32R)
                kv32 = fb("kv32", [P, 2, T])
                q32 = fb("q32", [P, 2, T])
                q_hi, q_lo = fb("q_hi", [P, 2, T], F32R), fb("q_lo", [P, 2, T], F32R)
                p32 = fb("p32", [P, 4, T])
                pt_hi, pt_lo = fb("pt_hi", [P, 3, T], F32R), fb("pt_lo", [P, 3, T], F32R)
                o_hi, o_lo = fb("o_hi", [P, 2, T], F32R), fb("o_lo", [P, 2, T], F32R)
                o32 = fb("o32", [P, T])
                k_add = fb("k_add", [P, T])
                st = fb("st", [P, 2, 3, 4])
                maskr, idr = fb("maskr", [P, P], F32R), fb("idr", [P, P], F32R)

        ps = ctx.enter_context(nc.psum_tensor("ps", [P, 8, T], F32))
        ident = const[:, K_ID:K_ID + P]

        loaded = sem("loaded")
        loaded_late = sem("loaded_late")
        ffn_in = [sem(f"ffn_in{k}") for k in range(3)]
        ones_set = sem("ones_set")
        w_split = sem("w_split")
        w_hi_c = sem("w_hi_c")
        w_split_c = sem("w_split_c")
        stored = sem("stored")
        phase_end = sem("phase_end")
        a_in, a_hi, a_lo = sem("a_in"), sem("a_hi"), sem("a_lo")

        class Signals:

            def __init__(self, sems, base):
                self.sems, self.base = sems, base

            def __getitem__(self, name):
                return self.sems[name]

            def __call__(self, name, n):
                return self.sems[name], self.base[name] + n

        def group(tag, counts, runs):
            sems = {n: sem(f"{tag}_{n}") for n in counts}
            primed.extend(sems.values())
            return [Signals(sems, {n: 1 + k * c for n, c in counts.items()}) for k in range(runs)]

        primed, primed_all = [], sem("primed_all")

        TILES = 2 * NB + CH * NB
        ROUTE_STEPS = 25
        LN = group("ln", dict.fromkeys("mean centred squared var dev inv diag spread normed xn_hi xn_lo".split(), NB), 6)
        F1, F2 = group("ffn", {"gate": 4 * NB, "up": 4 * NB, "silu": 4 * NB, "hidden": 4 * NB, "mid": 8 * NB, "gelu": 8 * NB,
                               "hid_hi": 12 * NB, "hid_lo": 12 * NB, "out": NB, "x_new": NB}, 2)
        E1, E2 = group("moe", {"raw_in0": 32 * PAIRS, "raw_in1": 32 * PAIRS, "small_in": 32, "small_hi": 2, "small_lo": 2,
                               "logits": 2, "scores": 2, "route": ROUTE_STEPS, "routed": 2, "rw_t": 4, "rwt": 4,
                               "spread": CH * NB, "w_hi": 2 * CH, "w_lo": 2 * CH, "x_new": NB}
                       | dict.fromkeys("gate up silu gated weighted h_hi h_lo down".split(), TILES), 2)
        M, = group("mix", dict.fromkeys((
            "raw_in w_hi w_lo dt_w sel_set inproj zproj biased conv xc sz xc_hi xc_lo bcdt "
            "bc_hi bc_lo v nabs e ln dt du b_spread c_spread da db h c_copy hc y_sum ylin "
            "gated g_hi g_lo out x_new aexp bc_zero dt_b").split(), 0), 1)
        A, = group("att", dict.fromkeys((
            "mask k_add xb_hi xb_lo kp vp k32 k_hi k_lo v32 v_hi v_lo qp q32 q_hi q_lo s "
            "min p inv pn pt pt_hi pt_lo o o32 o_hi o_lo y x_new").split(), 0), 1)

        block = ctx.enter_context(nc.Block())

        def end_phase(eng):
            eng.drain().then_inc(phase_end, 1)

        def start_phase(eng, k):
            eng.wait_ge(phase_end, 4 * k)

        def cut(b):
            return slice(b * T, (b + 1) * T)

        def mm3(pe, out, w_hi, w_lo, x_hi, x_lo, start, stop):
            pe.matmul(out, w_hi, x_hi, start=start, stop=False, skip_group_check=True)
            pe.matmul(out, w_hi, x_lo, start=False, stop=False, skip_group_check=True)
            return pe.matmul(out, w_lo, x_hi, start=False, stop=stop, skip_group_check=True)

        def split_hi(act, hi, full):
            return act.activation(hi, full, ACT.Identity)

        def split_lo(eng, lo, full, hi):
            return eng.tensor_tensor(lo, full, hi.bitcast(F32), ALU.subtract)

        def ln_pe(pe, L):
            def mean(b):
                pe.matmul(ps[:, b, :], mean_w[:, :], x[:, cut(b)], start=True, stop=True).then_inc(L["mean"], 1)

            def var(b):
                pe.wait_ge(*L("squared", b + 1))
                for t in range(4):
                    tt = slice(b * T + t * P, b * T + (t + 1) * P)
                    last = pe.matmul(ps[:, 4 + b, t:t + 1], ln_t[:, tt], mean_w[:, 0:1], start=True, stop=True, skip_group_check=True)
                last.then_inc(L["var"], 1)

            def spread(b):
                pe.wait_ge(*L("diag", b + 1))
                pe.matmul(ps[:, 4 + b, :], mean_w[:, :], ln_t[:, cut(b)], start=True, stop=True).then_inc(L["spread"], 1)

            mean(0)
            mean(1)
            var(0)
            mean(2)
            var(1)
            spread(0)
            mean(3)
            var(2)
            spread(1)
            var(3)
            spread(2)
            spread(3)

        def banks_free(pe, L):
            pe.wait_ge(*L("centred", NB))
            pe.wait_ge(*L("normed", NB))

        def ln_dve(dve, L, between=lambda step: None):
            def centre(b):
                dve.wait_ge(*L("mean", b + 1))
                dve.tensor_tensor(ln_c[:, cut(b)], x[:, cut(b)], ps[:, b, :], ALU.subtract).then_inc(L["centred"], 1)

            def diagonal(b):
                r = rstd[:, 4 * b:4 * b + 4]
                dve.wait_ge(*L("dev", b + 1))
                dve.reciprocal(r, r).then_inc(L["inv"], 1)
                dve.wait_ge(*L("inv", b + 1))
                dve.scalar_tensor_tensor(ln_t[:, cut(b)].rearrange("p (t n) -> p t n", t=4), ident.unsqueeze(1).broadcast_to([P, 4, P]),
                                         float(P), r.unsqueeze(2).broadcast_to([P, 4, P]), ALU.mult, ALU.mult).then_inc(L["diag"], 1)

            def normalise(b):
                dve.wait_ge(*L("spread", b + 1))
                dve.tensor_tensor(ln_c[:, cut(b)], ln_c[:, cut(b)], ps[:, 4 + b, :], ALU.mult).then_inc(L["normed"], 1)

            centre(0)
            centre(1)
            diagonal(0)
            centre(2)
            diagonal(1)
            normalise(0)
            between(0)
            centre(3)
            diagonal(2)
            between(1)
            normalise(1)
            diagonal(3)
            between(2)
            normalise(2)
            between(3)
            normalise(3)

        def ln_act(act, L):
            def square(b):
                act.wait_ge(*L("centred", b + 1))
                act.activation(ln_t[:, cut(b)], ln_c[:, cut(b)], ACT.Square).then_inc(L["squared"], 1)

            def deviation(b):
                act.wait_ge(*L("var", b + 1))
                act.activation(rstd[:, 4 * b:4 * b + 4], ps[:, 4 + b, 0:4], ACT.Sqrt, bias=cols[:, C_EPS:C_EPS + 1]).then_inc(L["dev"], 1)

            def high(b):
                act.wait_ge(*L("normed", b + 1))
                split_hi(act, xn_hi[:, cut(b)], ln_c[:, cut(b)]).then_inc(L["xn_hi"], 1)

            square(0)
            square(1)
            deviation(0)
            square(2)
            deviation(1)
            high(0)
            square(3)
            deviation(2)
            high(1)
            deviation(3)
            high(2)
            high(3)

        def ln_pool(pool, L):
            for b in range(NB):
                pool.wait_ge(*L("xn_hi", b + 1))
                split_lo(pool, xn_lo[:, cut(b)], ln_c[:, cut(b)], xn_hi[:, cut(b)]).then_inc(L["xn_lo"], 1)

        MEAN_BANK, VAR_BANK, SPREAD_BANK = 4, 6, 7
        one_c, one_t, one_r = ln_c[:, 0:T], ln_t[:, 0:T], rstd[:, 0:4]

        def one_mean(pe, L, blk, bank=MEAN_BANK):
            pe.matmul(ps[:, bank, :], mean_w[:, :], x[:, blk], start=True, stop=True).then_inc(L["mean"], 1)

        def one_var(pe, L, b, bank=VAR_BANK):
            pe.wait_ge(*L("squared", b + 1))
            for t in range(4):
                last = pe.matmul(ps[:, bank, t:t + 1], one_t[:, t * P:(t + 1) * P], mean_w[:, 0:1], start=True, stop=True, skip_group_check=True)
            last.then_inc(L["var"], 1)

        def one_spread(pe, L, b, bank=SPREAD_BANK):
            pe.wait_ge(*L("diag", b + 1))
            pe.matmul(ps[:, bank, :], mean_w[:, :], one_t, start=True, stop=True).then_inc(L["spread"], 1)

        def one_centre(dve, L, b, blk, bank=MEAN_BANK):
            dve.wait_ge(*L("mean", b + 1))
            dve.wait_ge(*L("xn_lo", b))
            dve.tensor_tensor(one_c, x[:, blk], ps[:, bank, :], ALU.subtract).then_inc(L["centred"], 1)

        def one_diagonal(dve, L, b):
            dve.wait_ge(*L("dev", b + 1))
            dve.reciprocal(one_r, one_r).then_inc(L["inv"], 1)
            dve.wait_ge(*L("inv", b + 1))
            dve.scalar_tensor_tensor(one_t.rearrange("p (t n) -> p t n", t=4), ident.unsqueeze(1).broadcast_to([P, 4, P]),
                                     float(P), one_r.unsqueeze(2).broadcast_to([P, 4, P]), ALU.mult, ALU.mult).then_inc(L["diag"], 1)

        def one_normalise(dve, L, b, bank=SPREAD_BANK):
            dve.wait_ge(*L("spread", b + 1))
            dve.tensor_tensor(one_c, one_c, ps[:, bank, :], ALU.mult).then_inc(L["normed"], 1)

        def one_square(act, L, b):
            act.wait_ge(*L("centred", b + 1))
            act.activation(one_t, one_c, ACT.Square).then_inc(L["squared"], 1)

        def one_deviation(act, L, b, bank=VAR_BANK):
            act.wait_ge(*L("var", b + 1))
            act.activation(one_r, ps[:, bank, 0:4], ACT.Sqrt, bias=cols[:, C_EPS:C_EPS + 1]).then_inc(L["dev"], 1)

        def one_high(act, L, b, blk):
            act.wait_ge(*L("normed", b + 1))
            act.wait_ge(primed_all, 1)
            split_hi(act, xn_hi[:, blk], one_c).then_inc(L["xn_hi"], 1)

        def one_low(pool, L, b, blk):
            pool.wait_ge(*L("xn_hi", b + 1))
            split_lo(pool, xn_lo[:, blk], one_c, xn_hi[:, blk]).then_inc(L["xn_lo"], 1)

        LAST = NB - 1

        def last_dve(dve, L):
            one_centre(dve, L, LAST, cut(LAST))
            one_diagonal(dve, L, LAST)
            one_normalise(dve, L, LAST)

        def last_act(act, L):
            one_square(act, L, LAST)
            one_deviation(act, L, LAST)
            one_high(act, L, LAST, cut(LAST))

        def ffn_blocks(eng, block_):
            block_(0, cut(0), None)
            with eng.Fori(1, NB) as i:
                block_(i, bass.ds(i * T, T), bass.ds((i - 1) * T, T))

        def ffn_pe(pe, S, L, N):
            def block_(i, blk, before):
                pe.wait_ge(*L("xn_lo", i + 1))
                for o in range(HC):
                    g = slice(W_G + o * P, W_G + (o + 1) * P)
                    u = slice(W_U + o * P, W_U + (o + 1) * P)
                    if o == 3:
                        pe.wait_ge(*S("x_new", i))
                    mm3(pe, ps[:, o, :], wh[:, g], wl[:, g], xn_hi[:, blk], xn_lo[:, blk], True, True).then_inc(S["gate"], 1)
                    mm3(pe, ps[:, 4 + o, :], wh[:, u], wl[:, u], xn_hi[:, blk], xn_lo[:, blk], True, True).then_inc(S["up"], 1)
                for layer_, (w0, bank) in enumerate(((W_H1, 0), (W_H2, 4))):
                    if S is F1 and layer_ == 1:
                        pe.wait_ge(w_split_c, 1)
                    for k in range(HC):
                        pe.wait_ge(*S("hid_lo", 12 * i + 4 * layer_ + k + 1))
                        if before is not None and layer_ == 0:
                            if k == 0:
                                one_mean(pe, N, before)
                            if k == 2:
                                one_var(pe, N, i - 1)
                            if k == 3:
                                one_spread(pe, N, i - 1)
                        for o in range(HC):
                            if layer_ == 0 and k == 0:
                                pe.wait_ge(*S("silu", 4 * i + o + 1))
                            if before is not None and layer_ == 1 and k == 0 and o == 3:
                                pe.wait_ge(*N("normed", i))
                            w = slice(w0 + k * HID + o * P, w0 + k * HID + (o + 1) * P)
                            last = mm3(pe, ps[:, bank + o, :], wh[:, w], wl[:, w], hid_hi[:, layer_, k, :],
                                       hid_lo[:, layer_, k, :], k == 0, k == HC - 1)
                            if k == HC - 1:
                                last.then_inc(S["mid"], 1)
                for k in range(HC):
                    pe.wait_ge(*S("hid_lo", 12 * i + 8 + k + 1))
                    w = slice(W_3 + k * P, W_3 + (k + 1) * P)
                    last = mm3(pe, ps[:, 3, :], wh[:, w], wl[:, w], hid_hi[:, 2, k, :], hid_lo[:, 2, k, :], k == 0, k == HC - 1)
                last.then_inc(S["out"], 1)

            banks_free(pe, L)
            ffn_blocks(pe, block_)

        def ffn_act(act, S, N):
            def block_(i, blk, before):
                for o in range(HC):
                    act.wait_ge(*S("gate", 4 * i + o + 1))
                    act.activation(f_s[:, o, :], ps[:, o, :], ACT.Silu, scale=cols[:, C_W1 + o:C_W1 + o + 1]).then_inc(S["silu"], 1)
                if before is not None:
                    one_square(act, N, i - 1)
                    one_deviation(act, N, i - 1)
                act.activation(unused[:, :], cols[:, 0:1], ACT.Gelu)
                for layer_, (c0, bank) in enumerate(((C_H1, 0), (C_H2, 4))):
                    for o in range(HC):
                        act.wait_ge(*S("mid", 8 * i + 4 * layer_ + o + 1))
                        act.wait_ge(*S("hid_lo", 12 * i + 4 * layer_ + o + 1))
                        act.activation(f_h[:, o, :], ps[:, bank + o, :], ACT.Gelu, scale=cols[:, c0 + o:c0 + o + 1]).then_inc(S["gelu"], 1)
                    if before is not None and layer_ == 0:
                        one_high(act, N, i - 1, before)
                act.activation(unused[:, :], cols[:, 0:1], ACT.Silu)

            ffn_blocks(act, block_)

        def ffn_dve(dve, S, N):
            def split(i, layer_, o):
                q = 4 * layer_ + o
                dve.tensor_copy(hid_hi[:, layer_, o, :], f_h[:, o, :]).then_inc(S["hid_hi"], 1)
                dve.wait_ge(*S("hid_hi", 12 * i + q + 1))
                split_lo(dve, hid_lo[:, layer_, o, :], f_h[:, o, :], hid_hi[:, layer_, o, :]).then_inc(S["hid_lo"], 1)

            def block_(i, blk, before):
                for o in range(HC):
                    dve.wait_ge(*S("up", 4 * i + o + 1))
                    dve.wait_ge(*S("silu", 4 * i + o + 1))
                    dve.scalar_tensor_tensor(f_h[:, o, :], ps[:, 4 + o, :], cols[:, C_W2 + o:C_W2 + o + 1], f_s[:, o, :],
                                             ALU.mult, ALU.mult).then_inc(S["hidden"], 1)
                    dve.wait_ge(*S("hidden", 4 * i + o + 1))
                    split(i, 0, o)
                    if before is not None and o == 0:
                        one_centre(dve, N, i - 1, before)
                if before is not None:
                    one_diagonal(dve, N, i - 1)
                    one_normalise(dve, N, i - 1)
                for layer_ in (1, 2):
                    for o in range(HC):
                        dve.wait_ge(*S("gelu", 8 * i + 4 * (layer_ - 1) + o + 1))
                        split(i, layer_, o)
                dve.wait_ge(*S("out", i + 1))
                dve.scalar_tensor_tensor(x[:, blk], ps[:, 3, :], w3_half[:, :], x[:, blk], ALU.mult, ALU.add).then_inc(S["x_new"], 1)

            ffn_blocks(dve, block_)

        def ffn_pool(pool, N):
            with pool.Fori(0, NB - 1) as i:
                one_low(pool, N, i, bass.ds(i * T, T))

        ITEMS, HEAD = DS * MC, 8
        DEEP = 4

        def after(eng, name, n):
            if not isinstance(n, int) or n > 0:
                eng.wait_ge(*M(name, n))

        def scan_blocks(eng, item, finish):
            for q in range(HEAD):
                item(0, cut(0), q, False)
            with eng.Fori(0, NB - 1) as i:
                blk, following = bass.ds(i * T, T), bass.ds((i + 1) * T, T)
                for q in range(HEAD, ITEMS):
                    item(i, blk, q, False)
                for q in range(HEAD):
                    item(i + 1, following, q, False)
                    finish(i, blk, q)
            for q in range(HEAD, ITEMS):
                item(NB - 1, cut(NB - 1), q, True)
            for q in range(HEAD):
                finish(NB - 1, cut(NB - 1), q)

        def mix_pe(pe, L):
            def in_proj(i, blk):
                after(pe, "conv", 6 * i)
                after(pe, "sz", 2 * i)
                for o in range(2 * MC):
                    w = slice(M_IN + o * P, M_IN + (o + 1) * P)
                    mm3(pe, ps[:, o, :], mh[:, w], ml[:, w], xn_hi[:, blk], xn_lo[:, blk], True, True)\
                        .then_inc(M["inproj"] if o < MC else M["zproj"], 1)

            def x_proj(i):
                for m in range(MC):
                    pe.wait_ge(*M("xc_lo", 2 * i + m + 1))
                    if m == 0:
                        after(pe, "bc_lo", i)
                        after(pe, "v", 2 * i)
                    w = slice(M_X + 33 * m + 1, M_X + 33 * m + 33)
                    mm3(pe, ps[0:2 * DS, 4, :], mh[:, w], ml[:, w], g_hi[:, m, :], g_lo[:, m, :], m == 0, m == MC - 1)
                    last = mm3(pe, ps[:, 5, :], dtw_hi[:, m, :], dtw_lo[:, m, :], g_hi[:, m, :], g_lo[:, m, :], m == 0, m == MC - 1)
                last.then_inc(M["bcdt"], 1)

            one_mean(pe, L, cut(LAST))
            pe.wait_ge(*M("w_lo", 1))
            in_proj(0, cut(0))
            one_var(pe, L, LAST)
            one_spread(pe, L, LAST)
            pe.wait_ge(*M("dt_w", 2))
            pe.wait_ge(*L("xn_lo", NB))
            with pe.Fori(0, NB - 1) as i:
                in_proj(i + 1, bass.ds((i + 1) * T, T))
                x_proj(i)
            x_proj(NB - 1)

            def spread(i, blk, n):
                after(pe, "db", 32 * i + 2 * n - 2)
                pe.matmul(ps[:, n % 2, :], sel_bc[:, n, :], bc[:, blk], start=True, stop=True).then_inc(M["b_spread"], 1)
                after(pe, "c_copy", 16 * i + n - 1)
                pe.matmul(ps[:, 2 + n % 2, :], sel_bc[:, DS + n, :], bc[:, blk], start=True, stop=True).then_inc(M["c_spread"], 1)

            def item(i, blk, q, last):
                n, m = q // MC, q % MC
                if m == 1 and n + 2 < DS:
                    spread(i, blk, n + 2)
                elif m == 1 and not last:
                    spread(i + 1, bass.ds((i + 1) * T, T), n + 2 - DS)
                if n == 0:
                    after(pe, "ylin", 2 * i + m - 1)
                pe.wait_ge(*M("hc", 32 * i + q + 1))
                pe.matmul(ps[:, 4 + m, :], ident, m_hc[:, q % DEEP, :], start=(n == 0), stop=(n == DS - 1),
                          skip_group_check=True).then_inc(M["y_sum"], 1)

            def finish(i, blk, q):
                if q == 4:
                    after(pe, "x_new", i)
                    for m in range(MC):
                        pe.wait_ge(*M("g_lo", 2 * i + m + 1))
                        w = slice(M_OUT + m * P, M_OUT + (m + 1) * P)
                        last = mm3(pe, ps[:, 6, :], mh[:, w], ml[:, w], g_hi[:, m, :], g_lo[:, m, :], m == 0, m == MC - 1)
                    last.then_inc(M["out"], 1)

            pe.wait_ge(*M("sel_set", 1))
            pe.wait_ge(*M("bc_zero", 1))
            pe.wait_ge(*M("conv", 6 * NB))
            pe.wait_ge(*M("sz", 2 * NB))
            pe.wait_ge(*M("bc_lo", NB))
            pe.wait_ge(*M("v", 2 * NB))
            spread(0, cut(0), 0)
            spread(0, cut(0), 1)
            scan_blocks(pe, item, finish)

        def mix_act(act):
            def before_conv(i):
                for m in range(MC):
                    act.wait_ge(*M("inproj", 2 * i + m + 1))
                    after(act, "xc", 2 * (i - 1) + m + 1)
                    act.activation(m_y[:, m, :], ps[:, m, :], ACT.Identity, scale=cols[:, C_CONV + 4 * m + 3:C_CONV + 4 * m + 4],
                                   bias=cols[:, C_CB + m:C_CB + m + 1]).then_inc(M["biased"], 1)

            def silus(i, blk, out, name, source, done, count):
                for m in range(MC):
                    act.wait_ge(*M(done, count * (i * MC + m + 1)))
                    act.wait_ge(phase_end, 4)
                    act.activation(out[:, m, blk], source[:, m, :], ACT.Silu).then_inc(M[name], 1)

            def after_proj(i, blk):
                act.wait_ge(*M("bcdt", i + 1))
                act.wait_ge(phase_end, 4)
                act.activation(bc[0:2 * DS, blk], ps[0:2 * DS, 4, :], ACT.Identity).then_inc(M["bc_hi"], 1)
                for m in range(MC):
                    act.wait_ge(phase_end, 4)
                    act.activation(dt[:, m, blk], ps[:, 5, :], ACT.Identity, scale=cols[:, C_DTW + m:C_DTW + m + 1],
                                   bias=cols[:, C_DTB + m:C_DTB + m + 1]).then_inc(M["v"], 1)

            act.activation(unused[:, :], cols[:, 0:1], ACT.Silu)
            before_conv(0)
            silus(0, cut(0), sz, "sz", ps[:, MC:2 * MC, :], "zproj", 1)
            silus(0, cut(0), xc, "xc", m_y, "conv", 3)
            with act.Fori(0, NB - 1) as i:
                blk, following = bass.ds(i * T, T), bass.ds((i + 1) * T, T)
                before_conv(i + 1)
                silus(i + 1, following, sz, "sz", ps[:, MC:2 * MC, :], "zproj", 1)
                after_proj(i, blk)
                silus(i + 1, following, xc, "xc", m_y, "conv", 3)
            after_proj(NB - 1, cut(NB - 1))
            act.activation(neg_a[:, :], cols[:, C_ALOG:C_ALOG + MC * DS], ACT.Exp).then_inc(M["aexp"], 1)
            for b in range(NB):
                act.wait_ge(*M("nabs", b + 1))
                act.activation(du[:, :, cut(b)], du[:, :, cut(b)], ACT.Exp).then_inc(M["e"], 1)
            for b in range(NB):
                act.wait_ge(*M("e", b + 1))
                act.activation(du[:, :, cut(b)], du[:, :, cut(b)], ACT.Ln, bias=1.0).then_inc(M["ln"], 1)
            act.wait_ge(*M("aexp", 2))

            def item(i, blk, q, last):
                n, m = q // MC, q % MC
                if q == 0:
                    act.wait_ge(*M("dt_b", i + 1))
                after(act, "h", 32 * i + q + 1 - DEEP)
                act.activation(m_da[:, q % DEEP, :], dt_b[:, m, :], ACT.Exp,
                               scale=neg_a[:, m * DS + n:m * DS + n + 1]).then_inc(M["da"], 1)
                if m == 1:
                    act.wait_ge(*M("c_spread", 16 * i + n + 1))
                    after(act, "hc", 32 * i + 2 * n - 2)
                    act.activation(m_c[:, n % 2, :], ps[:, 2 + n % 2, :], ACT.Identity).then_inc(M["c_copy"], 1)

            def finish(i, blk, q):
                if q == 3:
                    after(act, "out", i)
                    for m in range(MC):
                        act.wait_ge(*M("gated", 2 * i + m + 1))
                        split_hi(act, g_hi[:, m, :], m_y[:, m, :]).then_inc(M["g_hi"], 1)

            scan_blocks(act, item, finish)

        def mix_dve(dve):
            dve.wait_ge(*M("w_lo", 1))
            for half, (src, dst) in enumerate(((mh, dtw_hi), (ml, dtw_lo))):
                v = src[:, M_X:M_X + 66].rearrange("p (m c) -> p m c", m=MC)[:, :, 0:1].bitcast(F32)
                dve.tensor_copy(dst[:, :, :], v.broadcast_to([P, MC, P])).then_inc(M["dt_w"], 1)

            def conv(i):
                for m in range(MC):
                    dve.wait_ge(*M("biased", 2 * i + m + 1))
                    for s_, j in enumerate((2, 1, 0)):
                        back = 3 - j
                        after(dve, "conv", 6 * i + 3 * m + s_)
                        dve.scalar_tensor_tensor(m_y[:, m, back:T], ps[:, m, 0:T - back], cols[:, C_CONV + 4 * m + j:C_CONV + 4 * m + j + 1],
                                                 m_y[:, m, back:T], ALU.mult, ALU.add).then_inc(M["conv"], 1)

            def split(i, blk):
                for m in range(MC):
                    dve.wait_ge(*M("xc", 2 * i + m + 1))
                    after(dve, "bcdt", i)
                    dve.tensor_copy(g_hi[:, m, :], xc[:, m, blk]).then_inc(M["xc_hi"], 1)
                    dve.wait_ge(*M("xc_hi", 2 * i + m + 1))
                    split_lo(dve, g_lo[:, m, :], xc[:, m, blk], g_hi[:, m, :]).then_inc(M["xc_lo"], 1)

            def after_proj(i, blk):
                dve.wait_ge(*M("bc_hi", i + 1))
                split_lo(dve, bc[2 * DS:4 * DS, blk], ps[0:2 * DS, 4, :], bc[0:2 * DS, blk]).then_inc(M["bc_lo"], 1)
                dve.wait_ge(*M("v", 2 * i + 2))
                dve.scalar_tensor_tensor(du[:, :, blk], dt[:, :, blk], -1.0, dt[:, :, blk], ALU.mult, ALU.min).then_inc(M["nabs"], 1)

            conv(0)
            with dve.Fori(0, NB - 1) as i:
                blk = bass.ds(i * T, T)
                split(i, blk)
                conv(i + 1)
                after_proj(i, blk)
            split(NB - 1, cut(NB - 1))
            after_proj(NB - 1, cut(NB - 1))
            dve.wait_ge(*M("aexp", 1))
            dve.tensor_scalar(neg_a[:, :], neg_a[:, :], -1.0, None, ALU.mult).then_inc(M["aexp"], 1)

            def dt_copy(i, blk):
                dve.tensor_copy(dt_b, dt[:, :, blk]).then_inc(M["dt_b"], 1)

            def softplus_end(b):
                dve.wait_ge(*M("ln", b + 1))
                dve.scalar_tensor_tensor(dt[:, :, cut(b)], dt[:, :, cut(b)], 0.0, du[:, :, cut(b)], ALU.max, ALU.add).then_inc(M["dt"], 1)

            def dt_times_xc(b):
                dve.wait_ge(*M("dt", b + 1))
                dve.tensor_tensor(du[:, :, cut(b)], dt[:, :, cut(b)], xc[:, :, cut(b)], ALU.mult).then_inc(M["du"], 1)

            softplus_end(0)
            dve.wait_ge(*M("dt", 1))
            dt_copy(0, cut(0))
            dt_times_xc(0)

            def input_term(i, blk, q):
                n, m = q // MC, q % MC
                after(dve, "h", 32 * i + q + 1 - DEEP)
                dve.wait_ge(*M("b_spread", 16 * i + n + 1))
                dve.tensor_tensor(m_db[:, q % DEEP, :], du[:, m, blk], ps[:, n % 2, :], ALU.mult).then_inc(M["db"], 1)

            def item(i, blk, q, last):
                following = bass.ds((i + 1) * T, T)
                if q == ITEMS - 2 and not last:
                    dve.wait_ge(*M("da", 32 * i + ITEMS))
                    dt_copy(i + 1, following)
                if q + 1 < ITEMS:
                    input_term(i, blk, q + 1)
                elif not last:
                    input_term(i + 1, following, 0)
                dve.wait_ge(*M("da", 32 * i + q + 1))
                dve.wait_ge(*M("db", 32 * i + q + 1))
                after(dve, "hc", 32 * i + q + 1 - DEEP)
                dve.tensor_tensor_scan(m_h[:, q % DEEP, :], m_da[:, q % DEEP, :], m_db[:, q % DEEP, :], 0.0,
                                       ALU.mult, ALU.add).then_inc(M["h"], 1)
                if isinstance(i, int) and i == 0 and q < HEAD:
                    if q % 2 == 0 and q // 2 + 1 < NB:
                        softplus_end(q // 2 + 1)
                    if q % 2 == 1 and q // 2 + 1 < NB:
                        dt_times_xc(q // 2 + 1)
                    if q == HEAD - 1:
                        dve.wait_ge(*M("du", NB))

            def finish(i, blk, q):
                if q == 1:
                    for m in range(MC):
                        dve.wait_ge(*M("y_sum", 32 * i + 31 + m))
                        dve.scalar_tensor_tensor(m_y[:, m, :], xc[:, m, blk], cols[:, C_D + m:C_D + m + 1], ps[:, 4 + m, :],
                                                 ALU.mult, ALU.add).then_inc(M["ylin"], 1)
                if q == 2:
                    for m in range(MC):
                        dve.wait_ge(*M("ylin", 2 * i + m + 1))
                        dve.tensor_tensor(m_y[:, m, :], m_y[:, m, :], sz[:, m, blk], ALU.mult).then_inc(M["gated"], 1)
                if q == 4:
                    for m in range(MC):
                        dve.wait_ge(*M("g_hi", 2 * i + m + 1))
                        split_lo(dve, g_lo[:, m, :], m_y[:, m, :], g_hi[:, m, :]).then_inc(M["g_lo"], 1)
                if q == 7:
                    dve.wait_ge(*M("out", i + 1))
                    dve.tensor_tensor(x[:, blk], x[:, blk], ps[:, 6, :], ALU.add).then_inc(M["x_new"], 1)

            dve.wait_ge(*M("du", 1))
            input_term(0, cut(0), 0)
            scan_blocks(dve, item, finish)

        def mix_pool(pool):
            pool.tensor_copy(sel_bc[:, :, :], const[:, K_ID32:K_ID32 + 2 * DS].unsqueeze(2).broadcast_to([P, 2 * DS, P]))\
                .then_inc(M["sel_set"], 1)

            def item(i, blk, q, last):
                n = q // MC
                pool.wait_ge(*M("h", 32 * i + q + 1))
                if q % MC == 0:
                    pool.wait_ge(*M("c_copy", 16 * i + n + 1))
                after(pool, "y_sum", 32 * i + q + 1 - DEEP)
                pool.tensor_tensor(m_hc[:, q % DEEP, :], m_h[:, q % DEEP, :], m_c[:, n % 2, :], ALU.mult).then_inc(M["hc"], 1)

            scan_blocks(pool, item, lambda i, blk, q: None)

        SHARED = 2 * NB
        PER = 2 * NB
        AHEAD = 3

        def moe_pe(pe, S, L, last_block):
            if last_block:
                one_mean(pe, L, cut(LAST))
            else:
                pe.wait_ge(*L("centred", NB))
            pe.wait_ge(*S("small_lo", 1))
            for t in range(NTT):
                if last_block and t == 4:
                    one_var(pe, L, LAST)
                if last_block and t == 8:
                    one_spread(pe, L, LAST)
                pe.wait_ge(*L("xn_lo", t // 4 + 1))
                tt = slice(t * P, (t + 1) * P)
                r = slice(S_R, S_R + E)
                out = ps[:, t // 8, (t % 8) * E:(t % 8 + 1) * E]
                pe.matmul(out, xn_hi[:, tt], sh[:, r], start=True, stop=False, skip_group_check=True)
                pe.matmul(out, xn_hi[:, tt], sl[:, r], start=False, stop=False, skip_group_check=True)
                last = pe.matmul(out, xn_lo[:, tt], sh[:, r], start=False, stop=True, skip_group_check=True)
                if t % 8 == 7:
                    last.then_inc(S["logits"], 1)
            pe.wait_ge(*S("small_lo", 2))
            banks_free(pe, L)

            def gate_up(t, gh, gl, uh, ul, b, rows_):
                pe.wait_ge(*S("silu", t))
                mm3(pe, ps[0:rows_, 4, :], gh, gl, xn_hi[:, cut(b)], xn_lo[:, cut(b)], True, True).then_inc(S["gate"], 1)
                pe.wait_ge(*S("gated", t))
                mm3(pe, ps[0:rows_, 5, :], uh, ul, xn_hi[:, cut(b)], xn_lo[:, cut(b)], True, True).then_inc(S["up"], 1)

            def down(t, dh, dl, b, start, stop, rows_):
                pe.wait_ge(*S("h_lo", t + 1))
                mm3(pe, ps[:, b, :], dh, dl, e_hi[0:rows_, b, :], e_lo[0:rows_, b, :], start, stop).then_inc(S["down"], 1)

            def shared_gate_up(t):
                c, b = t // NB, t % NB
                g = slice(S_G + c * I, S_G + (c + 1) * I)
                u = slice(S_U + c * I, S_U + (c + 1) * I)
                gate_up(t, sh[:, g], sl[:, g], sh[:, u], sl[:, u], b, I)

            def shared_down(t):
                c, b = t // NB, t % NB
                down(t, sd_h[:, c, :], sd_l[:, c, :], b, c == 0, False, I)

            def expert_gate_up(i, j, spread=True):
                c, b = j // NB, j % NB
                t = PER * i + SHARED + j
                if b == 0:
                    pe.wait_ge(*S("w_lo", 4 * i + 2 * c + 1))
                gate_up(t, eh[:, c, 1, :], el[:, c, 1, :], eh[:, c, 2, :], el[:, c, 2, :], b, P)
                if spread:
                    expert_spread(i, j)

            def expert_spread(i, j):
                c, b = j // NB, j % NB
                pe.wait_ge(*S("weighted", PER * i + SHARED + j - 1))
                pe.matmul(ps[:, 6 + j % 2, :], eh[:, c, 3, :], rwt[:, cut(b)], start=True, stop=True).then_inc(S["spread"], 1)

            def expert_down(i, j, stop):
                c, b = j // NB, j % NB
                if b == 0:
                    pe.wait_ge(*S("w_lo", 4 * i + 2 * c + 2))
                down(PER * i + SHARED + j, eh[:, c, 0, :], el[:, c, 0, :], b, False, stop, P)

            pe.wait_ge(*S("scores", 2))
            for t in range(SHARED):
                shared_gate_up(t)
                if t >= AHEAD:
                    shared_down(t - AHEAD)
            for t in range(SHARED - AHEAD, SHARED):
                shared_down(t)
            expert_gate_up(0, 0, False)
            pe.wait_ge(*S("routed", 2))
            for g in range(4):
                if g >= 2:
                    pe.wait_ge(*S("rwt", g - 1))
                for t in range(4):
                    last = pe.transpose(ps[:, 6 + g % 2, t * P:(t + 1) * P],
                                        rw_cat[:, 4 * g + t, :, :].rearrange("p a e -> p (a e)"), ident)
                last.then_inc(S["rw_t"], 1)
            pe.wait_ge(*S("rwt", 4))
            expert_spread(0, 0)
            for j in range(1, AHEAD):
                expert_gate_up(0, j)
            with pe.Fori(0, PAIRS - 1) as i:
                for j in range(PER):
                    expert_gate_up(i + (j + AHEAD) // PER, (j + AHEAD) % PER)
                    expert_down(i, j, False)
            for j in range(PER):
                if j + AHEAD < PER:
                    expert_gate_up(PAIRS - 1, j + AHEAD)
                expert_down(PAIRS - 1, j, j >= NB)

        def moe_act(act, S):
            act.wait_ge(*S("small_in", 32))
            act.activation(sh[:, :], s_raw[:, :], ACT.Identity).then_inc(S["small_hi"], 1)
            act.activation(sd_h[:, :, :], sd_raw[:, :, :], ACT.Identity).then_inc(S["small_hi"], 1)

        def moe_act_tiles(act, S, attention):
            for half in range(2):
                act.wait_ge(*S("logits", half + 1))
                act.activation(r_s[:, 8 * half:8 * half + 8, :].rearrange("p t e -> p (t e)"), ps[:, half, :], ACT.Sigmoid)\
                    .then_inc(S["scores"], 1)

            def gate_up_high(i, c, read):
                act.wait_ge(*S(f"raw_in{c}", 32 * i + 32))
                act.wait_ge(*S("spread", read))
                act.activation(eh[:, c, 1:4, :], e_raw[:, c, 1:4, :], ACT.Identity).then_inc(S["w_hi"], 1)

            def down_high(i, c, read):
                act.wait_ge(*S("down", read))
                act.activation(eh[:, c, 0, :], e_raw[:, c, 0, :], ACT.Identity).then_inc(S["w_hi"], 1)

            def silu(t, buf, rows_):
                act.wait_ge(*S("gate", t + 1))
                if not (isinstance(t, int) and t < 4):
                    act.wait_ge(*S("gated", t - 3))
                act.activation(e_s[0:rows_, buf, :], ps[0:rows_, 4, :], ACT.Silu).then_inc(S["silu"], 1)

            def high(t, buf, rows_):
                act.wait_ge(*S("gated" if rows_ == I else "weighted", t + 1))
                if not (isinstance(t, int) and t < 4):
                    act.wait_ge(*S("down", t - 3))
                split_hi(act, e_hi[0:rows_, buf, :], e_h[0:rows_, buf, :]).then_inc(S["h_hi"], 1)

            gate_up_high(0, 0, 0)
            down_high(0, 0, 0)
            for t in range(SHARED):
                silu(t, t % 4, I)
                if t:
                    high(t - 1, (t - 1) % 4, I)
                if t == 4 and attention:
                    act.wait_ge(a_in, 16)
                    split_hi(act, ah[:, :], a_raw[:, :]).then_inc(a_hi, 1)
            high(SHARED - 1, 3, I)
            silu(SHARED, 0, P)
            for g in range(4):
                act.wait_ge(*S("rw_t", g + 1))
                act.activation(rwt[:, cut(g)], ps[:, 6 + g % 2, :], ACT.Identity).then_inc(S["rwt"], 1)

            def pair(i, last):
                for j in range(PER):
                    t = PER * i + SHARED + j
                    if j + 1 < PER or not last:
                        silu(t + 1, (j + 1) % 4, P)
                    high(t, j % 4, P)
                    if j == 0:
                        gate_up_high(i, 1, PER * i)
                    if j == 3:
                        down_high(i, 1, PER * i + SHARED)
                    if j == 4 and not last:
                        gate_up_high(i + 1, 0, PER * i + 4)
                    if j == 7 and not last:
                        down_high(i + 1, 0, PER * i + SHARED + 4)

            with act.Fori(0, PAIRS - 1) as i:
                pair(i, False)
            pair(PAIRS - 1, True)

        def moe_pool(pool, S):
            pool.wait_ge(*S("small_hi", 1))
            split_lo(pool, sl[:, :], s_raw[:, :], sh[:, :]).then_inc(S["small_lo"], 1)
            pool.wait_ge(*S("small_hi", 2))
            split_lo(pool, sd_l[:, :, :], sd_raw[:, :, :], sd_h[:, :, :]).then_inc(S["small_lo"], 1)

        def moe_pool_tiles(pool, S, attention):
            def gate_up_low(i, c):
                pool.wait_ge(*S("w_hi", 4 * i + 2 * c + 1))
                split_lo(pool, el[:, c, 1:3, :], e_raw[:, c, 1:3, :], eh[:, c, 1:3, :]).then_inc(S["w_lo"], 1)

            def down_low(i, c):
                pool.wait_ge(*S("w_hi", 4 * i + 2 * c + 2))
                split_lo(pool, el[:, c, 0, :], e_raw[:, c, 0, :], eh[:, c, 0, :]).then_inc(S["w_lo"], 1)

            def low(t, buf, rows_):
                pool.wait_ge(*S("h_hi", t + 1))
                split_lo(pool, e_lo[0:rows_, buf, :], e_h[0:rows_, buf, :], e_hi[0:rows_, buf, :]).then_inc(S["h_lo"], 1)

            gate_up_low(0, 0)
            down_low(0, 0)
            for t in range(SHARED):
                low(t, t % 4, I)
                if t == 4 and attention:
                    pool.wait_ge(a_hi, 1)
                    split_lo(pool, al[:, :], a_raw[:, :], ah[:, :]).then_inc(a_lo, 1)

            def pair(i, last):
                for j in range(PER):
                    low(PER * i + SHARED + j, j % 4, P)
                    if j == 0:
                        gate_up_low(i, 1)
                    if j == 3:
                        down_low(i, 1)
                    if j == 4 and not last:
                        gate_up_low(i + 1, 0)
                    if j == 7 and not last:
                        down_low(i + 1, 0)

            with pool.Fori(0, PAIRS - 1) as i:
                pair(i, False)
            pair(PAIRS - 1, True)

        def moe_dve(dve, S):
            def shared_gate(t):
                dve.wait_ge(*S("up", t + 1))
                dve.wait_ge(*S("silu", t + 1))
                if t >= 4:
                    dve.wait_ge(*S("h_lo", t - 3))
                dve.tensor_tensor(e_h[0:I, t % 4, :], e_s[0:I, t % 4, :], ps[0:I, 5, :], ALU.mult).then_inc(S["gated"], 1)
                dve.sem_inc(S["weighted"], 1)

            steps = [0]

            def step(ins):
                steps[0] += 1
                ins.then_inc(S["route"], 1)
                if steps[0] % 3 == 1 and steps[0] // 3 < SHARED:
                    shared_gate(steps[0] // 3)
                dve.wait_ge(*S("route", steps[0]))

            NGT = NTT * NG
            small = [r_small[:, k, :] for k in range(4)]

            def pairs_of(tile, lo, n):
                v = tile[:, lo:lo + NGT * n].rearrange("p (g k) -> p g k", k=n)
                return v[:, :, 0:n // 2], v[:, :, n // 2:n]

            def out_of(tile, lo, n):
                return tile[:, lo:lo + NGT * n].rearrange("p (g k) -> p g k", k=n)

            dve.wait_ge(*S("scores", 2))
            bias = rows[:, R_GB:R_GB + E].unsqueeze(1).broadcast_to([P, NTT, E])
            step(dve.tensor_tensor(r_c[:, :, :], r_s[:, :, :], bias, ALU.add))
            c8 = r_c[:, :, :].rearrange("p t (g k) -> p (t g) k", k=8)
            a, b = c8[:, :, 0:4], c8[:, :, 4:8]
            step(dve.tensor_tensor(out_of(r_t, 0, 4), a, b, ALU.max))
            step(dve.tensor_tensor(out_of(r_u, 0, 4), a, b, ALU.min))
            a, b = pairs_of(r_t, 0, 4)
            ma, mb = pairs_of(r_u, 0, 4)
            step(dve.tensor_tensor(out_of(r_u, 512, 2), a, b, ALU.min))
            step(dve.tensor_tensor(out_of(r_t, 512, 2), a, b, ALU.max))
            step(dve.tensor_tensor(out_of(r_t, 768, 2), ma, mb, ALU.max))
            step(dve.tensor_tensor(out_of(r_u, 768, 2), out_of(r_u, 512, 2), out_of(r_t, 768, 2), ALU.max))
            a, b = pairs_of(r_t, 512, 2)
            ma, mb = pairs_of(r_u, 768, 2)
            one = [s_.unsqueeze(2) for s_ in small]
            step(dve.tensor_tensor(one[0], a, b, ALU.max))
            step(dve.tensor_tensor(one[1], a, b, ALU.min))
            step(dve.tensor_tensor(one[2], ma, mb, ALU.max))
            step(dve.tensor_tensor(small[1], small[1], small[2], ALU.max))
            step(dve.tensor_tensor(small[0], small[0], small[1], ALU.add))
            g3 = small[0].rearrange("p (t g) -> p t g", g=NG)
            other = g3.unsqueeze(2).broadcast_to([P, NTT, NG, NG])
            own = g3.unsqueeze(3).broadcast_to([P, NTT, NG, NG])
            t4 = r_t[:, :].rearrange("p (t g k) -> p t g k", g=NG, k=NG)
            tie = const[:, K_TIE:K_TIE + E].unsqueeze(1).broadcast_to([P, NTT, E])
            t3 = r_t[:, :].rearrange("p (t e) -> p t e", e=E)
            u3 = r_u[:, :].rearrange("p (t e) -> p t e", e=E)
            step(dve.tensor_tensor(t4, other, own, ALU.subtract))
            step(dve.scalar_tensor_tensor(u3, t3, 0.0, tie, ALU.is_equal, ALU.mult))
            step(dve.scalar_tensor_tensor(r_t[:, :], r_t[:, :], 0.0, r_u[:, :], ALU.is_gt, ALU.add))
            step(dve.tensor_reduce(small[1], out_of(r_t, 0, 8), AX, ALU.add))
            step(dve.tensor_scalar(small[1], small[1], 4.0, None, ALU.is_lt))
            step(dve.tensor_tensor(c8, c8, small[1].unsqueeze(2).broadcast_to([P, NGT, 8]), ALU.mult))
            for t in range(NTT):
                ins = dve.max(small[2][:, t * 8:t * 8 + 8], r_c[:, t, :])
                if t == NTT - 1:
                    step(ins)
            for t in range(NTT):
                ins = dve.match_replace(t3[:, t, :], small[2][:, t * 8:t * 8 + 8], r_c[:, t, :], GONE)
                if t == NTT - 1:
                    step(ins)
            step(dve.scalar_tensor_tensor(u3, t3, GONE, r_s[:, :, :], ALU.is_equal, ALU.mult))
            total = small[3][:, 0:NTT]
            step(dve.tensor_reduce(total, u3, AX, ALU.add))
            step(dve.tensor_scalar(total, total, 1e-20, None, ALU.add))
            step(dve.reciprocal(total, total))
            step(dve.scalar_tensor_tensor(t3, u3, 2.5, total.unsqueeze(2).broadcast_to([P, NTT, E]), ALU.mult, ALU.mult))
            dve.tensor_copy(rw_cat[:, :, 0, :].bitcast(F32R), t3).then_inc(S["routed"], 1)
            dve.wait_ge(*S("routed", 1))
            dve.tensor_tensor(rw_cat[:, :, 1, :].bitcast(F32R), t3, rw_cat[:, :, 0, :], ALU.subtract).then_inc(S["routed"], 1)

            assert steps[0] == ROUTE_STEPS

            def gate(t, buf, rows_):
                dve.wait_ge(*S("up", t + 1))
                dve.wait_ge(*S("silu", t + 1))
                dve.wait_ge(*S("weighted", t - 1))
                dve.tensor_tensor(e_p[0:rows_, buf % 2, :], e_s[0:rows_, buf, :], ps[0:rows_, 5, :], ALU.mult).then_inc(S["gated"], 1)
                dve.wait_ge(*S("gated", t + 1))
                dve.wait_ge(*S("h_lo", t - 3))

            with dve.Fori(0, PAIRS) as i:
                for j in range(PER):
                    t = PER * i + SHARED + j
                    gate(t, j % 4, P)
                    dve.wait_ge(*S("spread", PER * i + j + 1))
                    dve.tensor_tensor(e_h[:, j % 4, :], e_p[:, j % 2, :], ps[:, 6 + j % 2, :], ALU.mult).then_inc(S["weighted"], 1)
            for b in range(NB):
                dve.wait_ge(*S("down", SHARED + PER * (PAIRS - 1) + NB + b + 1))
                dve.scalar_tensor_tensor(x[:, cut(b)], ps[:, b, :], 0.5, x[:, cut(b)], ALU.mult, ALU.add).then_inc(S["x_new"], 1)

        def moe_load_small(sp, S):
            sp.dma_start(s_raw[:, :], d["l1_small"]).then_inc(S["small_in"], 16)
            sp.dma_start(sd_raw[:, :, :], d["sd"]).then_inc(S["small_in"], 16)

        def moe_load(sp, S):
            def chunk(i, c):
                sp.dma_start(e_raw[:, c, 0:3, :], d["experts"][bass.ds(2 * i + c, 1)].rearrange("a p k n -> p (a k) n"))\
                    .then_inc(S[f"raw_in{c}"], 16)
                sp.dma_start(e_raw[:, c, 3, :], d["pick"][bass.ds(2 * i + c, 1)].rearrange("a p n -> p (a n)"))\
                    .then_inc(S[f"raw_in{c}"], 16)

            chunk(0, 0)
            chunk(0, 1)
            with sp.Fori(0, PAIRS - 1) as i:
                for c in range(2):
                    sp.wait_ge(*S("w_lo", 4 * i + 2 * c + 2))
                    chunk(i + 1, c)

        SCALE = float(P) ** -0.5
        S_AT = {0: (1, 384), 1: (2, 0), 2: (1, 0), 3: (0, 0)}
        PT_AT = {0: (3, 0), 1: (4, 0), 2: (2, 256), 3: (4, 384)}
        ORDER = (3, 2, 0, 1)

        def scores_at(r):
            bank, lo = S_AT[r]
            return ps[:, bank, lo:lo + P * (r + 1)]

        PT_UNITS = (((2,), 2, 256, 2), ((1, 3), 1, T, 4), ((0,), 0, T, 4))
        PT_PART = {0: (0, 0), 1: (1, 0), 2: (2, 0), 3: (1, 384)}

        def pt_at(kb):
            bank, lo = PT_AT[kb]
            return ps[:, bank, lo:lo + T - P * kb]

        def pt_psum(unit):
            (kb, *_), _, n, _ = PT_UNITS[unit]
            bank, lo = PT_AT[kb]
            return ps[:, bank, lo:lo + n]

        def att_pe(pe, L):
            def k_proj(i, blk, first=False):
                if not first:
                    pe.wait_ge(*A("q32", 8 * i - 2))
                w = slice(A_K, A_K + P)
                mm3(pe, ps[:, 5, :], ah[:, w], al[:, w], xn_hi[:, blk], xn_lo[:, blk], True, True).then_inc(A["kp"], 1)

            def v_proj(i, x_hi, x_lo, first=False):
                if not first:
                    pe.wait_ge(*A("xb_lo", i))
                    pe.wait_ge(*A("p", 32 * i - 3))
                w = slice(A_V, A_V + P)
                for t in range(4):
                    tt = slice(t * P, (t + 1) * P)
                    out = ps[:, 0, tt]
                    pe.matmul(out, x_hi[:, tt], ah[:, w], start=True, stop=False, skip_group_check=True)
                    pe.matmul(out, x_hi[:, tt], al[:, w], start=False, stop=False, skip_group_check=True)
                    last = pe.matmul(out, x_lo[:, tt], ah[:, w], start=False, stop=True, skip_group_check=True)
                last.then_inc(A["vp"], 1)

            def q_proj(i, blk, h):
                if h == 0:
                    pe.wait_ge(*A("k32", i + 1))
                else:
                    pe.wait_ge(*A("q32", 8 * i + h))
                w = slice(A_Q + h * P, A_Q + (h + 1) * P)
                mm3(pe, ps[:, 5, :], ah[:, w], al[:, w], xn_hi[:, blk], xn_lo[:, blk], True, True).then_inc(A["qp"], 1)

            def score(i, h, first=False):
                g = 8 * i + h
                if h == 0:
                    pe.wait_ge(*A("k_lo", i + 1))
                    pe.wait_ge(*A("v32", i + 1))
                pe.wait_ge(*A("q_lo", g + 1))
                for k, r in enumerate(ORDER):
                    if not first and r != 0:
                        pe.wait_ge(*A("p", 4 * g - 4 + {3: 1, 2: 3, 1: 4}[r]))
                        if r == 1:
                            pe.wait_ge(*A("pt_lo", 3 * g - 2))
                    n = P * (r + 1)
                    q = slice(r * P, n)
                    out = scores_at(r)
                    pe.matmul(out, q_hi[:, h % 2, q], k_hi[:, 0:n], start=True, stop=False, skip_group_check=True)
                    pe.matmul(out, q_hi[:, h % 2, q], k_lo[:, 0:n], start=False, stop=False, skip_group_check=True)
                    pe.matmul(out, q_lo[:, h % 2, q], k_hi[:, 0:n], start=False, stop=False, skip_group_check=True)
                    last = pe.matmul(out[:, r * P:n], idr[:, :], maskr[:, :], start=False, stop=True, skip_group_check=True)
                    if r != 2:
                        last.then_inc(A["s"], 1)

            def turn(i, h):
                g = 8 * i + h
                pe.wait_ge(*A("p", 4 * g + 4))
                pe.wait_ge(*A("pt_lo", 3 * g))
                for tiles, _, _, need in PT_UNITS:
                    pe.wait_ge(*A("pn", 4 * g + need))
                    for kb in tiles:
                        for r in range(kb, 4):
                            last = pe.transpose(pt_at(kb)[:, (r - kb) * P:(r - kb + 1) * P], p32[:, r, kb * P:(kb + 1) * P], ident)
                    last.then_inc(A["pt"], 1)

            def values(i, h):
                g = 8 * i + h
                if h == 0:
                    pe.wait_ge(*A("v_lo", i + 1))
                pe.wait_ge(*A("o32", g))
                pe.wait_ge(*A("pt_lo", 3 * g + 3))
                for kb in range(4):
                    part, lo = PT_PART[kb]
                    n = T - kb * P
                    last = mm3(pe, ps[:, 6, kb * P:T], v_hi[:, kb, :], v_lo[:, kb, :], pt_hi[:, part, lo:lo + n],
                               pt_lo[:, part, lo:lo + n], kb == 0, kb == 3)
                last.then_inc(A["o"], 1)

            def out_proj(i, h):
                pe.wait_ge(*A("o_lo", 8 * i + h + 1))
                if h == 0:
                    pe.wait_ge(*A("x_new", i))
                w = slice(A_O + h * P, A_O + (h + 1) * P)
                mm3(pe, ps[:, 7, :], ah[:, w], al[:, w], o_hi[:, h % 2, :], o_lo[:, h % 2, :], h == 0, h == HEADS - 1)\
                    .then_inc(A["y"], 1)

            def heads(i, last):
                blk, following = bass.ds(i * T, T), bass.ds((i + 1) * T, T)
                for h in range(HEADS):
                    if h:
                        score(i, h)
                        values(i, h - 1)
                    if h < HEADS - 2:
                        q_proj(i, blk, h + 2)
                    elif h == HEADS - 2 and not last:
                        k_proj(i + 1, following)
                    elif not last:
                        q_proj(i + 1, following, 0)
                    if h >= 2:
                        out_proj(i, h - 2)
                    turn(i, h)
                if not last:
                    v_proj(i + 1, xb_hi, xb_lo)
                out_proj(i, HEADS - 2)
                values(i, HEADS - 1)
                if not last:
                    q_proj(i + 1, following, 1)
                    score(i + 1, 0)
                out_proj(i, HEADS - 1)

            pe.wait_ge(*A("mask", 2))
            pe.wait_ge(a_lo, 1)
            banks_free(pe, L)
            pe.wait_ge(*L("xn_lo", NB))
            k_proj(0, cut(0), True)
            v_proj(0, xn_hi[:, 0:T], xn_lo[:, 0:T], True)
            q_proj(0, cut(0), 0)
            q_proj(0, cut(0), 1)
            score(0, 0, True)
            with pe.Fori(0, NB - 1) as i:
                heads(i, False)
            heads(NB - 1, True)

        def att_act(act):
            def k_high(i):
                act.wait_ge(*A("k32", i + 1))
                act.wait_ge(*A("s", 24 * i))
                split_hi(act, k_hi[:, :], kv32[:, 0, :]).then_inc(A["k_hi"], 1)

            def v_high(i):
                act.wait_ge(*A("v32", i + 1))
                act.wait_ge(*A("o", 8 * i))
                act.activation(v_hi[:, :, :].rearrange("p t n -> p (t n)"), kv32[:, 1, :], ACT.Identity).then_inc(A["v_hi"], 1)

            def q_high(i, h, first=False):
                g = 8 * i + h
                act.wait_ge(*A("q32", g + 1))
                if not first:
                    act.wait_ge(*A("s", 3 * g - 3))
                split_hi(act, q_hi[:, h % 2, :], q32[:, h % 2, :]).then_inc(A["q_hi"], 1)

            def probs(i, h):
                g = 8 * i + h
                act.wait_ge(*A("pt", 3 * g))
                for k, r in enumerate(ORDER):
                    act.wait_ge(*A("min", 4 * g + (1, 3, 3, 4)[k]))
                    act.activation(p32[:, r, 0:P * (r + 1)], scores_at(r), ACT.Exp, scale=-1.0, bias=st[:, h % 2, 0, r:r + 1],
                                   accum_out=st[:, h % 2, 1, r:r + 1]).then_inc(A["p"], 1)

            def output(i, h):
                g = 8 * i + h
                act.wait_ge(*A("o", g + 1))
                act.wait_ge(*A("o_lo", g))
                act.activation(o32[:, :], ps[:, 6, :], ACT.Identity).then_inc(A["o32"], 1)
                act.wait_ge(*A("o32", g + 1))
                act.wait_ge(*A("y", max(g - 1, 0) if isinstance(g, int) else (g - 1 if h else g)))
                split_hi(act, o_hi[:, h % 2, :], o32[:, :]).then_inc(A["o_hi"], 1)

            def heads(i, last):
                for h in range(HEADS):
                    if h:
                        probs(i, h)
                        output(i, h - 1)
                    for unit, (_, part, n, _) in enumerate(PT_UNITS):
                        act.wait_ge(*A("pt", 3 * (8 * i + h) + unit + 1))
                        act.wait_ge(*A("o", 8 * i + h))
                        act.activation(pt_hi[:, part, 0:n], pt_psum(unit), ACT.Identity).then_inc(A["pt_hi"], 1)
                    if h < HEADS - 2:
                        q_high(i, h + 2)
                    elif h == HEADS - 1 and not last:
                        k_high(i + 1)
                        q_high(i + 1, 0)
                output(i, HEADS - 1)
                if not last:
                    v_high(i + 1)
                    q_high(i + 1, 1)
                    probs(i + 1, 0)

            k_high(0)
            q_high(0, 0, True)
            v_high(0)
            q_high(0, 1, True)
            probs(0, 0)
            with act.Fori(0, NB - 1) as i:
                heads(i, False)
            heads(NB - 1, True)

        def att_dve(dve, L):
            dve.tensor_copy(idr[:, :], ident).then_inc(A["mask"], 1)
            dve.tensor_copy(maskr[:, :], const[:, K_MASK:K_MASK + P]).then_inc(A["mask"], 1)
            pe_t = const[:, K_PE:K_PE + T]
            dve.tensor_scalar(k_add[:, :], pe_t, cols[:, C_BK:C_BK + 1], -SCALE, ALU.add, ALU.mult).then_inc(A["k_add"], 1)
            dve.wait_ge(*A("k_add", 1))

            def k_full(i):
                dve.wait_ge(*A("kp", i + 1))
                dve.wait_ge(*A("k_lo", i))
                dve.scalar_tensor_tensor(kv32[:, 0, :], ps[:, 5, :], -SCALE, k_add[:, :], ALU.mult, ALU.add).then_inc(A["k32"], 1)

            def v_full(i):
                dve.wait_ge(*A("vp", i + 1))
                dve.wait_ge(*A("v_lo", i))
                dve.tensor_tensor(kv32[:, 1, :].rearrange("p (t n) -> p t n", t=4), ps[:, 0, :].rearrange("p (t n) -> p t n", t=4),
                                  rows[:, R_BV:R_BV + P].unsqueeze(1).broadcast_to([P, 4, P]), ALU.add).then_inc(A["v32"], 1)

            def q_full(i, h, first=False):
                g = 8 * i + h
                dve.wait_ge(*A("qp", g + 1))
                if not first:
                    dve.wait_ge(*A("q_lo", g - 1))
                dve.scalar_tensor_tensor(q32[:, h % 2, :], ps[:, 5, :], cols[:, C_BQ + h:C_BQ + h + 1], pe_t,
                                         ALU.add, ALU.add).then_inc(A["q32"], 1)

            def minima(i, h, tiles=ORDER):
                for r in tiles:
                    dve.wait_ge(*A("s", 3 * (8 * i + h) + {3: 1, 2: 2, 0: 2, 1: 3}[r]))
                    dve.tensor_reduce(st[:, h % 2, 0, r:r + 1], scores_at(r), AX, ALU.min).then_inc(A["min"], 1)

            def normalise(i, h):
                g = 8 * i + h
                for half, tiles in enumerate(((3, 2), (0, 1))):
                    lo = min(tiles)
                    dve.wait_ge(*A("p", 4 * g + 2 * half + 2))
                    dve.reciprocal(st[:, h % 2, 2, lo:lo + 2], st[:, h % 2, 1, lo:lo + 2]).then_inc(A["inv"], 1)
                    dve.wait_ge(*A("inv", 2 * g + half + 1))
                    for r in tiles:
                        n = P * (r + 1)
                        dve.tensor_scalar(p32[:, r, 0:n], p32[:, r, 0:n], st[:, h % 2, 2, r:r + 1], None, ALU.mult).then_inc(A["pn"], 1)

            def heads(i, last):
                blk = bass.ds(i * T, T) if not last else cut(i)
                for h in range(HEADS):
                    normalise(i, h)
                    if h < HEADS - 2:
                        q_full(i, h + 2)
                    elif h == HEADS - 2 and not last:
                        k_full(i + 1)
                    elif not last:
                        q_full(i + 1, 0)
                    for unit, (_, part, n, _) in enumerate(PT_UNITS):
                        dve.wait_ge(*A("pt_hi", 3 * (8 * i + h) + unit + 1))
                        split_lo(dve, pt_lo[:, part, 0:n], pt_psum(unit), pt_hi[:, part, 0:n]).then_inc(A["pt_lo"], 1)
                        if h + 1 < HEADS and unit:
                            minima(i, h + 1, ORDER[0:1] if unit == 1 else ORDER[1:])
                if not last:
                    v_full(i + 1)
                    q_full(i + 1, 1)
                    minima(i + 1, 0)
                dve.wait_ge(*A("y", 8 * i + 8))
                dve.tensor_tensor(x[:, blk], x[:, blk], ps[:, 7, :], ALU.add).then_inc(A["x_new"], 1)

            k_full(0)
            q_full(0, 0, True)
            v_full(0)
            q_full(0, 1, True)
            minima(0, 0)
            with dve.Fori(0, NB - 1) as i:
                heads(i, False)
            heads(NB - 1, True)

        def att_pool(pool):
            def k_low(i):
                pool.wait_ge(*A("k_hi", i + 1))
                split_lo(pool, k_lo[:, :], kv32[:, 0, :], k_hi[:, :]).then_inc(A["k_lo"], 1)

            def v_low(i):
                pool.wait_ge(*A("v_hi", i + 1))
                split_lo(pool, v_lo[:, :, :].rearrange("p t n -> p (t n)"), kv32[:, 1, :],
                         v_hi[:, :, :].rearrange("p t n -> p (t n)")).then_inc(A["v_lo"], 1)

            def q_low(i, h):
                pool.wait_ge(*A("q_hi", 8 * i + h + 1))
                split_lo(pool, q_lo[:, h % 2, :], q32[:, h % 2, :], q_hi[:, h % 2, :]).then_inc(A["q_lo"], 1)

            def o_low(i, h):
                pool.wait_ge(*A("o_hi", 8 * i + h + 1))
                split_lo(pool, o_lo[:, h % 2, :], o32[:, :], o_hi[:, h % 2, :]).then_inc(A["o_lo"], 1)

            def heads(i, last):
                for h in range(HEADS):
                    if h:
                        o_low(i, h - 1)
                    if h < HEADS - 2:
                        q_low(i, h + 2)
                    elif h == HEADS - 1 and not last:
                        k_low(i + 1)
                        q_low(i + 1, 0)
                    if h == 1 and not last:
                        pool.wait_ge(*A("vp", i + 1))
                        pool.tensor_copy(xb_hi[:, :], xn_hi[:, bass.ds((i + 1) * T, T)].bitcast(F32)).then_inc(A["xb_hi"], 1)
                    if h == 3 and not last:
                        pool.tensor_copy(xb_lo[:, :], xn_lo[:, bass.ds((i + 1) * T, T)].bitcast(F32)).then_inc(A["xb_lo"], 1)
                o_low(i, HEADS - 1)
                if not last:
                    v_low(i + 1)
                    q_low(i + 1, 1)

            k_low(0)
            q_low(0, 0)
            v_low(0)
            q_low(0, 1)
            with pool.Fori(0, NB - 1) as i:
                heads(i, False)
            heads(NB - 1, True)

        FFN_CUTS = (W_G, W_H1, W_H2, NW)

        @block.sync
        def _(sp):
            sp.dma_start(x[:, 0:T], d["x"][:, 0:T]).then_inc(loaded, 16)
            sp.dma_start(cols[:, :], d["cols"]).then_inc(loaded, 16)
            sp.dma_start(const[:, 0:P], d["const"][:, 0:P]).then_inc(loaded, 16)
            sp.dma_start(x[:, T:NT], d["x"][:, T:NT]).then_inc(loaded, 16)
            for k in range(3):
                w = slice(FFN_CUTS[k], FFN_CUTS[k + 1])
                sp.dma_start(w_raw[:, w], d["ffn"][:, w]).then_inc(ffn_in[k], 16)
            sp.dma_start(const[:, P:NCONST], d["const"][:, P:NCONST]).then_inc(loaded_late, 16)
            sp.dma_start(rows[:, :], d["rows"]).then_inc(loaded_late, 16)
            sp.wait_ge(primed_all, 1)
            sp.wait_ge(w_split, 4)
            sp.dma_start(m_raw[:, 0:NM], d["mixer"]).then_inc(M["raw_in"], 16)
            start_phase(sp, 2)
            moe_load_small(sp, E1)
            start_phase(sp, 3)
            sp.dma_start(a_raw[:, :], d["attn"]).then_inc(a_in, 16)
            moe_load(sp, E1)
            start_phase(sp, 5)
            moe_load_small(sp, E2)
            moe_load(sp, E2)
            start_phase(sp, 6)
            sp.dma_start(d["out"], x[:, :]).then_inc(stored, 16)
            sp.wait_ge(stored, 16)

        @block.tensor
        def _(pe):
            pe.wait_ge(primed_all, 1)
            pe.wait_ge(ones_set, 1)
            pe.wait_ge(loaded, 64)
            ln_pe(pe, LN[0])
            pe.wait_ge(w_split, 4)
            ffn_pe(pe, F1, LN[0], LN[1])
            end_phase(pe)
            start_phase(pe, 1)
            mix_pe(pe, LN[1])
            end_phase(pe)
            start_phase(pe, 2)
            ln_pe(pe, LN[2])
            ffn_pe(pe, F2, LN[2], LN[3])
            end_phase(pe)
            start_phase(pe, 3)
            moe_pe(pe, E1, LN[3], True)
            end_phase(pe)
            start_phase(pe, 4)
            ln_pe(pe, LN[4])
            att_pe(pe, LN[4])
            end_phase(pe)
            start_phase(pe, 5)
            ln_pe(pe, LN[5])
            moe_pe(pe, E2, LN[5], False)
            end_phase(pe)

        @block.scalar
        def _(act):
            act.wait_ge(primed_all, 1)
            act.wait_ge(loaded, 64)
            act.wait_ge(ones_set, 3)
            ln_act(act, LN[0])
            act.wait_ge(ffn_in[2], 16)
            split_hi(act, wh[:, W_H2:NW], w_raw[:, W_H2:NW]).then_inc(w_hi_c, 1)
            ffn_act(act, F1, LN[1])
            end_phase(act)
            start_phase(act, 1)
            one_square(act, LN[1], LAST)
            one_deviation(act, LN[1], LAST)
            one_high(act, LN[1], LAST, cut(LAST))
            mix_act(act)
            end_phase(act)
            start_phase(act, 2)
            ln_act(act, LN[2])
            ffn_act(act, F2, LN[3])
            end_phase(act)
            start_phase(act, 3)
            moe_act(act, E1)
            last_act(act, LN[3])
            moe_act_tiles(act, E1, True)
            end_phase(act)
            start_phase(act, 4)
            ln_act(act, LN[4])
            att_act(act)
            end_phase(act)
            start_phase(act, 5)
            moe_act(act, E2)
            ln_act(act, LN[5])
            moe_act_tiles(act, E2, False)
            end_phase(act)

        @block.vector
        def _(dve):
            dve.wait_ge(primed_all, 1)
            dve.memset(mean_w[:, :], 1.0 / P).then_inc(ones_set, 1)
            dve.wait_ge(loaded, 64)
            dve.tensor_scalar(w3_half[:, :], cols[:, C_W3:C_W3 + 1], 0.5, None, ALU.mult).then_inc(ones_set, 1)
            dve.memset(cols[:, C_EPS:C_EPS + 1], EPS).then_inc(ones_set, 1)
            dve.wait_ge(ones_set, 3)

            def split_weights(step):
                k = step // 2
                w = slice(FFN_CUTS[k], FFN_CUTS[k + 1])
                if step % 2 == 0:
                    dve.wait_ge(ffn_in[k], 16)
                    dve.tensor_copy(wh[:, w], w_raw[:, w]).then_inc(w_split, 1)
                else:
                    dve.wait_ge(w_split, step)
                    split_lo(dve, wl[:, w], w_raw[:, w], wh[:, w]).then_inc(w_split, 1)

            ln_dve(dve, LN[0], split_weights)
            ffn_dve(dve, F1, LN[1])
            end_phase(dve)
            start_phase(dve, 1)
            dve.wait_ge(loaded_late, 32)
            last_dve(dve, LN[1])
            mix_dve(dve)
            end_phase(dve)
            start_phase(dve, 2)
            ln_dve(dve, LN[2])
            ffn_dve(dve, F2, LN[3])
            end_phase(dve)
            start_phase(dve, 3)
            last_dve(dve, LN[3])
            moe_dve(dve, E1)
            end_phase(dve)
            start_phase(dve, 4)
            ln_dve(dve, LN[4])
            att_dve(dve, LN[4])
            end_phase(dve)
            start_phase(dve, 5)
            ln_dve(dve, LN[5])
            moe_dve(dve, E2)
            end_phase(dve)

        @block.gpsimd
        def _(pool):
            for signal in primed:
                pool.sem_inc(signal, 1)
            pool.sem_inc(primed_all, 1)
            ln_pool(pool, LN[0])
            pool.wait_ge(w_hi_c, 1)
            split_lo(pool, wl[:, W_H2:NW], w_raw[:, W_H2:NW], wh[:, W_H2:NW]).then_inc(w_split_c, 1)
            pool.wait_ge(*M("raw_in", 16))
            pool.tensor_copy(mh[:, :], m_raw[:, 0:NM]).then_inc(M["w_hi"], 1)
            pool.wait_ge(*M("w_hi", 1))
            split_lo(pool, ml[:, :], m_raw[:, 0:NM], mh[:, :]).then_inc(M["w_lo"], 1)
            ffn_pool(pool, LN[1])
            end_phase(pool)
            start_phase(pool, 1)
            pool.wait_ge(loaded_late, 32)
            pool.memset(bc[4 * DS:P, :].bitcast(F32), 0.0).then_inc(M["bc_zero"], 1)
            pool.wait_ge(*M("bc_zero", 1))
            one_low(pool, LN[1], LAST, cut(LAST))
            mix_pool(pool)
            end_phase(pool)
            start_phase(pool, 2)
            ln_pool(pool, LN[2])
            ffn_pool(pool, LN[3])
            end_phase(pool)
            start_phase(pool, 3)
            moe_pool(pool, E1)
            one_low(pool, LN[3], LAST, cut(LAST))
            moe_pool_tiles(pool, E1, True)
            end_phase(pool)
            start_phase(pool, 4)
            ln_pool(pool, LN[4])
            att_pool(pool)
            end_phase(pool)
            start_phase(pool, 5)
            moe_pool(pool, E2)
            ln_pool(pool, LN[5])
            moe_pool_tiles(pool, E2, False)
            end_phase(pool)


def constants():
    k = np.zeros((P, NCONST), np.float32)
    p = np.arange(P)
    k[:, K_ID:K_ID + P] = np.eye(P)
    k[:, K_MASK:K_MASK + P] = np.where(p[None, :] > p[:, None], MASKED, 0.0)
    inv_freq = np.exp(np.float32(-np.log(10000.0)) * np.arange(0, P, 2, dtype=np.float32) / np.float32(P))
    ang = np.arange(T, dtype=np.float32)[:, None] * inv_freq.astype(np.float32)[None, :]
    k[0::2, K_PE:K_PE + T] = np.sin(ang).T
    k[1::2, K_PE:K_PE + T] = np.cos(ang).T
    g = np.arange(NG)
    k[:, K_TIE:K_TIE + E] = (g[None, :] < g[:, None]).reshape(-1)
    k[:2 * 2 * DS, K_ID32:K_ID32 + 2 * DS] = p[:2 * 2 * DS, None] % 32 == np.arange(2 * DS)[None, :]
    expert = np.arange(E * I) // I
    pick = (p[:, None] % E == expert[None, :]).astype(np.float32)
    return k, np.ascontiguousarray(pick.reshape(P, CH, P).transpose(1, 0, 2))


def kernel(**a):
    import concourse.bacc as bacc
    from concourse.bass_utils import run_bass_kernel_spmd

    a = {k: np.asarray(v) for k, v in a.items()}
    f, m, t, r = "L0_ffn_", "L0_attn_", "L1_attn_", "L1_ffn_"

    def chunks(w):
        return w.reshape(-1, P, w.shape[-1]).transpose(1, 0, 2).reshape(P, -1)

    def column(v):
        return v.reshape(-1, P).T

    arrays = {
        "x": a[m + "x"].reshape(NT, P).T,
        "ffn": np.concatenate([a[f + "w1_w"].T, a[f + "w2_w"].T, chunks(a[f + "h1_w"].T), chunks(a[f + "h2_w"].T),
                               chunks(a[f + "w3_w"].T)], axis=1),
        "mixer": np.concatenate([a[m + "in_proj_w"].T, chunks(a[m + "x_proj_w"].T), chunks(a[m + "out_proj_w"].T)], axis=1),
        "attn": np.concatenate([a[t + "Wq"], a[t + "Wkv"], chunks(a[t + "Wo"])], axis=1),
        "l1_small": np.concatenate([a[r + "gate_w"].T, a[r + "Sg"].T, a[r + "Su"].T], axis=1),
        "sd": a[r + "Sd"].T.reshape(2, I, P).transpose(1, 0, 2),
        "experts": np.stack([a[r + "Wd"].transpose(0, 2, 1).reshape(CH, P, P),
                             a[r + "Wg"].reshape(CH, P, P).transpose(0, 2, 1),
                             a[r + "Wu"].reshape(CH, P, P).transpose(0, 2, 1)], axis=2),
        "cols": np.concatenate(
            [column(a[f + n]) for n in ("w1_s", "w2_s", "h1_s", "h2_s", "w3_s")]
            + [a[m + "conv_w"].reshape(MC, P, 4).transpose(1, 0, 2).reshape(P, -1), column(a[m + "conv_b"]),
               column(a[m + "dt_proj_w"].reshape(-1)), column(a[m + "dt_proj_b"]), column(a[m + "D"]),
               a[m + "A_log"].reshape(MC, P, DS).transpose(1, 0, 2).reshape(P, -1),
               column(a[t + "bq"]), column(a[t + "bkv"][:P]), np.zeros((P, 1), np.float32)], axis=1),
        "rows": np.concatenate([np.broadcast_to(a[r + "gate_bias"], (P, E)), np.broadcast_to(a[t + "bkv"][P:], (P, P))], axis=1),
    }
    arrays["const"], arrays["pick"] = constants()
    arrays = {f"in_{k}": np.ascontiguousarray(v) for k, v in arrays.items()}

    nc = bacc.Bacc("TRN2", target_bir_lowering=False, num_devices=1)
    d = {k[3:]: nc.dram_tensor(k, v.shape, F32, kind="ExternalInput").ap() for k, v in arrays.items()}
    d["out"] = nc.dram_tensor("out", (P, NT), F32, kind="ExternalOutput").ap()
    program(nc, d)
    got = run_bass_kernel_spmd(nc, [arrays], core_ids=[0]).results[0]["out"]
    return np.ascontiguousarray(got.T).reshape(NB, T, P)
```
